# Optimizing a Trainium2 kernel written in Bass

```python
import numpy as np
import jax
import jax.numpy as jnp

def _softmax(x, axis=-1):
    return jax.nn.softmax(x, axis=axis)

def _gelu(x):
    return jax.nn.gelu(x, approximate=True)

def _silu(x):
    return jax.nn.silu(x)

def _sigmoid(x):
    return jax.nn.sigmoid(x)

def _layernorm(x, axis=-1, eps=1e-05):
    m = jnp.mean(x, axis=axis, keepdims=True)
    v = jnp.var(x, axis=axis, keepdims=True)
    return (x - m) / jnp.sqrt(v + eps)

def _scatter_add(tgt, idx, src, axis=0):
    return tgt.at[idx].add(src)

def _segment_sum(src, seg, n):
    return jax.ops.segment_sum(src, seg, n)
kernel_name = 'mk_sandwich_d1_jaxref_r4_ce00f2'

def setup_inputs(seed: int=0):
    np.random.seed(seed)
    _w = jnp.asarray

    def _L0_attn_setup():
        import jax, jax.numpy as jnp
        import numpy as np
        D_MODEL = 256
        D_STATE = 64
        HEADDIM = 64
        MIMO_RANK = 2
        CHUNK = 128
        EXPAND = 2
        D_INNER = EXPAND * D_MODEL
        NHEADS = D_INNER // HEADDIM
        G = MIMO_RANK * D_STATE
        D_CONV = 4
        D_XBC = D_INNER + 2 * NHEADS * G
        D_IN_PROJ = 2 * D_INNER + 2 * NHEADS * G + NHEADS

        def rmsnorm(x, w, eps=1e-05):
            return x * w * jax.lax.rsqrt(jnp.mean(x * x, axis=-1, keepdims=True) + eps)

        def _mamba3(u, in_proj_w, conv_w, conv_b, dt_bias, A_log, D_skip, gnorm_w, out_proj_w):
            B, L, _ = u.shape
            H, P = (NHEADS, HEADDIM)
            nc = L // CHUNK
            zxbcdt = u @ in_proj_w.T
            z, xbc, dt_raw = jnp.split(zxbcdt, [D_INNER, D_INNER + D_XBC], axis=-1)
            xp = jnp.pad(xbc, ((0, 0), (D_CONV - 1, 0), (0, 0)))
            conv = conv_b + sum((xp[:, k:k + L, :] * conv_w[:, k] for k in range(D_CONV)))
            xbc = jax.nn.silu(conv)
            xh, Bm, Cm = jnp.split(xbc, [D_INNER, D_INNER + H * G], axis=-1)
            Xc = xh.reshape(B, nc, CHUNK, H, P)
            Bc = Bm.reshape(B, nc, CHUNK, H, G)
            Cc = Cm.reshape(B, nc, CHUNK, H, G)
            dt = jax.nn.softplus(dt_raw + dt_bias)
            A = -jnp.exp(A_log)
            dtc = dt.reshape(B, nc, CHUNK, H)
            a = dtc * A
            cum = jnp.cumsum(a, axis=2)
            cumT = cum.transpose(0, 1, 3, 2)
            diff = cumT[..., :, None] - cumT[..., None, :]
            mask = jnp.tril(jnp.ones((CHUNK, CHUNK), bool))
            decay = jnp.where(mask, jnp.exp(jnp.where(mask, diff, 0.0)), 0.0)
            dtT = dtc.transpose(0, 1, 3, 2)
            scores = jnp.einsum('bclhg,bcshg->bchls', Cc, Bc) * decay * dtT[:, :, :, None, :]
            Y_intra = jnp.einsum('bchls,bcshp->bclhp', scores, Xc)
            w = jnp.exp(cum[:, :, -1:, :] - cum) * dtc
            S = jnp.einsum('bcshg,bcshp->bchgp', Bc * w[..., None], Xc)
            dlast = jnp.exp(cum[:, :, -1, :])

            def step(carry, inp):
                dl, s = inp
                return (dl[:, :, None, None] * carry + s, carry)
            init = jnp.zeros((B, H, G, P), u.dtype)
            _, Hprev = jax.lax.scan(step, init, (dlast.transpose(1, 0, 2), S.transpose(1, 0, 2, 3, 4)))
            Hprev = Hprev.transpose(1, 0, 2, 3, 4)
            Y_inter = jnp.einsum('bclhg,bchgp->bclhp', Cc * jnp.exp(cum)[..., None], Hprev)
            y = (Y_intra + Y_inter + D_skip[:, None] * Xc).reshape(B, L, D_INNER)
            y = rmsnorm(y * jax.nn.silu(z), gnorm_w)
            return y @ out_proj_w.T
        key = jax.random.key(seed)
        ks = jax.random.split(key, 8)
        B, L = (2, 512)
        x = jax.random.normal(ks[0], (B, L, D_MODEL), jnp.float32)
        norm_w = jnp.ones((D_MODEL,), jnp.float32)
        in_proj_w = jax.random.normal(ks[1], (D_IN_PROJ, D_MODEL), jnp.float32) * 0.02
        conv_w = jax.random.normal(ks[2], (D_XBC, D_CONV), jnp.float32) * 0.2
        conv_b = jnp.zeros((D_XBC,), jnp.float32)
        dt_bias = jax.random.uniform(ks[3], (NHEADS,), jnp.float32, minval=-4.0, maxval=-1.0)
        A_log = jnp.log(jax.random.uniform(ks[4], (NHEADS,), jnp.float32, minval=1.0, maxval=8.0))
        D_skip = jnp.ones((NHEADS,), jnp.float32)
        gnorm_w = jnp.ones((D_INNER,), jnp.float32)
        out_proj_w = jax.random.normal(ks[5], (D_MODEL, D_INNER), jnp.float32) * 0.02
        return dict(x=x, norm_w=norm_w, in_proj_w=in_proj_w, conv_w=conv_w, conv_b=conv_b, dt_bias=dt_bias, A_log=A_log, D_skip=D_skip, gnorm_w=gnorm_w, out_proj_w=out_proj_w)
    _L0_attn_in = _L0_attn_setup()

    def _L0_ffn_setup():
        import jax, jax.numpy as jnp
        import numpy as np
        B, T, H = (2, 512, 256)
        I = 1024
        HEADS = 4
        RET = 128
        NUM_EXPERTS = 1024
        NUM_KEYS = 64
        K = 8
        key = jax.random.key(seed)
        ks = jax.random.split(key, 7)
        return {'hidden_states': jax.random.normal(ks[0], (B, T, H), jnp.float32), 'W_up': jax.random.normal(ks[1], (I, H), jnp.float32) * 0.02, 'W_down': jax.random.normal(ks[2], (H, I), jnp.float32) * 0.02, 'W_q': jax.random.normal(ks[3], (HEADS * RET, H), jnp.float32) * 0.02, 'keys': jax.random.normal(ks[4], (HEADS, NUM_KEYS, 2, RET // 2), jnp.float32) * 0.02, 'down_embed': jax.random.normal(ks[5], (NUM_EXPERTS, H), jnp.float32) * 0.02, 'up_embed': jax.random.normal(ks[6], (NUM_EXPERTS, H), jnp.float32) * 0.02}
    _L0_ffn_in = _L0_ffn_setup()
    _d = {'L0_attn_x': _L0_attn_in['x'], 'L0_attn_norm_w': _L0_attn_in['norm_w'], 'L0_attn_in_proj_w': _L0_attn_in['in_proj_w'], 'L0_attn_conv_w': _L0_attn_in['conv_w'], 'L0_attn_conv_b': _L0_attn_in['conv_b'], 'L0_attn_dt_bias': _L0_attn_in['dt_bias'], 'L0_attn_A_log': _L0_attn_in['A_log'], 'L0_attn_D_skip': _L0_attn_in['D_skip'], 'L0_attn_gnorm_w': _L0_attn_in['gnorm_w'], 'L0_attn_out_proj_w': _L0_attn_in['out_proj_w'], 'L0_ffn_W_up': _L0_ffn_in['W_up'], 'L0_ffn_W_down': _L0_ffn_in['W_down'], 'L0_ffn_W_q': _L0_ffn_in['W_q'], 'L0_ffn_keys': _L0_ffn_in['keys'], 'L0_ffn_down_embed': _L0_ffn_in['down_embed'], 'L0_ffn_up_embed': _L0_ffn_in['up_embed']}
    _x0 = _d['L0_attn_x']
    _d['L0_attn_x'] = jax.random.normal(jax.random.fold_in(jax.random.key(seed), 1), (8, 1024, 256), dtype=_x0.dtype)
    del _x0
    return _d

def reference(L0_attn_x, L0_attn_norm_w, L0_attn_in_proj_w, L0_attn_conv_w, L0_attn_conv_b, L0_attn_dt_bias, L0_attn_A_log, L0_attn_D_skip, L0_attn_gnorm_w, L0_attn_out_proj_w, L0_ffn_W_up, L0_ffn_W_down, L0_ffn_W_q, L0_ffn_keys, L0_ffn_down_embed, L0_ffn_up_embed):

    def _L0_attn_ref(x, norm_w, in_proj_w, conv_w, conv_b, dt_bias, A_log, D_skip, gnorm_w, out_proj_w):
        import jax, jax.numpy as jnp
        import numpy as np
        D_MODEL = 256
        D_STATE = 64
        HEADDIM = 64
        MIMO_RANK = 2
        CHUNK = 128
        EXPAND = 2
        D_INNER = EXPAND * D_MODEL
        NHEADS = D_INNER // HEADDIM
        G = MIMO_RANK * D_STATE
        D_CONV = 4
        D_XBC = D_INNER + 2 * NHEADS * G
        D_IN_PROJ = 2 * D_INNER + 2 * NHEADS * G + NHEADS

        def rmsnorm(x, w, eps=1e-05):
            return x * w * jax.lax.rsqrt(jnp.mean(x * x, axis=-1, keepdims=True) + eps)

        def _mamba3(u, in_proj_w, conv_w, conv_b, dt_bias, A_log, D_skip, gnorm_w, out_proj_w):
            B, L, _ = u.shape
            H, P = (NHEADS, HEADDIM)
            nc = L // CHUNK
            zxbcdt = u @ in_proj_w.T
            z, xbc, dt_raw = jnp.split(zxbcdt, [D_INNER, D_INNER + D_XBC], axis=-1)
            xp = jnp.pad(xbc, ((0, 0), (D_CONV - 1, 0), (0, 0)))
            conv = conv_b + sum((xp[:, k:k + L, :] * conv_w[:, k] for k in range(D_CONV)))
            xbc = jax.nn.silu(conv)
            xh, Bm, Cm = jnp.split(xbc, [D_INNER, D_INNER + H * G], axis=-1)
            Xc = xh.reshape(B, nc, CHUNK, H, P)
            Bc = Bm.reshape(B, nc, CHUNK, H, G)
            Cc = Cm.reshape(B, nc, CHUNK, H, G)
            dt = jax.nn.softplus(dt_raw + dt_bias)
            A = -jnp.exp(A_log)
            dtc = dt.reshape(B, nc, CHUNK, H)
            a = dtc * A
            cum = jnp.cumsum(a, axis=2)
            cumT = cum.transpose(0, 1, 3, 2)
            diff = cumT[..., :, None] - cumT[..., None, :]
            mask = jnp.tril(jnp.ones((CHUNK, CHUNK), bool))
            decay = jnp.where(mask, jnp.exp(jnp.where(mask, diff, 0.0)), 0.0)
            dtT = dtc.transpose(0, 1, 3, 2)
            scores = jnp.einsum('bclhg,bcshg->bchls', Cc, Bc) * decay * dtT[:, :, :, None, :]
            Y_intra = jnp.einsum('bchls,bcshp->bclhp', scores, Xc)
            w = jnp.exp(cum[:, :, -1:, :] - cum) * dtc
            S = jnp.einsum('bcshg,bcshp->bchgp', Bc * w[..., None], Xc)
            dlast = jnp.exp(cum[:, :, -1, :])

            def step(carry, inp):
                dl, s = inp
                return (dl[:, :, None, None] * carry + s, carry)
            init = jnp.zeros((B, H, G, P), u.dtype)
            _, Hprev = jax.lax.scan(step, init, (dlast.transpose(1, 0, 2), S.transpose(1, 0, 2, 3, 4)))
            Hprev = Hprev.transpose(1, 0, 2, 3, 4)
            Y_inter = jnp.einsum('bclhg,bchgp->bclhp', Cc * jnp.exp(cum)[..., None], Hprev)
            y = (Y_intra + Y_inter + D_skip[:, None] * Xc).reshape(B, L, D_INNER)
            y = rmsnorm(y * jax.nn.silu(z), gnorm_w)
            return y @ out_proj_w.T
        return x + _mamba3(rmsnorm(x, norm_w), in_proj_w, conv_w, conv_b, dt_bias, A_log, D_skip, gnorm_w, out_proj_w)

    def _L0_ffn_ref(hidden_states, W_up, W_down, W_q, keys, down_embed, up_embed):
        import jax, jax.numpy as jnp
        import numpy as np
        B, T, H = (2, 512, 256)
        I = 1024
        HEADS = 4
        RET = 128
        NUM_EXPERTS = 1024
        NUM_KEYS = 64
        K = 8
        b, t, hd = hidden_states.shape
        h, nk, _, n = keys.shape
        q = jnp.einsum('btd,ed->bte', hidden_states, W_q)
        q = q.reshape(b, t, 2, h, n).transpose(2, 0, 1, 3, 4)
        sim = jnp.einsum('pbthn,hkpn->pbthk', q, keys)
        scores_xy, idx_xy = jax.lax.top_k(sim, K)
        sx, sy = (scores_xy[0], scores_xy[1])
        ix, iy = (idx_xy[0], idx_xy[1])
        all_scores = (sx[..., :, None] + sy[..., None, :]).reshape(b, t, h, K * K)
        all_idx = (ix[..., :, None] * nk + iy[..., None, :]).reshape(b, t, h, K * K)
        scores, pk = jax.lax.top_k(all_scores, K)
        indices = jnp.take_along_axis(all_idx, pk, axis=-1)
        de = down_embed[indices]
        ue = up_embed[indices]
        w = jax.nn.silu(jnp.einsum('btd,bthkd->bthk', hidden_states, de) * jax.nn.softmax(scores, axis=-1))
        experts_states = jnp.einsum('bthk,bthkd->btd', w, ue)
        dense = jnp.einsum('bti,di->btd', jax.nn.silu(jnp.einsum('btd,id->bti', hidden_states, W_up)), W_down)
        return dense + experts_states
    x = L0_attn_x
    x = x + _layernorm(_L0_attn_ref(_layernorm(x, axis=-1), L0_attn_norm_w, L0_attn_in_proj_w, L0_attn_conv_w, L0_attn_conv_b, L0_attn_dt_bias, L0_attn_A_log, L0_attn_D_skip, L0_attn_gnorm_w, L0_attn_out_proj_w), axis=-1)
    x = x + _layernorm(_L0_ffn_ref(_layernorm(x, axis=-1), L0_ffn_W_up, L0_ffn_W_down, L0_ffn_W_q, L0_ffn_keys, L0_ffn_down_embed, L0_ffn_up_embed), axis=-1)
    return x

_drawn_inputs = setup_inputs


def setup_inputs(seed=0):
    import zlib

    import numpy as np

    out = dict(_drawn_inputs(seed))
    spreads = {'L0_attn_norm_w': (1.0, 0.2),
     'L0_attn_conv_b': (0.0, 0.1),
     'L0_attn_D_skip': (1.0, 0.553),
     'L0_attn_gnorm_w': (1.0, 0.2)}
    factors = {'L0_attn_dt_bias': 8.0, 'L0_attn_A_log': 8.0, 'L0_ffn_W_q': 6.482, 'L0_ffn_keys': 6.462}
    for name, (base, spread) in spreads.items():
        noise = np.random.default_rng([zlib.crc32(name.encode()), seed]).standard_normal(out[name].shape)
        drawn = base * np.exp(spread * noise) if base else spread * noise
        out[name] = jnp.asarray(drawn.astype(out[name].dtype))
    for name, factor in factors.items():
        out[name] = (out[name] * factor).astype(out[name].dtype)
    return out
```

```python
from contextlib import ExitStack

import concourse.bass as bass
from concourse import mybir

P = 128
ALU = mybir.AluOpType
ACT = mybir.ActivationFunctionType
BF16 = mybir.dt.bfloat16
F32 = mybir.dt.float32
U32 = mybir.dt.uint32
AX_X = mybir.AxisListType.X

D = 256
DK = D // P
HEADS = 8
HD = 64
G = 128
INNER = HEADS * HD
XBC = INNER + 2 * HEADS * G
PROJ = INNER + XBC + HEADS
TAPS = 4
CHUNK = 128
CH = 2
TOK = CH * CHUNK
TILES = XBC // P
PAIRS = TILES // 2
XP, BP = INNER // TOK, HEADS // 2
FF = 1024
FT = FF // P
EXPERTS = 1024
ET = EXPERTS // P
RH = 4
KEYS = 64
XD = EXPERTS // KEYS
TOP = 8
CAND = [(0, 1, 8), (1, 1, 4), (2, 2, 2), (4, 4, 1)]
NC = sum(r * n for _, r, n in CAND)
EPS = 1e-5
LOWEST = -3.0e38
MASKED = -1.0e30
FLT_MAX = 3.4028234e38


class Sig:

    def __init__(self, sem, per=1):
        self.sem, self.per = sem, per

    def at(self, group, k=0):
        return group * self.per + k + 1


def later(group):
    return not (isinstance(group, int) and group == 0)


class Steps:

    def __init__(self):
        self.n = 0

    def one(self):
        self.n += 1
        return 1

    def restart(self):
        self.n = 0


def sandwich(nc, x, in_wT, norm_w, conv_w, conv_b, dt_bias, A_log, D_skip, gnorm_w, out_wT,
             upT, downT, wq, keysT, down_eT, up_e, out):
    NG = x.shape[0] // TOK
    SEQ = 1024 // TOK
    xv = x.rearrange("(g c p) d -> g p c d", c=CH, p=P)
    ov = out.rearrange("(g c p) d -> g p c d", c=CH, p=P)

    with ExitStack() as ctx:
        def sb(name, shape, dt=F32):
            return ctx.enter_context(nc.sbuf_tensor(name, shape, dt))

        def sem(name):
            return ctx.enter_context(nc.semaphore(name))

        def sig(name, per=1):
            return Sig(sem(name), per)

        w_in = sb("w_in", [P, DK, PROJ])
        w_out = sb("w_out", [P, INNER // P, D])
        w_up = sb("w_up", [P, DK, FF])
        w_down = sb("w_down", [P, FT, D])
        w_de = sb("w_de", [P, DK, EXPERTS])
        w_ue = sb("w_ue", [P, ET, D])
        w_sim = sb("w_sim", [P, DK, 2 * RH * KEYS])
        cw = sb("cw", [P, TILES, TAPS])
        cb = sb("cb", [P, TILES])
        nw = sb("nw", [P, DK])
        gw = sb("gw", [P, INNER // P])
        head_c = sb("head_c", [P, 3, HEADS])
        neg_a = sb("neg_a", [P, HEADS])
        tri = sb("tri", [P, P])
        ones = sb("ones", [P, P])
        ident = sb("ident", [P, P])
        ident_b = sb("ident_b", [P, P], BF16)
        mask_b = sb("mask_b", [P, 4, P], BF16)
        iota = sb("iota", [P, KEYS, TOP])
        rank_w = sb("rank_w", [P, TOP])
        keep_tab = sb("keep_tab", [P, 2, NG])
        half_neg = sb("half_neg", [P, 2 * CH])

        x_in = sb("x_in", [P, CH, D])
        x_res = sb("x_res", [P, CH, D])
        u = sb("u", [P, CH, D])
        hn = sb("hn", [P, CH, D])
        hT = sb("hT", [P, DK, TOK])
        xp = sb("xp", [P, 2, 2, TAPS - 1 + TOK])
        acc = sb("acc", [P, 2, 2, TOK])
        halo = sb("halo", [P, TILES, TAPS - 1])
        xbcT = sb("xbcT", [P, TILES, TOK])
        keep = sb("keep", [P, 2])
        dt0 = sb("dt0", [P, CH, HEADS])
        dt1 = sb("dt1", [P, CH, HEADS])
        dt2 = sb("dt2", [P, CH, HEADS])
        dte = sb("dte", [P, CH, HEADS])
        dts = sb("dts", [P, CH, HEADS])
        da = sb("da", [P, CH, HEADS])
        cum = sb("cum", [P, 3, CH, HEADS])
        ecum = sb("ecum", [P, 3, CH, HEADS])
        ncum = sb("ncum", [P, CH, HEADS])
        lnst = sb("lnst", [P, CH, 6])
        mv1 = sb("mv1", [P, CH, 2])
        mv2 = sb("mv2", [P, CH, 2])
        mv3 = sb("mv3", [P, CH, 2])
        rs1 = sb("rs1", [P, CH])
        rs1b = sb("rs1b", [P, CH])
        rs2 = sb("rs2", [P, CH])
        ve = sb("ve", [P, 2 * CH])
        rsy = sb("rsy", [P, CH])
        rs3 = sb("rs3", [P, CH])
        rs4 = sb("rs4", [P, CH])
        Xt = sb("Xt", [P, INNER])
        Xdt = sb("Xdt", [P, INNER])
        Xw = sb("Xw", [P, INNER])
        DX = sb("DX", [P, INNER])
        Btok = sb("Btok", [P, HEADS, G])
        Ldec = sb("Ldec", [P, HEADS, CHUNK])
        sL = sb("sL", [P, HEADS, CHUNK])
        H = sb("H", [P, INNER])
        zs = sb("zs", [P, INNER])
        yv = sb("yv", [P, CH, INNER])
        ysq = sb("ysq", [P, INNER])
        ssq = sb("ssq", [P, CH])
        yT = sb("yT", [P, CH, INNER])
        v = sb("v", [P, CH, D])
        x1 = sb("x1", [P, CH, D])
        h2 = sb("h2", [P, CH, D])
        h2T = sb("h2T", [P, DK, TOK])

        hid = sb("hid", [P, FT, TOK])
        sim = sb("sim", [P, 2, RH, KEYS])
        s8 = sb("s8", [P, 2, RH, TOP])
        i8 = sb("i8", [P, 2, RH, TOP], U32)
        cand = sb("cand", [P, RH, NC])
        c8 = sb("c8", [P, RH, TOP])
        rest = sb("rest", [P, RH, NC])
        chosen = sb("chosen", [P, RH, NC])
        n8 = sb("n8", [P, RH, TOP])
        earg = sb("earg", [P, RH, XD + KEYS + NC])
        ee = sb("ee", [P, RH, XD + KEYS + NC])
        psel = sb("psel", [P, RH, NC])
        psum8 = sb("psum8", [P, RH])
        rden = sb("rden", [P, RH])
        cmask = sb("cmask", [P, RH, TOP])
        clz = sb("clz", [P, RH, NC])
        cls = sb("cls", [P, RH, NC])
        clsum = sb("clsum", [P, 1])
        eqx = sb("eqx", [P, RH, XD, TOP])
        i8b = sb("i8b", [P, 2, RH, TOP])
        eqy = sb("eqy", [P, KEYS, TOP])
        nx = sb("nx", [P, RH, XD])
        ry = sb("ry", [P, RH, KEYS])
        Dm = sb("Dm", [P, RH, XD, KEYS], BF16)
        Em = sb("Em", [P, 2, XD, KEYS])
        Z = sb("Z", [P, 2, EXPERTS])
        W = sb("W", [P, EXPERTS])
        WT = sb("WT", [P, ET, P])
        f = sb("f", [P, CH, D])
        fst = sb("fst", [P, CH, 6])
        mvf = sb("mvf", [P, CH, 2])
        vf = sb("vf", [P, CH])
        rsf = sb("rsf", [P, CH])

        pool_psum = [ctx.enter_context(nc.psum_tensor(f"bank{i}", [P, 512], F32)) for i in range(8)]
        ring = pool_psum[0:2]
        pairb = pool_psum[2:4]
        yb = pool_psum[4]
        f0 = pool_psum[5]
        fA = pool_psum[6:8]

        loaded_c = sem("loaded_c")
        loaded_w = sem("loaded_w")
        consts = sem("consts")
        folded = sem("folded")
        simw_ps, simw_sb = sem("simw_ps"), sem("simw_sb")
        x_loaded, xres_loaded = sem("x_loaded"), sem("xres_loaded")
        x_read = sig("x_read")
        stored = sem("stored")
        own_dve, own_act, own_pool = sem("own_dve"), sem("own_act"), sem("own_pool")
        arrived_dve, arrived_act, arrived_pool = sem("arrived_dve"), sem("arrived_act"), sem("arrived_pool")
        stats1, root1 = sig("stats1"), sig("root1")
        hn_done, hT_ps, hT_sb = sig("hn_done"), sig("hT_ps"), sig("hT_sb")
        dt_ps, dt_read = sig("dt_ps"), sig("dt_read")
        dte_done, da_done = sig("dte_done"), sig("da_done")
        cum_ps, cum_read, cum_sb, ecum_done = sig("cum_ps"), sig("cum_read"), sig("cum_sb"), sig("ecum_done")
        pair_ps, pair_copied, pair_read = sig("pair_ps", PAIRS), sig("pair_copied", PAIRS), sig("pair_read", PAIRS)
        halo_in, halo_out = sig("halo_in", PAIRS), sig("halo_out", PAIRS)
        conv_done, silu_done = sig("conv_done", PAIRS), sig("silu_done", PAIRS)
        rows_ps, decay_done = sig("rows_ps", 2 * CH), sig("decay_done", 2 * CH)
        X_ps, X_sb, z_ps, z_done = sig("X_ps", CH), sig("X_sb", CH), sig("z_ps", CH), sig("z_done", CH)
        Bt_ps, Bt_sb = sig("Bt_ps", 2 * CH), sig("Bt_sb", 2 * CH)
        sc_ps, sL_done = sig("sc_ps", 2 * CH), sig("sL_done", 2 * CH)
        Yi_ps, Yi_read = sig("Yi_ps", CH), sig("Yi_read", CH)
        Xw_done, DX_done = sig("Xw_done", CH), sig("DX_done", CH)
        S_ps, H_done = sig("S_ps", CH), sig("H_done", CH)
        H_kept = sig("H_kept")
        Yn_ps, Yn_read = sig("Yn_ps", CH), sig("Yn_read", CH)
        y_done, sq_done = sig("y_done", CH), sig("sq_done", CH)
        yT_ps, yT_sb = sig("yT_ps", CH), sig("yT_sb", CH)
        rooty = sig("rooty")
        out_ps, out_read = sig("out_ps"), sig("out_read")
        stats3, root3, stats4, root4 = sig("stats3"), sig("root3"), sig("stats4"), sig("root4")
        h2_done, h2T_ps, h2T_sb = sig("h2_done"), sig("h2T_ps"), sig("h2T_sb")
        xres_read = sig("xres_read")
        sim_ps, sim_sb = sig("sim_ps", CH), sig("sim_sb", CH)
        A_ps, A_read = sig("A_ps", CH), sig("A_read", CH)
        up_ps, up_done = sig("up_ps", FT // 2), sig("up_done", FT // 2)
        earg_done, ee_done = sig("earg_done", CH), sig("ee_done", CH)
        dense_in = sig("dense_in", CH)
        D_done, Z_done, Zs_done, Em_done = (sig(n, CH * RH) for n in ("D_done", "Z_done", "Zs_done", "Em_done"))
        P_done = sig("P_done", CH * RH)
        clz_done, cls_done = sig("clz_done", CH), sig("cls_done", CH)
        Wsum_done, W_done = sig("Wsum_done", CH), sig("W_done", CH)
        WT_ps, WT_sb = sig("WT_ps", 2 * CH), sig("WT_sb", 2 * CH)
        f_ps, f_sb = sig("f_ps", CH), sig("f_sb", CH)
        statsf, rootf, o_done = sig("statsf"), sig("rootf"), sig("o_done")

        block = ctx.enter_context(nc.Block())

        def bc(ap, axis, n):
            return ap.unsqueeze(axis).to_broadcast([*ap.shape[:axis], n, *ap.shape[axis:]])

        @block.sync
        def _(sp):
            sp.dma_start(x_in[:], xv[0]).then_inc(x_loaded, 16)
            sp.dma_start(nw[:], norm_w).then_inc(loaded_c, 16)
            sp.dma_start(gw[:], gnorm_w).then_inc(loaded_c, 16)
            sp.dma_start(cw[:], conv_w).then_inc(loaded_c, 16)
            sp.dma_start(cb[:], conv_b).then_inc(loaded_c, 16)
            sp.dma_start(head_c[:, 0, :], dt_bias).then_inc(loaded_c, 16)
            sp.dma_start(head_c[:, 1, :], A_log).then_inc(loaded_c, 16)
            sp.dma_start(head_c[:, 2, :], D_skip).then_inc(loaded_c, 16)
            sp.dma_start(hid[0:64, :, :], wq).then_inc(loaded_c, 16)
            sp.dma_start(xbcT[0:64, 0:2, :], keysT).then_inc(loaded_c, 16)
            sp.dma_start(w_in[:], in_wT).then_inc(loaded_w, 16)
            sp.dma_start(w_out[:], out_wT).then_inc(loaded_w, 16)
            sp.dma_start(w_up[:], upT).then_inc(loaded_w, 16)
            sp.dma_start(w_de[:], down_eT).then_inc(loaded_w, 16)
            sp.dma_start(w_down[:], downT).then_inc(loaded_w, 16)
            sp.dma_start(w_ue[:], up_e).then_inc(loaded_w, 16)

            def mixer(g, more):
                if later(g):
                    sp.wait_ge(xres_read.sem, xres_read.at(g - 1))
                sp.dma_start(x_res[:], xv[g]).then_inc(xres_loaded, 16)
                if more:
                    sp.wait_ge(x_read.sem, x_read.at(g))
                    sp.dma_start(x_in[:], xv[g + 1]).then_inc(x_loaded, 16)

            def ffn(e):
                sp.wait_ge(o_done.sem, o_done.at(e))
                sp.dma_start(ov[e], f[:]).then_inc(stored, 16)

            mixer(0, True)
            mixer(1, True)
            ffn(0)
            with sp.Fori(2, NG - 1) as g:
                mixer(g, True)
                ffn(g - 1)
            mixer(NG - 1, False)
            ffn(NG - 2)
            ffn(NG - 1)
            sp.wait_ge(stored, 16 * NG)

        @block.gpsimd
        def _(pool):
            own = Steps()
            nc.gpsimd.memset(tri[:], 1.0).then_inc(own_pool, own.one())
            nc.gpsimd.memset(ones[:], 1.0).then_inc(own_pool, own.one())
            nc.gpsimd.memset(ident[:], 0.0).then_inc(own_pool, own.one())
            nc.gpsimd.memset(mask_b[:], 0.0).then_inc(own_pool, own.one())
            nc.gpsimd.memset(halo[:], 0.0).then_inc(own_pool, own.one())
            nc.gpsimd.memset(H[:], 0.0).then_inc(own_pool, own.one())
            nc.gpsimd.memset(half_neg[:], -0.5).then_inc(own_pool, own.one())
            nc.gpsimd.memset(keep_tab[:, 0], FLT_MAX).then_inc(own_pool, own.one())
            nc.gpsimd.memset(keep_tab[:, 1], -FLT_MAX).then_inc(own_pool, own.one())
            for r in range(TOP):
                nc.gpsimd.memset(rank_w[:, r:r + 1], float(TOP - r)).then_inc(own_pool, own.one())
            nc.gpsimd.iota(iota[:], pattern=[[1, KEYS], [0, TOP]], base=0, channel_multiplier=0,
                                  allow_small_or_imprecise_dtypes=True).then_inc(own_pool, own.one())
            pool.wait_ge(own_pool, own.n)
            nc.gpsimd.memset(keep_tab[:, :, 0:NG:SEQ], 0.0).then_inc(own_pool, own.one())
            nc.gpsimd.affine_select(out=tri[:], in_=tri[:], compare_op=ALU.is_ge, fill=0.0,
                                           base=0, pattern=[[1, P]], channel_multiplier=-1).then_inc(own_pool, own.one())
            nc.gpsimd.affine_select(out=mask_b[:], in_=mask_b[:], compare_op=ALU.is_ge, fill=MASKED,
                                           base=0, pattern=[[0, 4], [1, P]], channel_multiplier=-1).then_inc(own_pool, own.one())
            nc.gpsimd.affine_select(out=ident[:], in_=ident[:], compare_op=ALU.not_equal, fill=1.0,
                                           base=0, pattern=[[-1, P]], channel_multiplier=1).then_inc(own_pool, own.one())
            pool.wait_ge(own_pool, own.n)
            nc.gpsimd.tensor_copy(ident_b[:], ident[:]).then_inc(consts, 1)
            pool.wait_ge(own_pool, own.n)
            pool.sem_clear(own_pool)
            own.restart()

            def mixer_norm(g):
                pool.wait_ge(stats1.sem, stats1.at(g))
                pool.sem_inc(arrived_pool, 1)
                nc.gpsimd.tensor_scalar(ve[:, 0:CH], mv1[:, :, 1], EPS, None, ALU.add).then_inc(own_pool, own.one())
                pool.wait_ge(own_pool, own.n)
                nc.gpsimd.tensor_tensor(rs1[:], ve[:, 0:CH], half_neg[:, 0:CH], ALU.pow).then_inc(own_pool, own.one())
                pool.wait_ge(own_pool, own.n)
                nc.gpsimd.tensor_tensor(rs1b[:], rs1[:], rs1[:], ALU.mult).then_inc(own_pool, own.one())
                pool.wait_ge(own_pool, own.n)
                nc.gpsimd.tensor_tensor(ve[:, CH:2 * CH], rs1b[:], mv1[:, :, 1], ALU.mult).then_inc(own_pool, own.one())
                pool.wait_ge(own_pool, own.n)
                nc.gpsimd.tensor_scalar(ve[:, CH:2 * CH], ve[:, CH:2 * CH], EPS, None, ALU.add).then_inc(own_pool, own.one())
                pool.wait_ge(own_pool, own.n)
                nc.gpsimd.tensor_tensor(rs2[:], ve[:, CH:2 * CH], half_neg[:, 0:CH], ALU.pow).then_inc(root1.sem, 1)
            def mixer_halo(g):
                for j in range(PAIRS):
                    r = j % 2
                    if j >= 2:
                        pool.wait_ge(conv_done.sem, conv_done.at(g, j - 2))
                    else:
                        if later(g):
                            pool.wait_ge(conv_done.sem, conv_done.at(g - 1, PAIRS - 2 + j))
                    if j == 0:
                        pool.wait_ge(hn_done.sem, hn_done.at(g))
                    pool.sem_inc(arrived_pool, 1)
                    nc.gpsimd.tensor_scalar(xp[:, r, :, 0:TAPS - 1], halo[:, 2 * j:2 * j + 2, :], keep[:, 0:1], keep[:, 1:2],
                                            ALU.min, ALU.max).then_inc(halo_in.sem, 1)
                    pool.wait_ge(pair_copied.sem, pair_copied.at(g, j))
                    pool.wait_ge(halo_in.sem, halo_in.at(g, j))
                    pool.sem_inc(arrived_pool, 1)
                    nc.gpsimd.tensor_copy(halo[:, 2 * j:2 * j + 2, :], xp[:, r, :, TOK:TOK + TAPS - 1])\
                        .then_inc(halo_out.sem, 1)

            def mixer_skip(g, c):
                pool.wait_ge(X_sb.sem, X_sb.at(g, c))
                nc.gpsimd.tensor_tensor(DX[:].rearrange("p (h d) -> p h d", h=HEADS),
                                        Xt[:].rearrange("p (h d) -> p h d", h=HEADS),
                                        bc(head_c[:, 2, :], 2, HD), ALU.mult).then_inc(DX_done.sem, 1)

            def experts(e, c):
                pool.wait_ge(dense_in.sem, dense_in.at(e, c))
                for h in range(RH):
                    if c or later(e):
                        pool.wait_ge(P_done.sem, P_done.at(e, (c - 1) * RH + h))
                    nc.gpsimd.tensor_tensor(Dm[:, h], bc(nx[:, h, :], 2, KEYS), bc(ry[:, h, :], 1, XD),
                                            ALU.add).then_inc(D_done.sem, 1)

            def do_group(g, e):
                if g is not None:
                    mixer_norm(g)
                if e is not None:
                    experts(e, 0)
                if g is not None:
                    mixer_halo(g)
                    mixer_skip(g, 0)
                if e is not None:
                    experts(e, 1)
                if g is not None:
                    mixer_skip(g, 1)
                    pool.wait_ge(sq_done.sem, sq_done.at(g, CH - 1))
                    pool.sem_inc(arrived_pool, 1)
                    nc.gpsimd.tensor_scalar(ve[:, 0:CH], ssq[:], 1.0 / INNER, EPS, ALU.mult, ALU.add).then_inc(own_pool, own.one())
                    pool.wait_ge(own_pool, own.n)
                    nc.gpsimd.tensor_tensor(rsy[:], ve[:, 0:CH], half_neg[:, 0:CH], ALU.pow).then_inc(rooty.sem, 1)
                if e is not None:
                    pool.wait_ge(statsf.sem, statsf.at(e))
                    pool.sem_inc(arrived_pool, 1)
                    nc.gpsimd.tensor_scalar(vf[:], mvf[:, :, 1], EPS, None, ALU.add).then_inc(own_pool, own.one())
                    pool.wait_ge(own_pool, own.n)
                    nc.gpsimd.tensor_tensor(rsf[:], vf[:], half_neg[:, 0:CH], ALU.pow).then_inc(rootf.sem, 1)
                if g is not None:
                    pool.wait_ge(rooty.sem, rooty.at(g))
                    pool.sem_inc(arrived_pool, 1)
                    for stats, mv, dst, done in ((stats3, mv2, rs3, root3), (stats4, mv3, rs4, root4)):
                        pool.wait_ge(stats.sem, stats.at(g))
                        pool.sem_inc(arrived_pool, 1)
                        nc.gpsimd.tensor_scalar(ve[:, 0:CH], mv[:, :, 1], EPS, None, ALU.add).then_inc(own_pool, own.one())
                        pool.wait_ge(own_pool, own.n)
                        nc.gpsimd.tensor_tensor(dst[:], ve[:, 0:CH], half_neg[:, 0:CH], ALU.pow)\
                            .then_inc(done.sem, 1)
                pool.wait_ge(own_pool, own.n)
                pool.sem_clear(own_pool)
                own.restart()

            do_group(0, None)
            do_group(1, 0)
            with pool.Fori(2, NG) as g:
                do_group(g, g - 1)
            do_group(None, NG - 1)

        @block.scalar
        def _(act):
            own = Steps()
            act.wait_ge(loaded_c, 16 * 9)
            nc.scalar.activation(neg_a[:], head_c[:, 1, :], ACT.Exp).then_inc(own_act, own.one())
            for k in range(DK):
                act.wait_ge(simw_ps, k + 1)
                nc.scalar.activation(w_sim[:, k, :], ring[k][:, :], ACT.Copy).then_inc(own_act, own.one())
            act.wait_ge(own_act, own.n)
            act.sem_inc(simw_sb, 1)
            act.wait_ge(own_act, own.n)
            act.sem_clear(own_act)
            own.restart()

            def mixer_hT(g):
                act.wait_ge(hT_ps.sem, hT_ps.at(g))
                nc.scalar.activation(hT[:], ring[0][:].rearrange("p (k t) -> p k t", k=DK), ACT.Copy)\
                    .then_inc(hT_sb.sem, 1)

            def mixer_dt(g):
                act.wait_ge(dt_read.sem, dt_read.at(g))
                nc.scalar.activation(dte[:], dt1[:], ACT.Exp, scale=-1.0).then_inc(dte_done.sem, 1)

            def mixer_pairs(g):
                def silu(j):
                    act.wait_ge(conv_done.sem, conv_done.at(g, j))
                    nc.scalar.activation(xbcT[:, 2 * j:2 * j + 2, :], acc[:, j % 2], ACT.Silu)\
                        .then_inc(silu_done.sem, 1)

                for j in range(PAIRS):
                    r = j % 2
                    ps = ring[j % 2]
                    act.wait_ge(pair_ps.sem, pair_ps.at(g, j))
                    if j >= 2:
                        act.wait_ge(conv_done.sem, conv_done.at(g, j - 2))
                        act.wait_ge(halo_out.sem, halo_out.at(g, j - 2))
                    else:
                        if later(g):
                            act.wait_ge(conv_done.sem, conv_done.at(g - 1, PAIRS - 2 + j))
                        if later(g):
                            act.wait_ge(halo_out.sem, halo_out.at(g - 1, PAIRS - 2 + j))
                    nc.scalar.activation(xp[:, r, :, TAPS - 1:], ps[:].rearrange("p (a t) -> p a t", a=2), ACT.Copy)\
                        .then_inc(pair_copied.sem, 1)
                    if j >= 2:
                        act.wait_ge(silu_done.sem, silu_done.at(g, j - 2))
                    else:
                        if later(g):
                            act.wait_ge(silu_done.sem, silu_done.at(g - 1, PAIRS - 2 + j))
                    for a in range(2):
                        t = 2 * j + a
                        last = nc.scalar.activation(acc[:, r, a], ps[:, a * TOK:(a + 1) * TOK], ACT.Identity,
                                                    scale=cw[:, t, TAPS - 1:TAPS], bias=cb[:, t:t + 1])
                    last.then_inc(pair_read.sem, 1)
                    if j >= 1:
                        silu(j - 1)
                silu(PAIRS - 1)

            def mixer_exp(g):
                act.wait_ge(cum_sb.sem, cum_sb.at(g))
                nc.scalar.activation(ecum[:], cum[:], ACT.Exp).then_inc(ecum_done.sem, 1)

            def mixer_decay(g, c):
                for q in range(2):
                    act.wait_ge(rows_ps.sem, rows_ps.at(g, 2 * c + q))
                    k = 2 * c + q
                    if k >= 2 or later(g):
                        act.wait_ge(sL_done.sem, sL_done.at(g, k - 2))
                    for i in range(4):
                        h = 4 * q + i
                        last = nc.scalar.activation(Ldec[:, h, :], pairb[q][:, i * P:(i + 1) * P], ACT.Exp,
                                                    bias=ncum[:, c, h:h + 1])
                    last.then_inc(decay_done.sem, 1)

            def mixer_move(g, c):
                act.wait_ge(X_ps.sem, X_ps.at(g, c))
                if c or later(g):
                    act.wait_ge(Xw_done.sem, Xw_done.at(g, c - 1))
                if c or later(g):
                    act.wait_ge(DX_done.sem, DX_done.at(g, c - 1))
                nc.scalar.activation(Xt[:], ring[1][:], ACT.Copy).then_inc(X_sb.sem, 1)
                for q in range(2):
                    act.wait_ge(Bt_ps.sem, Bt_ps.at(g, 2 * c + q))
                    if c or later(g):
                        act.wait_ge(S_ps.sem, S_ps.at(g, c - 1))
                    nc.scalar.activation(Btok[:, 4 * q:4 * q + 4, :],
                                         pairb[q][:].rearrange("p (h t) -> p h t", h=4), ACT.Copy)\
                        .then_inc(Bt_sb.sem, 1)

            def mixer_z(g, c):
                act.wait_ge(z_ps.sem, z_ps.at(g, c))
                if c or later(g):
                    act.wait_ge(y_done.sem, y_done.at(g, c - 1))
                nc.scalar.activation(zs[:], ring[0][:], ACT.Silu).then_inc(z_done.sem, 1)

            def mixer_square(g, c):
                act.wait_ge(y_done.sem, y_done.at(g, c))
                if c == 0:
                    if later(g):
                        act.wait_ge(rooty.sem, rooty.at(g - 1))
                if c or later(g):
                    act.wait_ge(sq_done.sem, sq_done.at(g, c - 1))
                nc.scalar.activation(ysq[:], yv[:, c], ACT.Square, accum_out=ssq[:, c:c + 1]).then_inc(sq_done.sem, 1)

            def mixer_yT(g, c):
                act.wait_ge(yT_ps.sem, yT_ps.at(g, c))
                if later(g):
                    act.wait_ge(out_ps.sem, out_ps.at(g - 1))
                nc.scalar.activation(yT[:, c, :], ring[1 - c][:], ACT.Copy).then_inc(yT_sb.sem, 1)

            def mixer_h2T(g):
                act.wait_ge(h2T_ps.sem, h2T_ps.at(g))
                nc.scalar.activation(h2T[:], ring[0][:].rearrange("p (k t) -> p k t", k=DK), ACT.Copy)\
                    .then_inc(h2T_sb.sem, 1)

            def ffn_sim(e, c):
                act.wait_ge(sim_ps.sem, sim_ps.at(e, c))
                if c or later(e):
                    act.wait_ge(earg_done.sem, earg_done.at(e, c - 1))
                nc.scalar.activation(sim[:].rearrange("p a h k -> p (a h k)"), f0[:], ACT.Copy)\
                    .then_inc(sim_sb.sem, 1)

            def ffn_up(e):
                for j in range(FT // 2):
                    act.wait_ge(up_ps.sem, up_ps.at(e, j))
                    if later(e):
                        act.wait_ge(f_ps.sem, f_ps.at(e - 1, CH - 1))
                    nc.scalar.activation(hid[:, 2 * j:2 * j + 2, :], f0[:].rearrange("p (a t) -> p a t", a=2), ACT.Silu)\
                        .then_inc(up_done.sem, 1)

            def ffn_exp(e, c):
                act.wait_ge(earg_done.sem, earg_done.at(e, c))
                nc.scalar.activation(ee[:], earg[:], ACT.Exp).then_inc(ee_done.sem, 1)

            def ffn_experts(e, c):
                act.wait_ge(clz_done.sem, clz_done.at(e, c))
                nc.scalar.activation(cls[:], clz[:], ACT.Silu, accum_out=clsum[:, 0:1]).then_inc(cls_done.sem, 1)
                for h in range(RH):
                    act.wait_ge(Z_done.sem, Z_done.at(e, c * RH + h))
                    nc.scalar.activation(Z[:, h % 2, :], Z[:, h % 2, :], ACT.Silu, scale=rden[:, h:h + 1])\
                        .then_inc(Zs_done.sem, 1)

            def ffn_WT(e, c):
                for q in range(2):
                    act.wait_ge(WT_ps.sem, WT_ps.at(e, 2 * c + q))
                    if c or later(e):
                        act.wait_ge(f_ps.sem, f_ps.at(e, c - 1))
                    nc.scalar.activation(WT[:, 4 * q:4 * q + 4, :],
                                         fA[q][:].rearrange("p (h t) -> p h t", h=4), ACT.Copy)\
                        .then_inc(WT_sb.sem, 1)

            def do_group(g, e):
                a, b = g is not None, e is not None
                if b:
                    ffn_sim(e, 0)
                if a:
                    mixer_hT(g)
                if b:
                    ffn_exp(e, 0)
                if a:
                    mixer_dt(g)
                if b:
                    ffn_up(e)
                if a:
                    mixer_pairs(g)
                if b:
                    ffn_sim(e, 1)
                    ffn_experts(e, 0)
                if a:
                    mixer_exp(g)
                    mixer_decay(g, 0)
                    mixer_move(g, 0)
                    mixer_z(g, 0)
                if b:
                    ffn_WT(e, 0)
                    ffn_exp(e, 1)
                if a:
                    mixer_decay(g, 1)
                    mixer_square(g, 0)
                    mixer_move(g, 1)
                    mixer_z(g, 1)
                if b:
                    ffn_experts(e, 1)
                if a:
                    mixer_yT(g, 0)
                if b:
                    ffn_WT(e, 1)
                if a:
                    mixer_square(g, 1)
                    mixer_yT(g, 1)
                    mixer_h2T(g)

            do_group(0, None)
            do_group(1, 0)
            with act.Fori(2, NG) as g:
                do_group(g, g - 1)
            do_group(None, NG - 1)

        @block.vector
        def _(dve):
            own = Steps()
            V = nc.vector
            dve.wait_ge(loaded_c, 16 * 9)
            dve.wait_ge(loaded_w, 16 * 6)
            for k in range(DK):
                last = V.tensor_scalar(w_in[:, k, :], w_in[:, k, :], nw[:, k:k + 1], None, ALU.mult)
                last.then_inc(own_dve, own.one())
            for k in range(INNER // P):
                V.tensor_scalar(w_out[:, k, :], w_out[:, k, :], gw[:, k:k + 1], None, ALU.mult).then_inc(own_dve, own.one())
            dve.wait_ge(own_dve, own.n)
            dve.sem_inc(folded, 1)
            dve.wait_ge(consts, 1)

            dve.wait_ge(own_dve, own.n)
            dve.sem_clear(own_dve)
            own.restart()

            def heads3(ap):
                return ap.rearrange("p (h d) -> p h d", h=HEADS)

            def mixer_norm(g):
                dve.wait_ge(x_loaded, 16 * (g + 1))
                for c in range(CH):
                    V.bn_stats(lnst[:, c, :], x_in[:, c, :]).then_inc(own_dve, own.one())
                dve.wait_ge(own_dve, own.n)
                for c in range(CH):
                    last = V.bn_aggr(mv1[:, c, :], lnst[:, c, :])
                last.then_inc(stats1.sem, 1)
                if later(g):
                    dve.wait_ge(halo_in.sem, halo_in.at(g - 1, PAIRS - 1))
                V.tensor_copy(keep[:].unsqueeze(2), keep_tab[:, :, bass.ds(g, 1)]).then_inc(own_dve, own.one())
                dve.wait_ge(root1.sem, root1.at(g))
                dve.wait_ge(own_dve, own.n)
                for c in range(CH):
                    last = V.tensor_scalar(u[:, c, :], x_in[:, c, :], mv1[:, c, 0:1], rs1[:, c:c + 1],
                                           ALU.subtract, ALU.mult)
                    if c == CH - 1:
                        last.then_inc(x_read.sem, 1)
                    else:
                        last.then_inc(own_dve, own.one())
                dve.wait_ge(x_read.sem, x_read.at(g))
                dve.wait_ge(own_dve, own.n)
                for c in range(CH):
                    if c == CH - 1:
                        V.tensor_scalar(hn[:, c, :], u[:, c, :], rs2[:, c:c + 1], None, ALU.mult)\
                            .then_inc(hn_done.sem, 1)
                    else:
                        V.tensor_scalar(hn[:, c, :], u[:, c, :], rs2[:, c:c + 1], None, ALU.mult).then_inc(own_dve, own.one())

            def mixer_dt_raw(g):
                dve.wait_ge(dt_ps.sem, dt_ps.at(g))
                V.tensor_tensor(dt0[:], ring[1][:, 0:CH * HEADS].rearrange("p (c h) -> p c h", c=CH),
                                       bc(head_c[:, 0, :], 1, CH), ALU.add).then_inc(own_dve, own.one())
                dve.wait_ge(own_dve, own.n)
                V.tensor_scalar(dt2[:], dt0[:], -1.0, None, ALU.mult).then_inc(own_dve, own.one())
                dve.wait_ge(own_dve, own.n)
                V.tensor_tensor(dt1[:], dt0[:], dt2[:], ALU.max).then_inc(dt_read.sem, 1)

            def mixer_dt(g):
                dve.wait_ge(dte_done.sem, dte_done.at(g))
                V.tensor_scalar(dt1[:], dte[:], 2.0, None, ALU.add).then_inc(own_dve, own.one())
                dve.wait_ge(own_dve, own.n)
                V.reciprocal(dt2[:], dt1[:]).then_inc(own_dve, own.one())
                dve.wait_ge(own_dve, own.n)
                V.tensor_tensor(dt1[:], dt2[:], dte[:], ALU.mult).then_inc(own_dve, own.one())
                dve.wait_ge(own_dve, own.n)
                V.tensor_tensor(dt2[:], dt1[:], dt1[:], ALU.mult).then_inc(own_dve, own.one())
                dve.wait_ge(own_dve, own.n)
                V.tensor_scalar(dts[:], dt2[:], 1.0 / 19, 1.0 / 17, ALU.mult, ALU.add).then_inc(own_dve, own.one())
                for n in (15, 13, 11, 9, 7, 5, 3, 1):
                    dve.wait_ge(own_dve, own.n)
                    V.tensor_tensor(dts[:], dts[:], dt2[:], ALU.mult).then_inc(own_dve, own.one())
                    dve.wait_ge(own_dve, own.n)
                    V.tensor_scalar(dts[:], dts[:], 1.0 / n, None, ALU.add).then_inc(own_dve, own.one())
                dve.wait_ge(own_dve, own.n)
                V.tensor_tensor(dts[:], dts[:], dt1[:], ALU.mult).then_inc(own_dve, own.one())
                V.tensor_scalar(dt2[:], dt0[:], 0.0, None, ALU.max).then_inc(own_dve, own.one())
                dve.wait_ge(own_dve, own.n)
                V.scalar_tensor_tensor(dts[:], dts[:], 2.0, dt2[:], ALU.mult, ALU.add).then_inc(own_dve, own.one())
                dve.wait_ge(own_dve, own.n)
                V.scalar_tensor_tensor(da[:], dts[:], -1.0, bc(neg_a[:], 1, CH), ALU.mult, ALU.mult)\
                    .then_inc(da_done.sem, 1)

            def mixer_cum(g):
                dve.wait_ge(cum_ps.sem, cum_ps.at(g))
                ps = ring[0][:, 0:2 * CH * HEADS].rearrange("p (a c h) -> p a c h", a=2, c=CH)
                V.tensor_copy(cum[:, 0], ps[:, 0]).then_inc(own_dve, own.one())
                V.tensor_scalar(ncum[:], ps[:, 0], -1.0, None, ALU.mult).then_inc(own_dve, own.one())
                V.tensor_copy(cum[:, 2], ps[:, 1]).then_inc(cum_read.sem, 1)
                dve.wait_ge(own_dve, own.n)
                dve.wait_ge(cum_read.sem, cum_read.at(g))
                V.tensor_tensor(cum[:, 1], cum[:, 2], cum[:, 0], ALU.subtract).then_inc(cum_sb.sem, 1)
                if later(g):
                    dve.wait_ge(H_done.sem, H_done.at(g - 1, CH - 1))
                if later(g):
                    dve.wait_ge(Yi_ps.sem, Yi_ps.at(g - 1, CH - 1))
                V.tensor_scalar(H[:], H[:], keep[:, 0:1], keep[:, 1:2], ALU.min, ALU.max).then_inc(H_kept.sem, 1)

            def mixer_conv(g):
                for j in range(PAIRS):
                    r = j % 2
                    dve.wait_ge(pair_read.sem, pair_read.at(g, j))
                    dve.wait_ge(halo_in.sem, halo_in.at(g, j))
                    dve.wait_ge(pair_copied.sem, pair_copied.at(g, j))
                    before = [None, None]
                    for k in range(TAPS - 1):
                        for a in range(2):
                            t = 2 * j + a
                            if before[a] is not None:
                                dve.wait_ge(own_dve, before[a])
                            ins = V.scalar_tensor_tensor(acc[:, r, a], xp[:, r, a, k:k + TOK], cw[:, t, k:k + 1],
                                                         acc[:, r, a], ALU.mult, ALU.add)
                            if k == TAPS - 2 and a == 1:
                                ins.then_inc(conv_done.sem, 1)
                            else:
                                ins.then_inc(own_dve, own.one())
                                before[a] = own.n
                    dve.wait_ge(own_dve, own.n)

            def mixer_chunk_a(g, c):
                dve.wait_ge(X_sb.sem, X_sb.at(g, c))
                if c or later(g):
                    dve.wait_ge(Yn_ps.sem, Yn_ps.at(g, c - 1))
                V.tensor_tensor(heads3(Xdt[:]), heads3(Xt[:]), bc(dts[:, c, :], 2, HD), ALU.mult).then_inc(own_dve, own.one())
                dve.wait_ge(own_dve, own.n)
                dve.wait_ge(ecum_done.sem, ecum_done.at(g))
                if c or later(g):
                    dve.wait_ge(S_ps.sem, S_ps.at(g, c - 1))
                V.tensor_tensor(heads3(Xw[:]), heads3(Xdt[:]), bc(ecum[:, 1, c, :], 2, HD), ALU.mult)\
                    .then_inc(Xw_done.sem, 1)
                for q in range(2):
                    dve.wait_ge(sc_ps.sem, sc_ps.at(g, 2 * c + q))
                    dve.wait_ge(decay_done.sem, decay_done.at(g, 2 * c + q))
                    V.tensor_tensor(sL[:, 4 * q:4 * q + 4, :], pairb[q][:].rearrange("p (h t) -> p h t", h=4),
                                    Ldec[:, 4 * q:4 * q + 4, :], ALU.mult).then_inc(sL_done.sem, 1)
                dve.wait_ge(Yi_ps.sem, Yi_ps.at(g, c))
                if later(g):
                    dve.wait_ge(yT_ps.sem, yT_ps.at(g - 1, c))
                if later(g):
                    dve.wait_ge(sq_done.sem, sq_done.at(g - 1, c))
                V.tensor_tensor(heads3(yv[:, c]), heads3(ring[1][:]), bc(ecum[:, 0, c, :], 2, HD), ALU.mult)\
                    .then_inc(Yi_read.sem, 1)
                dve.wait_ge(Yi_read.sem, Yi_read.at(g, c))
                V.tensor_tensor(heads3(H[:]), heads3(H[:]), bc(ecum[:, 2, c, :], 2, HD), ALU.mult).then_inc(own_dve, own.one())
                dve.wait_ge(own_dve, own.n)
                dve.wait_ge(S_ps.sem, S_ps.at(g, c))
                V.tensor_tensor(H[:], H[:], ring[0][:], ALU.add).then_inc(H_done.sem, 1)

            def mixer_chunk_b(g, c):
                dve.wait_ge(DX_done.sem, DX_done.at(g, c))
                V.tensor_tensor(yv[:, c], yv[:, c], DX[:], ALU.add).then_inc(own_dve, own.one())
                dve.wait_ge(own_dve, own.n)
                dve.wait_ge(Yn_ps.sem, Yn_ps.at(g, c))
                V.tensor_tensor(yv[:, c], yv[:, c], yb[:], ALU.add).then_inc(Yn_read.sem, 1)
                dve.wait_ge(Yn_read.sem, Yn_read.at(g, c))
                dve.wait_ge(z_done.sem, z_done.at(g, c))
                V.tensor_tensor(yv[:, c], yv[:, c], zs[:], ALU.mult).then_inc(y_done.sem, 1)

            def mixer_tail(g):
                dve.wait_ge(rooty.sem, rooty.at(g))
                dve.wait_ge(out_ps.sem, out_ps.at(g))
                for c in range(CH):
                    ins = V.scalar_tensor_tensor(v[:, c, :], ring[1][:, c * D:(c + 1) * D], rsy[:, c:c + 1],
                                                 u[:, c, :], ALU.mult, ALU.add)
                    if c < CH - 1:
                        ins.then_inc(own_dve, own.one())
                    else:
                        ins.then_inc(out_read.sem, 1)
                dve.wait_ge(own_dve, own.n)
                dve.wait_ge(out_read.sem, out_read.at(g))
                for c in range(CH):
                    V.bn_stats(lnst[:, c, :], v[:, c, :]).then_inc(own_dve, own.one())
                dve.wait_ge(own_dve, own.n)
                for c in range(CH):
                    ins = V.bn_aggr(mv2[:, c, :], lnst[:, c, :])
                ins.then_inc(stats3.sem, 1)
                dve.wait_ge(root3.sem, root3.at(g))
                for c in range(CH):
                    V.tensor_scalar(v[:, c, :], v[:, c, :], mv2[:, c, 0:1], rs3[:, c:c + 1],
                                           ALU.subtract, ALU.mult).then_inc(own_dve, own.one())
                dve.wait_ge(own_dve, own.n)
                dve.wait_ge(xres_loaded, 16 * (g + 1))
                V.tensor_tensor(x1[:], v[:], x_res[:], ALU.add).then_inc(xres_read.sem, 1)
                dve.wait_ge(xres_read.sem, xres_read.at(g))
                for c in range(CH):
                    V.bn_stats(lnst[:, c, :], x1[:, c, :]).then_inc(own_dve, own.one())
                dve.wait_ge(own_dve, own.n)
                for c in range(CH):
                    ins = V.bn_aggr(mv3[:, c, :], lnst[:, c, :])
                ins.then_inc(stats4.sem, 1)
                dve.wait_ge(root4.sem, root4.at(g))
                for c in range(CH):
                    ins = V.tensor_scalar(h2[:, c, :], x1[:, c, :], mv3[:, c, 0:1], rs4[:, c:c + 1],
                                          ALU.subtract, ALU.mult)
                    if c < CH - 1:
                        ins.then_inc(own_dve, own.one())
                    else:
                        ins.then_inc(h2_done.sem, 1)

            def ffn_route(e, c):
                dve.wait_ge(sim_sb.sem, sim_sb.at(e, c))
                dve.sem_inc(arrived_dve, 1)
                for s in range(2):
                    for h in range(RH):
                        V.max(s8[:, s, h, :], sim[:, s, h, :]).then_inc(own_dve, own.one())
                dve.wait_ge(own_dve, own.n)
                for s in range(2):
                    for h in range(RH):
                        V.max_index(i8[:, s, h, :], s8[:, s, h, :], sim[:, s, h, :]).then_inc(own_dve, own.one())
                at = 0
                for first, rows, n in CAND:
                    sx = s8[:, 0, :, first:first + rows]
                    sy = s8[:, 1, :, 0:n]
                    V.tensor_tensor(cand[:, :, at:at + rows * n].rearrange("p h (r n) -> p h r n", n=n),
                                           bc(sx, 3, n), bc(sy, 2, rows), ALU.add).then_inc(own_dve, own.one())
                    at += rows * n
                dve.wait_ge(own_dve, own.n)
                V.tensor_copy(i8b[:], i8[:]).then_inc(own_dve, own.one())
                for h in range(RH):
                    V.max(c8[:, h, :], cand[:, h, :]).then_inc(own_dve, own.one())
                dve.wait_ge(own_dve, own.n)
                for h in range(RH):
                    V.match_replace(rest[:, h, :], c8[:, h, :], cand[:, h, :], LOWEST).then_inc(own_dve, own.one())
                V.tensor_tensor(earg[:, :, 0:XD], sim[:, 0, :, 0:XD], bc(s8[:, 0, :, 0], 2, XD), ALU.subtract).then_inc(own_dve, own.one())
                V.tensor_tensor(earg[:, :, XD:XD + KEYS], sim[:, 1], bc(s8[:, 1, :, 0], 2, KEYS), ALU.subtract).then_inc(own_dve, own.one())
                V.tensor_tensor(earg[:, :, XD + KEYS:], cand[:], bc(c8[:, :, 0], 2, NC), ALU.subtract)\
                    .then_inc(earg_done.sem, 1)
                dve.wait_ge(own_dve, own.n)
                V.tensor_tensor(chosen[:], rest[:], cand[:], ALU.not_equal).then_inc(own_dve, own.one())
                dve.wait_ge(own_dve, own.n)
                at = 0
                for first, rows, n in CAND:
                    part = chosen[:, :, at:at + rows * n].rearrange("p h (r n) -> p h r n", n=n)
                    V.tensor_reduce(n8[:, :, first:first + rows], part, AX_X, ALU.add).then_inc(own_dve, own.one())
                    at += rows * n
                dve.wait_ge(own_dve, own.n)
                V.tensor_tensor(eqx[:], bc(i8b[:, 0], 2, XD), bc(iota[:, 0:XD, :], 1, RH), ALU.is_equal).then_inc(own_dve, own.one())
                dve.wait_ge(own_dve, own.n)
                V.tensor_tensor(eqx[:], eqx[:], bc(n8[:], 2, XD), ALU.mult).then_inc(own_dve, own.one())
                dve.wait_ge(own_dve, own.n)
                V.tensor_reduce(nx[:], eqx[:], AX_X, ALU.add).then_inc(own_dve, own.one())
                dve.wait_ge(own_dve, own.n)
                V.tensor_scalar(nx[:], nx[:], -float(TOP), None, ALU.add).then_inc(own_dve, own.one())
                for h in range(RH):
                    V.tensor_tensor(eqy[:], bc(i8b[:, 1, h, :], 1, KEYS), iota[:], ALU.is_equal).then_inc(own_dve, own.one())
                    dve.wait_ge(own_dve, own.n)
                    V.tensor_tensor(eqy[:], eqy[:], bc(rank_w[:], 1, KEYS), ALU.mult).then_inc(own_dve, own.one())
                    dve.wait_ge(own_dve, own.n)
                    ins = V.tensor_reduce(ry[:, h, :], eqy[:], AX_X, ALU.add)
                    if h < RH - 1:
                        ins.then_inc(own_dve, own.one())
                        dve.wait_ge(own_dve, own.n)
                    else:
                        ins.then_inc(dense_in.sem, 1)
                dve.wait_ge(ee_done.sem, ee_done.at(e, c))
                V.tensor_tensor(psel[:], chosen[:], ee[:, :, XD + KEYS:], ALU.mult).then_inc(own_dve, own.one())
                V.tensor_scalar(cmask[:], i8b[:, 0], float(XD), None, ALU.is_ge).then_inc(own_dve, own.one())
                dve.wait_ge(own_dve, own.n)
                V.tensor_reduce(psum8[:], psel[:], AX_X, ALU.add).then_inc(own_dve, own.one())
                dve.wait_ge(own_dve, own.n)
                if c or later(e):
                    dve.wait_ge(Zs_done.sem, Zs_done.at(e, (c - 1) * RH + RH - 1))
                V.reciprocal(rden[:], psum8[:]).then_inc(own_dve, own.one())
                at = 0
                for first, rows, n in CAND:
                    V.tensor_tensor(clz[:, :, at:at + rows * n].rearrange("p h (r n) -> p h r n", n=n),
                                           psel[:, :, at:at + rows * n].rearrange("p h (r n) -> p h r n", n=n),
                                           bc(cmask[:, :, first:first + rows], 3, n), ALU.mult).then_inc(own_dve, own.one())
                    at += rows * n
                dve.wait_ge(own_dve, own.n)

            def ffn_experts(e, c):
                dve.wait_ge(A_ps.sem, A_ps.at(e, c))
                V.tensor_copy(psum8[:, 0:1], fA[1][:, 511:512]).then_inc(own_dve, own.one())
                dve.wait_ge(own_dve, own.n)
                V.scalar_tensor_tensor(clz[:], clz[:], psum8[:, 0:1], bc(rden[:], 2, NC), ALU.mult, ALU.mult)\
                    .then_inc(clz_done.sem, 1)

                def collect(h):
                    dve.wait_ge(Zs_done.sem, Zs_done.at(e, c * RH + h))
                    if h == 0:
                        if c or later(e):
                            dve.wait_ge(WT_ps.sem, WT_ps.at(e, 2 * (c - 1) + 1))
                        V.tensor_copy(W[:], Z[:, 0, :]).then_inc(own_dve, own.one())
                    else:
                        V.tensor_tensor(W[:], W[:], Z[:, h % 2, :], ALU.add).then_inc(own_dve, own.one())
                    dve.wait_ge(own_dve, own.n)

                for h in range(RH):
                    r = h % 2
                    V.tensor_tensor(Em[:, r], bc(ee[:, h, 0:XD], 2, KEYS),
                                           bc(ee[:, h, XD:XD + KEYS], 1, XD), ALU.mult).then_inc(own_dve, own.one())
                    dve.wait_ge(own_dve, own.n)
                    dve.wait_ge(D_done.sem, D_done.at(e, c * RH + h))
                    V.scalar_tensor_tensor(Em[:, r].rearrange("p a b -> p (a b)"),
                                           Dm[:, h].rearrange("p a b -> p (a b)"), 0.0,
                                           Em[:, r].rearrange("p a b -> p (a b)"), ALU.is_gt, ALU.mult)\
                        .then_inc(P_done.sem, 1)
                    if h >= 2:
                        collect(h - 2)
                    dve.wait_ge(P_done.sem, P_done.at(e, c * RH + h))
                    Eh = Em[:, r].rearrange("p a b -> p (a b)")
                    V.tensor_tensor(Z[:, r, 0:512], Eh[:, 0:512], fA[0][:], ALU.mult).then_inc(own_dve, own.one())
                    V.tensor_tensor(Z[:, r, 512:], Eh[:, 512:], fA[1][:], ALU.mult).then_inc(Z_done.sem, 1)
                    dve.wait_ge(own_dve, own.n)
                collect(RH - 2)
                collect(RH - 1)
                dve.wait_ge(cls_done.sem, cls_done.at(e, c))
                V.tensor_tensor(W[:, EXPERTS - 1:], W[:, EXPERTS - 1:], clsum[:], ALU.add).then_inc(W_done.sem, 1)

            def ffn_out(e, c):
                dve.wait_ge(f_ps.sem, f_ps.at(e, c))
                if c == 0:
                    if not (isinstance(e, int) and e == 0):
                        dve.wait_ge(stored, 16 * e)
                V.tensor_copy(f[:, c, :], f0[:, 0:D]).then_inc(f_sb.sem, 1)

            def ffn_tail(e):
                dve.wait_ge(f_sb.sem, f_sb.at(e, CH - 1))
                for c in range(CH):
                    V.bn_stats(fst[:, c, :], f[:, c, :]).then_inc(own_dve, own.one())
                dve.wait_ge(own_dve, own.n)
                for c in range(CH):
                    ins = V.bn_aggr(mvf[:, c, :], fst[:, c, :])
                ins.then_inc(statsf.sem, 1)
                dve.wait_ge(rootf.sem, rootf.at(e))
                for c in range(CH):
                    V.tensor_scalar(f[:, c, :], f[:, c, :], mvf[:, c, 0:1], rsf[:, c:c + 1],
                                           ALU.subtract, ALU.mult).then_inc(own_dve, own.one())
                dve.wait_ge(own_dve, own.n)
                V.tensor_tensor(f[:], f[:], x1[:], ALU.add).then_inc(o_done.sem, 1)

            def do_group(g, e):
                a, b = g is not None, e is not None
                if a:
                    mixer_norm(g)
                if b:
                    ffn_route(e, 0)
                if a:
                    mixer_dt_raw(g)
                    mixer_dt(g)
                    mixer_conv(g)
                    mixer_cum(g)
                if b:
                    ffn_experts(e, 0)
                if a:
                    mixer_chunk_a(g, 0)
                if b:
                    ffn_route(e, 1)
                if a:
                    mixer_chunk_b(g, 0)
                    mixer_chunk_a(g, 1)
                if b:
                    ffn_out(e, 0)
                    ffn_experts(e, 1)
                if a:
                    mixer_chunk_b(g, 1)
                if b:
                    ffn_out(e, 1)
                    ffn_tail(e)
                if a:
                    if b:
                        dve.wait_ge(o_done.sem, o_done.at(e))
                    mixer_tail(g)
                dve.wait_ge(own_dve, own.n)
                dve.sem_clear(own_dve)
                own.restart()

            do_group(0, None)
            do_group(1, 0)
            with dve.Fori(2, NG) as g:
                do_group(g, g - 1)
            do_group(None, NG - 1)

        @block.tensor
        def _(pe):
            mm = nc.tensor.matmul
            pe.wait_ge(consts, 1)
            pe.wait_ge(loaded_c, 16 * 9)
            for k in range(DK):
                for s in range(2 * RH):
                    last = mm(ring[k][:, s * KEYS:(s + 1) * KEYS], hid[0:64, s, k * P:(k + 1) * P],
                              xbcT[0:64, 0:2, :].rearrange("p a (b k) -> p (a b) k", k=KEYS)[:, s, :],
                              start=True, stop=True)
                last.then_inc(simw_ps, 1)
            pe.wait_ge(simw_sb, 1)
            pe.wait_ge(folded, 1)
            pe.wait_ge(loaded_w, 16 * 6)

            def mixer_hT(g):
                pe.wait_ge(hn_done.sem, hn_done.at(g))
                if later(g):
                    pe.wait_ge(h2T_sb.sem, h2T_sb.at(g - 1))
                for c in range(CH):
                    for k in range(DK):
                        last = nc.tensor.transpose(ring[0][:, k * TOK + c * P:k * TOK + (c + 1) * P],
                                                   hn[:, c, k * P:(k + 1) * P], ident[:])
                last.then_inc(hT_ps.sem, 1)

            def mixer_dt(g):
                pe.wait_ge(hT_sb.sem, hT_sb.at(g))
                if later(g):
                    pe.wait_ge(out_read.sem, out_read.at(g - 1))
                for c in range(CH):
                    for k in range(DK):
                        last = mm(ring[1][:, c * HEADS:(c + 1) * HEADS], hT[:, k, c * P:(c + 1) * P],
                                  w_in[:, k, INNER + XBC:], start=k == 0, stop=k == DK - 1)
                last.then_inc(dt_ps.sem, 1)

            def mixer_pair(g, j):
                if j == 0:
                    pe.wait_ge(hT_sb.sem, hT_sb.at(g))
                elif j == 1:
                    pe.wait_ge(dt_read.sem, dt_read.at(g))
                else:
                    pe.wait_ge(pair_read.sem, pair_read.at(g, j - 2))
                ps = ring[j % 2]
                for a in range(2):
                    at = INNER + (2 * j + a) * P
                    for k in range(DK):
                        last = mm(ps[:, a * TOK:(a + 1) * TOK], w_in[:, k, at:at + P], hT[:, k, :],
                                  start=k == 0, stop=k == DK - 1)
                last.then_inc(pair_ps.sem, 1)

            def mixer_cum(g):
                pe.wait_ge(da_done.sem, da_done.at(g))
                pe.wait_ge(pair_read.sem, pair_read.at(g, PAIRS - 2))
                ps = ring[0]
                n = CH * HEADS
                mm(ps[:, 0:n], tri[:], da[:].rearrange("p c h -> p (c h)"), start=True, stop=True)
                mm(ps[:, n:2 * n], ones[:], da[:].rearrange("p c h -> p (c h)"), start=True, stop=True)\
                    .then_inc(cum_ps.sem, 1)

            def mixer_rows(g, c):
                for q in range(2):
                    if c or later(g):
                        pe.wait_ge(sL_done.sem, sL_done.at(g, 2 * (c - 1) + q))
                    mm(pairb[q][:], ident_b[:], mask_b[:].rearrange("p h t -> p (h t)"), start=True, stop=False)
                    for i in range(4):
                        h = 4 * q + i
                        last = mm(pairb[q][:, i * P:(i + 1) * P], da[:, c, h:h + 1].to_broadcast([P, P]), tri[:],
                                  start=False, stop=i == 3)
                    last.then_inc(rows_ps.sem, 1)

            def mixer_X(g, c):
                pe.wait_ge(silu_done.sem, silu_done.at(g, XP - 1))
                if c == 0:
                    pe.wait_ge(pair_read.sem, pair_read.at(g, PAIRS - 1))
                else:
                    pe.wait_ge(Yi_read.sem, Yi_read.at(g, c - 1))
                for i in range(INNER // P):
                    last = nc.tensor.transpose(ring[1][:, i * P:(i + 1) * P],
                                               xbcT[:, i, c * P:(c + 1) * P], ident[:])
                last.then_inc(X_ps.sem, 1)

            def mixer_z(g, c):
                if c == 0:
                    pe.wait_ge(cum_read.sem, cum_read.at(g))
                else:
                    pe.wait_ge(H_done.sem, H_done.at(g, c - 1))
                for k in range(DK):
                    last = mm(ring[0][:], hT[:, k, c * P:(c + 1) * P], w_in[:, k, 0:INNER],
                              start=k == 0, stop=k == DK - 1)
                last.then_inc(z_ps.sem, 1)

            def mixer_B(g, c):
                pe.wait_ge(silu_done.sem, silu_done.at(g, XP + BP - 1))
                for q in range(2):
                    pe.wait_ge(decay_done.sem, decay_done.at(g, 2 * c + q))
                    for i in range(4):
                        last = nc.tensor.transpose(pairb[q][:, i * P:(i + 1) * P],
                                                   xbcT[:, INNER // P + 4 * q + i, c * P:(c + 1) * P], ident[:])
                    last.then_inc(Bt_ps.sem, 1)

            def mixer_Yi(g, c):
                pe.wait_ge(silu_done.sem, silu_done.at(g, PAIRS - 1))
                if c == 0:
                    pe.wait_ge(H_kept.sem, H_kept.at(g))
                else:
                    pe.wait_ge(H_done.sem, H_done.at(g, c - 1))
                pe.wait_ge(X_sb.sem, X_sb.at(g, c))
                for h in range(HEADS):
                    last = mm(ring[1][:, h * HD:(h + 1) * HD],
                              xbcT[:, INNER // P + HEADS + h, c * P:(c + 1) * P], H[:, h * HD:(h + 1) * HD],
                              start=True, stop=True)
                last.then_inc(Yi_ps.sem, 1)

            def mixer_scores(g, c):
                for q in range(2):
                    pe.wait_ge(Bt_sb.sem, Bt_sb.at(g, 2 * c + q))
                    for i in range(4):
                        h = 4 * q + i
                        last = mm(pairb[q][:, i * P:(i + 1) * P], xbcT[:, INNER // P + h, c * P:(c + 1) * P],
                                  xbcT[:, INNER // P + HEADS + h, c * P:(c + 1) * P], start=True, stop=True)
                    last.then_inc(sc_ps.sem, 1)

            def mixer_S(g, c):
                pe.wait_ge(Xw_done.sem, Xw_done.at(g, c))
                pe.wait_ge(z_done.sem, z_done.at(g, c))
                for h in range(HEADS):
                    last = mm(ring[0][:, h * HD:(h + 1) * HD], Btok[:, h, :], Xw[:, h * HD:(h + 1) * HD],
                              start=True, stop=True)
                last.then_inc(S_ps.sem, 1)

            def mixer_Yn(g, c):
                if c or later(g):
                    pe.wait_ge(Yn_read.sem, Yn_read.at(g, c - 1))
                pe.wait_ge(sL_done.sem, sL_done.at(g, 2 * c + 1))
                for h in range(HEADS):
                    last = mm(yb[:, h * HD:(h + 1) * HD], sL[:, h, :], Xdt[:, h * HD:(h + 1) * HD],
                              start=True, stop=True)
                last.then_inc(Yn_ps.sem, 1)

            def mixer_yT(g, c):
                pe.wait_ge(y_done.sem, y_done.at(g, c))
                if c == 0:
                    pe.wait_ge(Yi_read.sem, Yi_read.at(g, CH - 1))
                else:
                    pe.wait_ge(H_done.sem, H_done.at(g, CH - 1))
                for i in range(INNER // P):
                    last = nc.tensor.transpose(ring[1 - c][:, i * P:(i + 1) * P], yv[:, c, i * P:(i + 1) * P],
                                               ident[:])
                last.then_inc(yT_ps.sem, 1)

            def mixer_out(g):
                pe.wait_ge(yT_sb.sem, yT_sb.at(g, 0))
                pe.wait_ge(yT_sb.sem, yT_sb.at(g, CH - 1))
                for c in range(CH):
                    for i in range(INNER // P):
                        last = mm(ring[1][:, c * D:(c + 1) * D], yT[:, c, i * P:(i + 1) * P], w_out[:, i, :],
                                  start=i == 0, stop=i == INNER // P - 1)
                last.then_inc(out_ps.sem, 1)

            def mixer_h2T(g):
                pe.wait_ge(h2_done.sem, h2_done.at(g))
                pe.wait_ge(yT_sb.sem, yT_sb.at(g, 1))
                for c in range(CH):
                    for k in range(DK):
                        last = nc.tensor.transpose(ring[0][:, k * TOK + c * P:k * TOK + (c + 1) * P],
                                                   h2[:, c, k * P:(k + 1) * P], ident[:])
                last.then_inc(h2T_ps.sem, 1)

            def ffn_sim(e, c):
                pe.wait_ge(h2T_sb.sem, h2T_sb.at(e))
                if c == 0:
                    if later(e):
                        pe.wait_ge(f_sb.sem, f_sb.at(e - 1, CH - 1))
                else:
                    pe.wait_ge(up_done.sem, up_done.at(e, FT // 2 - 1))
                for k in range(DK):
                    last = mm(f0[:], h2T[:, k, c * P:(c + 1) * P], w_sim[:, k, :], start=k == 0, stop=k == DK - 1)
                last.then_inc(sim_ps.sem, 1)

            def ffn_A(e, c):
                for q in range(2):
                    if c or later(e):
                        pe.wait_ge(WT_sb.sem, WT_sb.at(e, 2 * (c - 1) + q))
                    for k in range(DK):
                        last = mm(fA[q][:], h2T[:, k, c * P:(c + 1) * P], w_de[:, k, q * 512:(q + 1) * 512],
                                  start=k == 0, stop=k == DK - 1)
                last.then_inc(A_ps.sem, 1)

            def ffn_up(e, j):
                if j == 0:
                    pe.wait_ge(sim_sb.sem, sim_sb.at(e, 0))
                else:
                    pe.wait_ge(up_done.sem, up_done.at(e, j - 1))
                for a in range(2):
                    for k in range(DK):
                        last = mm(f0[:, a * TOK:(a + 1) * TOK], w_up[:, k, (2 * j + a) * P:(2 * j + a + 1) * P],
                                  h2T[:, k, :], start=k == 0, stop=k == DK - 1)
                last.then_inc(up_ps.sem, 1)

            def ffn_WT(e, c):
                pe.wait_ge(W_done.sem, W_done.at(e, c))
                for q in range(2):
                    for i in range(4):
                        last = nc.tensor.transpose(fA[q][:, i * P:(i + 1) * P],
                                                   W[:, (4 * q + i) * P:(4 * q + i + 1) * P], ident[:])
                    last.then_inc(WT_ps.sem, 1)

            def ffn_out(e, c):
                if c == 0:
                    pe.wait_ge(sim_sb.sem, sim_sb.at(e, 1))
                else:
                    pe.wait_ge(f_sb.sem, f_sb.at(e, 0))
                for i in range(FT):
                    mm(f0[:, 0:D], hid[:, i, c * P:(c + 1) * P], w_down[:, i, :], start=i == 0, stop=False)
                for q in range(2):
                    pe.wait_ge(WT_sb.sem, WT_sb.at(e, 2 * c + q))
                    for i in range(4):
                        last = mm(f0[:, 0:D], WT[:, 4 * q + i, :], w_ue[:, 4 * q + i, :], start=False,
                                  stop=q == 1 and i == 3)
                last.then_inc(f_ps.sem, 1)

            def do_group(g, e):
                a, b = g is not None, e is not None
                if b:
                    ffn_sim(e, 0)
                    ffn_A(e, 0)
                if a:
                    mixer_hT(g)
                if b:
                    ffn_up(e, 0)
                if a:
                    mixer_dt(g)
                if b:
                    for j in range(1, FT // 2):
                        ffn_up(e, j)
                if a:
                    for j in range(PAIRS):
                        mixer_pair(g, j)
                    mixer_cum(g)
                if b:
                    ffn_sim(e, 1)
                if a:
                    mixer_rows(g, 0)
                    mixer_X(g, 0)
                    mixer_z(g, 0)
                    mixer_B(g, 0)
                    mixer_Yi(g, 0)
                    mixer_scores(g, 0)
                    mixer_S(g, 0)
                if b:
                    ffn_WT(e, 0)
                    ffn_out(e, 0)
                    ffn_A(e, 1)
                if a:
                    mixer_Yn(g, 0)
                    mixer_rows(g, 1)
                    mixer_X(g, 1)
                    mixer_z(g, 1)
                    mixer_B(g, 1)
                    mixer_Yi(g, 1)
                    mixer_scores(g, 1)
                    mixer_S(g, 1)
                    mixer_yT(g, 0)
                    mixer_Yn(g, 1)
                if b:
                    ffn_WT(e, 1)
                    ffn_out(e, 1)
                if a:
                    mixer_yT(g, 1)
                    mixer_out(g)
                    mixer_h2T(g)

            do_group(0, None)
            do_group(1, 0)
            with pe.Fori(2, NG) as g:
                do_group(g, g - 1)
            do_group(None, NG - 1)


def layouts(i):
    import numpy as np

    def tiles(wT):
        return np.ascontiguousarray(wT.reshape(-1, P, wT.shape[1]).transpose(1, 0, 2))

    def every(a):
        return np.ascontiguousarray(np.broadcast_to(a, (P, a.shape[0])))

    i = {k.replace("L0_", ""): np.asarray(a) for k, a in i.items()}
    return dict(
        x=i["attn_x"].reshape(-1, D),
        in_wT=tiles(i["attn_in_proj_w"].T),
        norm_w=np.ascontiguousarray(i["attn_norm_w"].reshape(DK, P).T),
        conv_w=np.ascontiguousarray(i["attn_conv_w"].reshape(TILES, P, TAPS).transpose(1, 0, 2)),
        conv_b=np.ascontiguousarray(i["attn_conv_b"].reshape(TILES, P).T),
        dt_bias=every(i["attn_dt_bias"]),
        A_log=every(i["attn_A_log"]),
        D_skip=every(i["attn_D_skip"]),
        gnorm_w=np.ascontiguousarray(i["attn_gnorm_w"].reshape(INNER // P, P).T),
        out_wT=tiles(i["attn_out_proj_w"].T),
        upT=tiles(i["ffn_W_up"].T),
        downT=tiles(i["ffn_W_down"].T),
        wq=np.ascontiguousarray(i["ffn_W_q"].reshape(2 * RH, 64, D).transpose(1, 0, 2)),
        keysT=np.ascontiguousarray(i["ffn_keys"].transpose(3, 2, 0, 1).reshape(64, 2, TOK)),
        down_eT=tiles(i["ffn_down_embed"].T),
        up_e=tiles(i["ffn_up_embed"]),
    )


def kernel(**inputs):
    import numpy as np
    import concourse.bacc as bacc
    from concourse.bass_utils import run_bass_kernel_spmd

    nc = bacc.Bacc("TRN2", target_bir_lowering=False, num_devices=1)
    arrays = layouts(inputs)
    args = {n: nc.dram_tensor(f"{n}_dram", a.shape, mybir.dt.from_np(a.dtype), kind="ExternalInput").ap()
            for n, a in arrays.items()}
    out = nc.dram_tensor("out_dram", arrays["x"].shape, F32, kind="ExternalOutput").ap()
    sandwich(nc, out=out, **args)
    r = run_bass_kernel_spmd(nc, [{f"{n}_dram": a for n, a in arrays.items()}], core_ids=[0])
    shape = np.shape(inputs["L0_attn_x"])
    return np.asarray(r.results[0]["out_dram"]).reshape(shape)
```

```python
from contextlib import ExitStack

import concourse.bass as bass
from concourse import mybir

P = 128
ALU = mybir.AluOpType
ACT = mybir.ActivationFunctionType
BF16 = mybir.dt.bfloat16
F32 = mybir.dt.float32
U32 = mybir.dt.uint32
AX_X = mybir.AxisListType.X

D = 256
DK = D // P
HEADS = 8
HD = 64
G = 128
INNER = HEADS * HD
XBC = INNER + 2 * HEADS * G
PROJ = INNER + XBC + HEADS
TAPS = 4
CHUNK = 128
CH = 2
TOK = CH * CHUNK
TILES = XBC // P
PAIRS = TILES // 2
XP, BP = INNER // TOK, HEADS // 2
FF = 1024
FT = FF // P
EXPERTS = 1024
ET = EXPERTS // P
RH = 4
KEYS = 64
XD = EXPERTS // KEYS
TOP = 8
CAND = [(0, 1, 8), (1, 1, 4), (2, 2, 2), (4, 4, 1)]
NC = sum(r * n for _, r, n in CAND)
EPS = 1e-5
LOWEST = -3.0e38
MASKED = -1.0e30
FLT_MAX = 3.4028234e38


class Sig:

    def __init__(self, sem, per=1):
        self.sem, self.per = sem, per

    def at(self, group, k=0):
        return group * self.per + k + 1


def later(group):
    return not (isinstance(group, int) and group == 0)


class Steps:

    def __init__(self):
        self.n = 0

    def one(self):
        self.n += 1
        return 1

    def restart(self):
        self.n = 0


def sandwich(nc, x, in_wT, norm_w, conv_w, conv_b, dt_bias, A_log, D_skip, gnorm_w, out_wT,
             upT, downT, wq, keysT, down_eT, up_e, out):
    NG = x.shape[0] // TOK
    SEQ = 1024 // TOK
    xv = x.rearrange("(g c p) d -> g p c d", c=CH, p=P)
    ov = out.rearrange("(g c p) d -> g p c d", c=CH, p=P)

    with ExitStack() as ctx:
        def sb(name, shape, dt=F32):
            return ctx.enter_context(nc.sbuf_tensor(name, shape, dt))

        def sem(name):
            return ctx.enter_context(nc.semaphore(name))

        def sig(name, per=1):
            return Sig(sem(name), per)

        w_in = sb("w_in", [P, DK, PROJ])
        w_out = sb("w_out", [P, INNER // P, D])
        w_up = sb("w_up", [P, DK, FF])
        w_down = sb("w_down", [P, FT, D])
        w_de = sb("w_de", [P, DK, EXPERTS])
        w_ue = sb("w_ue", [P, ET, D])
        w_sim = sb("w_sim", [P, DK, 2 * RH * KEYS])
        cw = sb("cw", [P, TILES, TAPS])
        cb = sb("cb", [P, TILES])
        nw = sb("nw", [P, DK])
        gw = sb("gw", [P, INNER // P])
        head_c = sb("head_c", [P, 3, HEADS])
        neg_a = sb("neg_a", [P, HEADS])
        tri = sb("tri", [P, P])
        ones = sb("ones", [P, P])
        ident = sb("ident", [P, P])
        ident_b = sb("ident_b", [P, P], BF16)
        zero_b = sb("zero_b", [P, P], BF16)
        mask_b = sb("mask_b", [P, 4, P], BF16)
        iota = sb("iota", [P, KEYS, TOP], BF16)
        rank_w = sb("rank_w", [P, TOP], BF16)
        keep_tab = sb("keep_tab", [P, 2, NG])
        half_neg = sb("half_neg", [P, 2 * CH])

        x_in = sb("x_in", [P, CH, D])
        x_res = sb("x_res", [P, CH, D])
        u = sb("u", [P, CH, D])
        hn = sb("hn", [P, CH, D])
        hT = sb("hT", [P, DK, TOK])
        xp = sb("xp", [P, 2, 2, TAPS - 1 + TOK])
        acc = sb("acc", [P, 2, 2, TOK])
        halo = sb("halo", [P, TILES, TAPS - 1])
        xbcT = sb("xbcT", [P, TILES, TOK])
        keep = sb("keep", [P, 2])
        dtp = sb("dtp", [P, CH, HEADS])
        dt0 = sb("dt0", [P, CH, HEADS])
        dt1 = sb("dt1", [P, CH, HEADS])
        dt2 = sb("dt2", [P, CH, HEADS])
        dte = sb("dte", [P, CH, HEADS])
        dte2 = sb("dte2", [P, CH, HEADS])
        dta = sb("dta", [P, CH, HEADS])
        minus1 = sb("minus1", [P, CH, HEADS])
        dts = sb("dts", [P, CH, HEADS])
        da = sb("da", [P, CH, HEADS])
        cum = sb("cum", [P, 3, CH, HEADS])
        ecum = sb("ecum", [P, 3, CH, HEADS])
        ncum = sb("ncum", [P, CH, HEADS])
        lnst = sb("lnst", [P, CH, 6])
        mv1 = sb("mv1", [P, CH, 2])
        mv2 = sb("mv2", [P, CH, 2])
        mv3 = sb("mv3", [P, CH, 2])
        rs1 = sb("rs1", [P, CH])
        rs1b = sb("rs1b", [P, CH])
        rs2 = sb("rs2", [P, CH])
        rs12 = sb("rs12", [P, CH])
        ve = sb("ve", [P, 2 * CH])
        ve3 = sb("ve3", [P, CH])
        ve4 = sb("ve4", [P, CH])
        vey = sb("vey", [P, CH])
        sumst = sb("sumst", [P, CH, 6])
        resst = sb("resst", [P, CH, 6])
        rsy = sb("rsy", [P, CH])
        rs3 = sb("rs3", [P, CH])
        rs4 = sb("rs4", [P, CH])
        Xt = sb("Xt", [P, INNER])
        Xdt = sb("Xdt", [P, INNER])
        Xw = sb("Xw", [P, INNER])
        DX = sb("DX", [P, INNER])
        Btok = sb("Btok", [P, HEADS, G])
        Ldec = sb("Ldec", [P, HEADS, CHUNK])
        sL = sb("sL", [P, HEADS, CHUNK])
        H = sb("H", [P, INNER])
        zs = sb("zs", [P, CH, INNER])
        yv = sb("yv", [P, CH, INNER])
        ssq = sb("ssq", [P, CH])
        yT = sb("yT", [P, INNER])
        v = sb("v", [P, CH, D])
        x1 = sb("x1", [P, CH, D])
        x1_late = sb("x1_late", [P, CH, D])
        h2T = sb("h2T", [P, DK, TOK])

        hid = sb("hid", [P, FT, TOK])
        sim = sb("sim", [P, CH, 2, RH, KEYS])
        s8 = sb("s8", [P, 2, RH, TOP])
        i8 = sb("i8", [P, 2, RH, TOP], U32)
        i8b = sb("i8b", [P, 2, RH, TOP], BF16)
        cand = sb("cand", [P, RH, NC])
        c8 = sb("c8", [P, RH, TOP])
        rest = sb("rest", [P, RH, NC])
        chosen = sb("chosen", [P, RH, NC])
        n8 = sb("n8", [P, RH, TOP], BF16)
        ee = sb("ee", [P, CH, RH, XD + KEYS + NC])
        psel = sb("psel", [P, RH, NC])
        den = sb("den", [P, RH])
        rden = sb("rden", [P, CH, RH])
        cmask = sb("cmask", [P, RH, TOP])
        clz = sb("clz", [P, CH, RH, NC])
        cls = sb("cls", [P, RH, NC])
        clsum = sb("clsum", [P, CH])
        last_a = sb("last_a", [P, 1])
        eq = sb("eq", [P, RH, XD + KEYS, TOP], BF16)
        rk = sb("rk", [P, CH, RH, XD + KEYS], BF16)
        Dm = sb("Dm", [P, RH, XD, KEYS], BF16)
        Em = sb("Em", [P, RH, XD, KEYS])
        W = sb("W", [P, EXPERTS])
        WT = sb("WT", [P, ET, P])
        f = sb("f", [P, CH, D])
        fst = sb("fst", [P, CH, 6])
        mvf = sb("mvf", [P, CH, 2])
        vf = sb("vf", [P, CH])
        rsf = sb("rsf", [P, CH])

        pool_psum = [ctx.enter_context(nc.psum_tensor(f"bank{i}", [P, 512], F32)) for i in range(8)]
        ring = pool_psum[0:2]
        pairb = pool_psum[2:4]
        yb = pool_psum[4]
        f0 = pool_psum[5]
        fA = pool_psum[6:8]

        loaded_c = sem("loaded_c")
        loaded_w = sem("loaded_w")
        consts = sem("consts")
        folded = sem("folded")
        simw_ps, simw_sb = sem("simw_ps"), sem("simw_sb")
        x_loaded, xres_loaded = sem("x_loaded"), sem("xres_loaded")
        x_read = sig("x_read")
        stored = sem("stored")
        own_dve, own_act, own_pool = sem("own_dve"), sem("own_act"), sem("own_pool")
        arrived_dve, arrived_act, arrived_pool = sem("arrived_dve"), sem("arrived_act"), sem("arrived_pool")
        stats1, root1, u_done = sig("stats1"), sig("root1"), sig("u_done")
        hn_done, hT_ps, hT_sb = sig("hn_done"), sig("hT_ps"), sig("hT_sb")
        dt_ps, dt_sb, dt_abs, dte_done, da_done = (sig(n) for n in ("dt_ps", "dt_sb", "dt_abs", "dte_done", "da_done"))
        cum_ps, cum_sb, cum_diff, ecum_done = (sig(n) for n in ("cum_ps", "cum_sb", "cum_diff", "ecum_done"))
        pair_ps, pair_copied, pair_read = sig("pair_ps", PAIRS), sig("pair_copied", PAIRS), sig("pair_read", PAIRS)
        conv_done, silu_done = sig("conv_done", PAIRS), sig("silu_done", PAIRS)
        rows_ps, decay_done = sig("rows_ps", 2 * CH), sig("decay_done", 2 * CH)
        X_ps, X_sb, z_ps, z_done = sig("X_ps", CH), sig("X_sb", CH), sig("z_ps", CH), sig("z_done", CH)
        Bt_ps, Bt_sb = sig("Bt_ps", 2 * CH), sig("Bt_sb", 2 * CH)
        sc_ps, sL_done = sig("sc_ps", 2 * CH), sig("sL_done", 2 * CH)
        Yi_ps, Yi_read = sig("Yi_ps", CH), sig("Yi_read", CH)
        Xw_done, DX_done = sig("Xw_done", CH), sig("DX_done", CH)
        S_ps, H_done, H_kept = sig("S_ps", CH), sig("H_done", CH), sig("H_kept")
        Yn_ps, Yn_read = sig("Yn_ps", CH), sig("Yn_read", CH)
        y_done, sq_done = sig("y_done", CH), sig("sq_done", CH)
        yT_ps, yT_sb = sig("yT_ps", CH), sig("yT_sb", CH)
        rooty, out_ps, out_read = sig("rooty"), sig("out_ps", CH), sig("out_read")
        stats3, root3, stats4, root4 = sig("stats3"), sig("root3"), sig("stats4"), sig("root4")
        h2_done, h2T_ps, h2T_sb, xres_read = sig("h2_done"), sig("h2T_ps"), sig("h2T_sb"), sig("xres_read")
        sim_ps, sim_sb = sig("sim_ps", CH), sig("sim_sb", CH)
        A_ps = sig("A_ps", CH)
        up_ps, up_done = sig("up_ps", FT // 2), sig("up_done", FT // 2)
        earg_done, ee_done, ranks_done = sig("earg_done", CH), sig("ee_done", CH), sig("ranks_done", CH)
        D_done, E_done, P_done, Z_done, Zs_done = (
            sig(n, CH * RH) for n in ("D_done", "E_done", "P_done", "Z_done", "Zs_done"))
        clz_done, cls_done = sig("clz_done", CH), sig("cls_done", CH)
        W_part, W_done = sig("W_part", CH * (RH - 1)), sig("W_done", CH)
        WT_ps, WT_sb = sig("WT_ps", 2 * CH), sig("WT_sb", 2 * CH)
        out_part, f_ps, f_sb, x1_kept = sig("out_part"), sig("f_ps"), sig("f_sb"), sig("x1_kept")
        down_ps = sig("down_ps", CH)
        statsf, rootf, o_done = sig("statsf"), sig("rootf"), sig("o_done")

        block = ctx.enter_context(nc.Block())

        def bc(ap, axis, n):
            return ap.unsqueeze(axis).to_broadcast([*ap.shape[:axis], n, *ap.shape[axis:]])

        @block.sync
        def _(sp):
            sp.dma_start(x_in[:], xv[0]).then_inc(x_loaded, 16)
            sp.dma_start(nw[:], norm_w).then_inc(loaded_c, 16)
            sp.dma_start(gw[:], gnorm_w).then_inc(loaded_c, 16)
            sp.dma_start(cw[:], conv_w).then_inc(loaded_c, 16)
            sp.dma_start(cb[:], conv_b).then_inc(loaded_c, 16)
            sp.dma_start(head_c[:, 0, :], dt_bias).then_inc(loaded_c, 16)
            sp.dma_start(head_c[:, 1, :], A_log).then_inc(loaded_c, 16)
            sp.dma_start(head_c[:, 2, :], D_skip).then_inc(loaded_c, 16)
            sp.dma_start(hid[0:64, :, :], wq).then_inc(loaded_c, 16)
            sp.dma_start(xbcT[0:64, 0:2, :], keysT).then_inc(loaded_c, 16)
            sp.dma_start(w_in[:], in_wT).then_inc(loaded_w, 16)
            sp.dma_start(w_out[:], out_wT).then_inc(loaded_w, 16)
            sp.dma_start(w_up[:], upT).then_inc(loaded_w, 16)
            sp.dma_start(w_de[:], down_eT).then_inc(loaded_w, 16)
            sp.dma_start(w_down[:], downT).then_inc(loaded_w, 16)
            sp.dma_start(w_ue[:], up_e).then_inc(loaded_w, 16)

            def rows_of(g, more):
                if later(g):
                    sp.wait_ge(xres_read.sem, xres_read.at(g - 1))
                sp.dma_start(x_res[:], xv[g]).then_inc(xres_loaded, 16)
                if more:
                    sp.wait_ge(x_read.sem, x_read.at(g))
                    sp.dma_start(x_in[:], xv[g + 1]).then_inc(x_loaded, 16)

            def store(e):
                sp.wait_ge(o_done.sem, o_done.at(e))
                sp.dma_start(ov[e], f[:]).then_inc(stored, 16)

            rows_of(0, True)
            rows_of(1, True)
            store(0)
            with sp.Fori(2, NG - 1) as g:
                rows_of(g, True)
                store(g - 1)
            rows_of(NG - 1, False)
            store(NG - 2)
            store(NG - 1)
            sp.wait_ge(stored, 16 * NG)

        @block.gpsimd
        def _(pool):
            own = Steps()
            nc.gpsimd.memset(tri[:], 1.0).then_inc(own_pool, own.one())
            nc.gpsimd.memset(ones[:], 1.0).then_inc(own_pool, own.one())
            nc.gpsimd.memset(ident[:], 0.0).then_inc(own_pool, own.one())
            nc.gpsimd.memset(mask_b[:], 0.0).then_inc(own_pool, own.one())
            nc.gpsimd.memset(zero_b[:], 0.0).then_inc(own_pool, own.one())
            nc.gpsimd.memset(halo[:], 0.0).then_inc(own_pool, own.one())
            nc.gpsimd.memset(H[:], 0.0).then_inc(own_pool, own.one())
            nc.gpsimd.memset(minus1[:], -1.0).then_inc(own_pool, own.one())
            nc.gpsimd.memset(half_neg[:], -0.5).then_inc(own_pool, own.one())
            nc.gpsimd.memset(keep_tab[:, 0], FLT_MAX).then_inc(own_pool, own.one())
            nc.gpsimd.memset(keep_tab[:, 1], -FLT_MAX).then_inc(own_pool, own.one())
            for r in range(TOP):
                nc.gpsimd.memset(rank_w[:, r:r + 1], float(TOP - r)).then_inc(own_pool, own.one())
            nc.gpsimd.iota(iota[:], pattern=[[1, KEYS], [0, TOP]], base=0, channel_multiplier=0,
                                  allow_small_or_imprecise_dtypes=True).then_inc(own_pool, own.one())
            pool.wait_ge(own_pool, own.n)
            nc.gpsimd.memset(keep_tab[:, :, 0:NG:SEQ], 0.0).then_inc(own_pool, own.one())
            nc.gpsimd.affine_select(out=tri[:], in_=tri[:], compare_op=ALU.is_ge, fill=0.0,
                                           base=0, pattern=[[1, P]], channel_multiplier=-1).then_inc(own_pool, own.one())
            nc.gpsimd.affine_select(out=mask_b[:], in_=mask_b[:], compare_op=ALU.is_ge, fill=MASKED,
                                           base=0, pattern=[[0, 4], [1, P]], channel_multiplier=-1).then_inc(own_pool, own.one())
            nc.gpsimd.affine_select(out=ident[:], in_=ident[:], compare_op=ALU.not_equal, fill=1.0,
                                           base=0, pattern=[[-1, P]], channel_multiplier=1).then_inc(own_pool, own.one())
            pool.wait_ge(own_pool, own.n)
            nc.gpsimd.tensor_copy(ident_b[:], ident[:]).then_inc(consts, 1)
            pool.wait_ge(own_pool, own.n)
            pool.sem_clear(own_pool)
            own.restart()

            def mixer_norm(g):
                pool.wait_ge(stats1.sem, stats1.at(g))
                pool.sem_inc(arrived_pool, 1)
                nc.gpsimd.tensor_scalar(ve[:, 0:CH], mv1[:, :, 1], EPS, None, ALU.add).then_inc(own_pool, own.one())
                pool.wait_ge(own_pool, own.n)
                nc.gpsimd.tensor_tensor(rs1[:], ve[:, 0:CH], half_neg[:, 0:CH], ALU.pow).then_inc(own_pool, own.one())
                pool.wait_ge(own_pool, own.n)
                nc.gpsimd.tensor_tensor(rs1b[:], rs1[:], rs1[:], ALU.mult).then_inc(own_pool, own.one())
                pool.wait_ge(own_pool, own.n)
                nc.gpsimd.tensor_tensor(ve[:, CH:], rs1b[:], mv1[:, :, 1], ALU.mult).then_inc(own_pool, own.one())
                pool.wait_ge(own_pool, own.n)
                nc.gpsimd.tensor_scalar(ve[:, CH:], ve[:, CH:], EPS, None, ALU.add).then_inc(own_pool, own.one())
                pool.wait_ge(own_pool, own.n)
                nc.gpsimd.tensor_tensor(rs2[:], ve[:, CH:], half_neg[:, 0:CH], ALU.pow).then_inc(own_pool, own.one())
                pool.wait_ge(own_pool, own.n)
                nc.gpsimd.tensor_tensor(rs12[:], rs1[:], rs2[:], ALU.mult).then_inc(root1.sem, 1)

            def mixer_dt_abs(g):
                pool.wait_ge(dt_sb.sem, dt_sb.at(g))
                nc.gpsimd.tensor_tensor(dt0[:], dtp[:], bc(head_c[:, 0, :], 1, CH), ALU.add)\
                    .then_inc(own_pool, own.one())
                pool.wait_ge(own_pool, own.n)
                nc.gpsimd.tensor_scalar(dt2[:], dt0[:], 0.0, 2.0, ALU.max, ALU.mult).then_inc(own_pool, own.one())
                pool.wait_ge(own_pool, own.n)
                nc.gpsimd.tensor_tensor(dt1[:], dt2[:], dt0[:], ALU.subtract).then_inc(dt_abs.sem, 1)

            def mixer_dt(g):
                pool.wait_ge(dte_done.sem, dte_done.at(g))
                pool.sem_inc(arrived_pool, 1)
                nc.gpsimd.tensor_scalar(dt1[:], dte[:], 2.0, None, ALU.add).then_inc(own_pool, own.one())
                pool.wait_ge(own_pool, own.n)
                nc.gpsimd.tensor_tensor(dts[:], dt1[:], minus1[:], ALU.pow).then_inc(own_pool, own.one())
                pool.wait_ge(own_pool, own.n)
                nc.gpsimd.tensor_tensor(dt1[:], dts[:], dte[:], ALU.mult).then_inc(own_pool, own.one())
                pool.wait_ge(own_pool, own.n)
                nc.gpsimd.tensor_tensor(dte2[:], dt1[:], dt1[:], ALU.mult).then_inc(own_pool, own.one())
                pool.wait_ge(own_pool, own.n)
                nc.gpsimd.tensor_scalar(dta[:], dte2[:], 2.0 / 17, 2.0 / 15, ALU.mult, ALU.add)\
                    .then_inc(own_pool, own.one())
                for n in (13, 11, 9, 7, 5, 3, 1):
                    pool.wait_ge(own_pool, own.n)
                    nc.gpsimd.tensor_tensor(dta[:], dta[:], dte2[:], ALU.mult).then_inc(own_pool, own.one())
                    pool.wait_ge(own_pool, own.n)
                    nc.gpsimd.tensor_scalar(dta[:], dta[:], 2.0 / n, None, ALU.add).then_inc(own_pool, own.one())
                pool.wait_ge(own_pool, own.n)
                nc.gpsimd.tensor_tensor(dta[:], dta[:], dt1[:], ALU.mult).then_inc(own_pool, own.one())
                nc.gpsimd.tensor_scalar(dt2[:], dt2[:], 0.5, None, ALU.mult).then_inc(own_pool, own.one())
                pool.wait_ge(own_pool, own.n)
                if later(g):
                    pool.wait_ge(Xw_done.sem, Xw_done.at(g - 1, CH - 1))
                nc.gpsimd.tensor_tensor(dts[:], dta[:], dt2[:], ALU.add).then_inc(own_pool, own.one())
                pool.wait_ge(own_pool, own.n)
                if later(g):
                    pool.wait_ge(rows_ps.sem, rows_ps.at(g - 1, 2 * CH - 1))
                nc.gpsimd.tensor_tensor(da[:], dts[:], bc(neg_a[:], 1, CH), ALU.mult).then_inc(da_done.sem, 1)

            def mixer_cum(g):
                pool.wait_ge(cum_sb.sem, cum_sb.at(g))
                nc.gpsimd.tensor_tensor(cum[:, 1], cum[:, 2], cum[:, 0], ALU.subtract).then_inc(own_pool, own.one())
                if later(g):
                    pool.wait_ge(decay_done.sem, decay_done.at(g - 1, 2 * CH - 1))
                pool.wait_ge(own_pool, own.n)
                pool.sem_inc(arrived_pool, 1)
                nc.gpsimd.tensor_scalar(ncum[:], cum[:, 0], -1.0, None, ALU.mult).then_inc(cum_diff.sem, 1)

            def mixer_skip(g, c):
                pool.wait_ge(X_sb.sem, X_sb.at(g, c))
                if c or later(g):
                    pool.wait_ge(Yn_read.sem, Yn_read.at(g, c - 1))
                nc.gpsimd.tensor_tensor(DX[:].rearrange("p (h d) -> p h d", h=HEADS),
                                        Xt[:].rearrange("p (h d) -> p h d", h=HEADS),
                                        bc(head_c[:, 2, :], 2, HD), ALU.mult).then_inc(DX_done.sem, 1)

            def mixer_root_y(g):
                pool.wait_ge(sq_done.sem, sq_done.at(g, CH - 1))
                pool.sem_inc(arrived_pool, 1)
                nc.gpsimd.tensor_scalar(vey[:], ssq[:], 1.0 / INNER, EPS, ALU.mult, ALU.add)\
                    .then_inc(own_pool, own.one())
                pool.wait_ge(own_pool, own.n)
                nc.gpsimd.tensor_tensor(rsy[:], vey[:], half_neg[:, 0:CH], ALU.pow).then_inc(rooty.sem, 1)

            def tail_root(t, stats, mv, scratch, dst, done):
                pool.wait_ge(stats.sem, stats.at(t))
                pool.sem_inc(arrived_pool, 1)
                nc.gpsimd.tensor_scalar(scratch[:], mv[:, :, 1], EPS, None, ALU.add).then_inc(own_pool, own.one())
                pool.wait_ge(own_pool, own.n)
                nc.gpsimd.tensor_tensor(dst[:], scratch[:], half_neg[:, 0:CH], ALU.pow).then_inc(done.sem, 1)

            def weigh(e, c, *heads):
                for h in heads:
                    if c or later(e):
                        pool.wait_ge(W_part.sem, W_part.at(e, (c - 1) * (RH - 1) + max(h - 1, 0)))
                    if h == 0:
                        pool.wait_ge(ee_done.sem, ee_done.at(e, c))
                    nc.gpsimd.tensor_tensor(Em[:, h], bc(ee[:, c, h, 0:XD], 2, KEYS),
                                            bc(ee[:, c, h, XD:XD + KEYS], 1, XD), ALU.mult).then_inc(E_done.sem, 1)

            def rank(e, c, *heads):
                for h in heads:
                    if c or later(e):
                        pool.wait_ge(P_done.sem, P_done.at(e, (c - 1) * RH + h))
                    if h == 0:
                        pool.wait_ge(ranks_done.sem, ranks_done.at(e, c))
                    nc.gpsimd.tensor_tensor(Dm[:, h], bc(rk[:, c, h, 0:XD], 2, KEYS),
                                            bc(rk[:, c, h, XD:], 1, XD), ALU.add).then_inc(D_done.sem, 1)

            def collect(e, c, *heads):
                flat = [Em[:, h].rearrange("p a b -> p (a b)") for h in range(RH)]
                for h in heads:
                    if h == 1:
                        pool.wait_ge(Zs_done.sem, Zs_done.at(e, c * RH))
                        if c or later(e):
                            pool.wait_ge(WT_ps.sem, WT_ps.at(e, 2 * (c - 1) + 1))
                    pool.wait_ge(Zs_done.sem, Zs_done.at(e, c * RH + h))
                    if h >= 2:
                        pool.wait_ge(W_part.sem, W_part.at(e, c * (RH - 1) + h - 2))
                    nc.gpsimd.tensor_tensor(W[:], flat[0] if h == 1 else W[:], flat[h], ALU.add)\
                        .then_inc(W_part.sem, 1)
                    if h == RH - 1:
                        pool.wait_ge(cls_done.sem, cls_done.at(e, c))
                        pool.wait_ge(W_part.sem, W_part.at(e, c * (RH - 1) + RH - 2))
                        nc.gpsimd.tensor_tensor(W[:, EXPERTS - 1:], W[:, EXPERTS - 1:], clsum[:, c:c + 1], ALU.add)\
                            .then_inc(W_done.sem, 1)

            def do_group(g, e, f, n):
                a, b, c = g is not None, e is not None, f is not None
                if b:
                    tail_root(e, stats4, mv3, ve4, rs4, root4)
                if c:
                    weigh(f, 1, 0)
                if a:
                    mixer_dt_abs(g)
                if c:
                    weigh(f, 1, 1, 2, 3)
                    rank(f, 1, 3)
                if a:
                    mixer_dt(g)
                if c:
                    collect(f, 1, 1, 2, 3)
                if a:
                    mixer_cum(g)
                if c:
                    tail_root(f, statsf, mvf, vf, rsf, rootf)
                if b:
                    weigh(e, 0, 0)
                    rank(e, 0, 0)
                if a:
                    mixer_skip(g, 0)
                if b:
                    weigh(e, 0, 1, 2)
                    rank(e, 0, 1, 2)
                if a:
                    mixer_skip(g, 1)
                if b:
                    weigh(e, 0, 3)
                    rank(e, 0, 3)
                    rank(e, 1, 0, 1)
                if a:
                    mixer_root_y(g)
                if n is not None:
                    mixer_norm(n)
                if b:
                    collect(e, 0, 1)
                if a:
                    tail_root(g, stats3, mv2, ve3, rs3, root3)
                if b:
                    rank(e, 1, 2)
                    collect(e, 0, 2, 3)
                pool.wait_ge(own_pool, own.n)
                pool.sem_clear(own_pool)
                own.restart()

            mixer_norm(0)
            do_group(0, None, None, 1)
            do_group(1, 0, None, 2)
            do_group(2, 1, 0, 3)
            with pool.Fori(3, NG - 1) as g:
                do_group(g, g - 1, g - 2, g + 1)
            do_group(NG - 1, NG - 2, NG - 3, None)
            do_group(None, NG - 1, NG - 2, None)
            do_group(None, None, NG - 1, None)

        @block.scalar
        def _(act):
            own = Steps()
            act.wait_ge(loaded_c, 16 * 9)
            nc.scalar.activation(neg_a[:], head_c[:, 1, :], ACT.Exp).then_inc(own_act, own.one())
            act.wait_ge(own_act, own.n)
            nc.scalar.mul(neg_a[:], neg_a[:], -1.0).then_inc(own_act, own.one())
            for k in range(DK):
                act.wait_ge(simw_ps, k + 1)
                nc.scalar.activation(w_sim[:, k, :], ring[k][:, :], ACT.Copy).then_inc(own_act, own.one())
            act.wait_ge(own_act, own.n)
            act.sem_inc(simw_sb, 1)
            act.wait_ge(own_act, own.n)
            act.sem_clear(own_act)
            own.restart()

            def mixer_hT(g):
                act.wait_ge(hT_ps.sem, hT_ps.at(g))
                nc.scalar.activation(hT[:], yb[:].rearrange("p (k t) -> p k t", k=DK), ACT.Copy)\
                    .then_inc(hT_sb.sem, 1)

            def mixer_dt(g):
                act.wait_ge(dt_ps.sem, dt_ps.at(g))
                if later(g):
                    act.wait_ge(da_done.sem, da_done.at(g - 1))
                nc.scalar.activation(dtp[:], ring[1][:, 0:CH * HEADS].rearrange("p (c h) -> p c h", c=CH), ACT.Copy)\
                    .then_inc(dt_sb.sem, 1)

            def mixer_dt_exp(g):
                act.wait_ge(dt_abs.sem, dt_abs.at(g))
                nc.scalar.activation(dte[:], dt1[:], ACT.Exp, scale=-1.0).then_inc(dte_done.sem, 1)

            def silu(g, j):
                act.wait_ge(conv_done.sem, conv_done.at(g, j))
                nc.scalar.activation(xbcT[:, 2 * j:2 * j + 2, :], acc[:, j % 2], ACT.Silu)\
                    .then_inc(silu_done.sem, 1)

            def mixer_pair(g, j):
                r = j % 2
                ps = ring[j % 2]
                act.wait_ge(pair_ps.sem, pair_ps.at(g, j))
                if j >= 2 or later(g):
                    act.wait_ge(conv_done.sem, conv_done.at(g, j - 2))
                nc.scalar.activation(xp[:, r, :, TAPS - 1:], ps[:].rearrange("p (a t) -> p a t", a=2), ACT.Copy)\
                    .then_inc(pair_copied.sem, 1)
                if j >= 2 or later(g):
                    act.wait_ge(silu_done.sem, silu_done.at(g, j - 2))
                for a in range(2):
                    t = 2 * j + a
                    last = nc.scalar.activation(acc[:, r, a], ps[:, a * TOK:(a + 1) * TOK], ACT.Identity,
                                                scale=cw[:, t, TAPS - 1:TAPS], bias=cb[:, t:t + 1])
                last.then_inc(pair_read.sem, 1)

            def mixer_cum(g):
                act.wait_ge(cum_ps.sem, cum_ps.at(g))
                if later(g):
                    act.wait_ge(ecum_done.sem, ecum_done.at(g - 1))
                nc.scalar.activation(cum[:, 0:3:2], yb[:, 0:2 * CH * HEADS].rearrange("p (a c h) -> p a c h", a=2, c=CH),
                                     ACT.Copy).then_inc(cum_sb.sem, 1)

            def mixer_exp(g):
                act.wait_ge(cum_diff.sem, cum_diff.at(g))
                if later(g):
                    act.wait_ge(H_done.sem, H_done.at(g - 1, CH - 1))
                nc.scalar.activation(ecum[:], cum[:], ACT.Exp).then_inc(ecum_done.sem, 1)

            def mixer_decay(g, c):
                for q in range(2):
                    act.wait_ge(rows_ps.sem, rows_ps.at(g, 2 * c + q))
                    k = 2 * c + q
                    if k >= 2 or later(g):
                        act.wait_ge(sL_done.sem, sL_done.at(g, k - 2))
                    for i in range(4):
                        h = 4 * q + i
                        last = nc.scalar.activation(Ldec[:, h, :], pairb[q][:, i * P:(i + 1) * P], ACT.Exp,
                                                    bias=ncum[:, c, h:h + 1])
                    last.then_inc(decay_done.sem, 1)

            def mixer_move(g, c):
                act.wait_ge(X_ps.sem, X_ps.at(g, c))
                if c or later(g):
                    act.wait_ge(Xw_done.sem, Xw_done.at(g, c - 1))
                if c or later(g):
                    act.wait_ge(DX_done.sem, DX_done.at(g, c - 1))
                nc.scalar.activation(Xt[:], ring[c][:], ACT.Copy).then_inc(X_sb.sem, 1)

            def mixer_B(g, c):
                for q in range(2):
                    act.wait_ge(Bt_ps.sem, Bt_ps.at(g, 2 * c + q))
                    if c or later(g):
                        act.wait_ge(S_ps.sem, S_ps.at(g, c - 1))
                    nc.scalar.activation(Btok[:, 4 * q:4 * q + 4, :],
                                         pairb[q][:].rearrange("p (h t) -> p h t", h=4), ACT.Copy)\
                        .then_inc(Bt_sb.sem, 1)

            def mixer_z(g, c):
                act.wait_ge(z_ps.sem, z_ps.at(g, c))
                if later(g):
                    act.wait_ge(sq_done.sem, sq_done.at(g - 1, c))
                nc.scalar.activation(zs[:, c], ring[c][:], ACT.Silu).then_inc(z_done.sem, 1)

            def mixer_square(g, c):
                act.wait_ge(y_done.sem, y_done.at(g, c))
                if c == 0 and later(g):
                    act.wait_ge(rooty.sem, rooty.at(g - 1))
                nc.scalar.activation(zs[:, c], yv[:, c], ACT.Square, accum_out=ssq[:, c:c + 1])\
                    .then_inc(sq_done.sem, 1)

            def mixer_yT(g, c):
                act.wait_ge(yT_ps.sem, yT_ps.at(g, c))
                if c or later(g):
                    act.wait_ge(out_ps.sem, out_ps.at(g, c - 1))
                nc.scalar.activation(yT[:], ring[c][:], ACT.Copy).then_inc(yT_sb.sem, 1)

            def tail_keep(t):
                act.wait_ge(xres_read.sem, xres_read.at(t))
                if later(t):
                    act.wait_ge(o_done.sem, o_done.at(t - 1))
                nc.scalar.activation(x1_late[:], x1[:], ACT.Copy).then_inc(x1_kept.sem, 1)

            def tail_h2T(t):
                act.wait_ge(h2T_ps.sem, h2T_ps.at(t))
                if later(t):
                    act.wait_ge(A_ps.sem, A_ps.at(t - 1, CH - 1))
                nc.scalar.activation(h2T[:], yb[:].rearrange("p (k t) -> p k t", k=DK), ACT.Copy)\
                    .then_inc(h2T_sb.sem, 1)

            def ffn_sim(e, c):
                act.wait_ge(sim_ps.sem, sim_ps.at(e, c))
                if later(e):
                    act.wait_ge(earg_done.sem, earg_done.at(e - 1, c))
                nc.scalar.activation(sim[:, c].rearrange("p a h k -> p (a h k)"), yb[:], ACT.Copy)\
                    .then_inc(sim_sb.sem, 1)

            def ffn_up(e, j):
                act.wait_ge(up_ps.sem, up_ps.at(e, j))
                if later(e):
                    act.wait_ge(down_ps.sem, down_ps.at(e - 1, CH - 1))
                nc.scalar.activation(hid[:, 2 * j:2 * j + 2, :], yb[:].rearrange("p (a t) -> p a t", a=2), ACT.Silu)\
                    .then_inc(up_done.sem, 1)

            def ffn_exp(e, c):
                act.wait_ge(earg_done.sem, earg_done.at(e, c))
                nc.scalar.activation(ee[:, c], ee[:, c], ACT.Exp).then_inc(ee_done.sem, 1)

            def ffn_experts(e, c, lo, hi):
                if lo == 0:
                    act.wait_ge(clz_done.sem, clz_done.at(e, c))
                    if c or later(e):
                        act.wait_ge(cls_done.sem, cls_done.at(e, c - 1))
                    if later(e):
                        act.wait_ge(W_done.sem, W_done.at(e - 1, c))
                    nc.scalar.activation(cls[:], clz[:, c], ACT.Silu, accum_out=clsum[:, c:c + 1])\
                        .then_inc(cls_done.sem, 1)
                for h in range(lo, hi):
                    act.wait_ge(Z_done.sem, Z_done.at(e, c * RH + h))
                    flat = Em[:, h].rearrange("p a b -> p (a b)")
                    nc.scalar.activation(flat, flat, ACT.Silu, scale=rden[:, c, h:h + 1]).then_inc(Zs_done.sem, 1)

            def ffn_WT(e, c):
                for q in range(2):
                    act.wait_ge(WT_ps.sem, WT_ps.at(e, 2 * c + q))
                    if c or later(e):
                        act.wait_ge(out_part.sem if c else f_ps.sem, out_part.at(e) if c else f_ps.at(e - 1))
                    nc.scalar.activation(WT[:, 4 * q:4 * q + 4, :],
                                         pairb[q][:].rearrange("p (h t) -> p h t", h=4), ACT.Copy)\
                        .then_inc(WT_sb.sem, 1)

            def ffn_out(e):
                act.wait_ge(f_ps.sem, f_ps.at(e))
                if later(e):
                    act.wait_ge(stored, 16 * e)
                nc.scalar.activation(f[:], f0[:].rearrange("p (c d) -> p c d", c=CH), ACT.Copy).then_inc(f_sb.sem, 1)

            def do_group(g, e, f, n):
                a, b, c = g is not None, e is not None, f is not None

                def pairs(*js):
                    for j in js:
                        if a:
                            if j >= 2:
                                silu(g, j - 2)
                            mixer_pair(g, j)

                if a:
                    mixer_dt(g)
                pairs(0)
                if a:
                    mixer_dt_exp(g)
                pairs(1)
                if c:
                    ffn_WT(f, 0)
                if b:
                    tail_h2T(e)
                pairs(2)
                if b:
                    ffn_sim(e, 0)
                if c:
                    ffn_experts(f, 1, 0, 1)
                pairs(3)
                if a:
                    mixer_z(g, 0)
                if b:
                    ffn_sim(e, 1)
                if a:
                    mixer_z(g, 1)
                if c:
                    ffn_experts(f, 1, 1, 2)
                pairs(4)
                if c:
                    ffn_experts(f, 1, 2, 3)
                pairs(5)
                if c:
                    ffn_experts(f, 1, 3, RH)
                pairs(6)
                if b:
                    ffn_up(e, 0)
                pairs(7)
                if b:
                    ffn_up(e, 1)
                    ffn_exp(e, 0)
                if a:
                    mixer_cum(g)
                pairs(8)
                if b:
                    ffn_up(e, 2)
                pairs(9)
                if b:
                    ffn_up(e, 3)
                if a:
                    silu(g, PAIRS - 2)
                    silu(g, PAIRS - 1)
                    mixer_move(g, 0)
                if c:
                    ffn_WT(f, 1)
                if a:
                    mixer_exp(g)
                    mixer_decay(g, 0)
                if c:
                    ffn_out(f)
                if a:
                    mixer_B(g, 0)
                if b:
                    ffn_exp(e, 1)
                if a:
                    mixer_move(g, 1)
                    mixer_decay(g, 1)
                    mixer_B(g, 1)
                    mixer_square(g, 0)
                    mixer_yT(g, 0)
                if b:
                    tail_keep(e)
                    ffn_experts(e, 0, 0, 2)
                if a:
                    mixer_square(g, 1)
                    mixer_yT(g, 1)
                if b:
                    ffn_experts(e, 0, 2, 3)
                if n is not None:
                    mixer_hT(n)
                if b:
                    ffn_experts(e, 0, 3, RH)

            mixer_hT(0)
            do_group(0, None, None, 1)
            do_group(1, 0, None, 2)
            do_group(2, 1, 0, 3)
            with act.Fori(3, NG - 1) as g:
                do_group(g, g - 1, g - 2, g + 1)
            do_group(NG - 1, NG - 2, NG - 3, None)
            do_group(None, NG - 1, NG - 2, None)
            do_group(None, None, NG - 1, None)

        @block.vector
        def _(dve):
            own = Steps()
            V = nc.vector
            dve.wait_ge(loaded_c, 16 * 9)
            dve.wait_ge(loaded_w, 16 * 6)
            for k in range(DK):
                last = V.tensor_scalar(w_in[:, k, :], w_in[:, k, :], nw[:, k:k + 1], None, ALU.mult)
                last.then_inc(own_dve, own.one())
            for k in range(INNER // P):
                V.tensor_scalar(w_out[:, k, :], w_out[:, k, :], gw[:, k:k + 1], None, ALU.mult).then_inc(own_dve, own.one())
            dve.wait_ge(own_dve, own.n)
            dve.sem_inc(folded, 1)
            dve.wait_ge(consts, 1)

            dve.wait_ge(own_dve, own.n)
            dve.sem_clear(own_dve)
            own.restart()

            def heads3(ap):
                return ap.rearrange("p (h d) -> p h d", h=HEADS)

            def mixer_stats(g):
                dve.wait_ge(x_loaded, 16 * (g + 1))
                for c in range(CH):
                    V.bn_stats(lnst[:, c, :], x_in[:, c, :]).then_inc(own_dve, own.one())
                dve.wait_ge(own_dve, own.n)
                for c in range(CH):
                    last = V.bn_aggr(mv1[:, c, :], lnst[:, c, :])
                last.then_inc(stats1.sem, 1)
                V.tensor_copy(keep[:].unsqueeze(2), keep_tab[:, :, bass.ds(g, 1)]).then_inc(own_dve, own.one())
                dve.wait_ge(own_dve, own.n)
                V.tensor_scalar(halo[:], halo[:], keep[:, 0:1], keep[:, 1:2], ALU.min, ALU.max)\
                    .then_inc(own_dve, own.one())
                if later(g):
                    dve.wait_ge(Yi_ps.sem, Yi_ps.at(g - 1, CH - 1))
                V.tensor_scalar(H[:], H[:], keep[:, 0:1], keep[:, 1:2], ALU.min, ALU.max).then_inc(H_kept.sem, 1)

            def mixer_norm(g, t):
                dve.wait_ge(root1.sem, root1.at(g))
                if t is not None:
                    dve.wait_ge(h2T_ps.sem, h2T_ps.at(t))
                elif later(g):
                    dve.wait_ge(hT_ps.sem, hT_ps.at(g - 1))
                for c in range(CH):
                    last = V.tensor_scalar(hn[:, c, :], x_in[:, c, :], mv1[:, c, 0:1], rs12[:, c:c + 1],
                                           ALU.subtract, ALU.mult)
                last.then_inc(hn_done.sem, 1)

            def mixer_u(g):
                dve.wait_ge(root1.sem, root1.at(g))
                if later(g):
                    dve.wait_ge(out_read.sem, out_read.at(g - 1))
                for c in range(CH):
                    V.tensor_scalar(u[:, c, :], x_in[:, c, :], mv1[:, c, 0:1], rs1[:, c:c + 1],
                                    ALU.subtract, ALU.mult).then_inc(own_dve, own.one())
                dve.wait_ge(own_dve, own.n)
                dve.wait_ge(hn_done.sem, hn_done.at(g))
                dve.sem_inc(x_read.sem, 1)

            def mixer_conv(g, j):
                r = j % 2
                V.tensor_copy(xp[:, r, :, 0:TAPS - 1], halo[:, 2 * j:2 * j + 2, :]).then_inc(own_dve, own.one())
                ahead = own.n
                dve.wait_ge(pair_read.sem, pair_read.at(g, j))
                dve.wait_ge(pair_copied.sem, pair_copied.at(g, j))
                before = [ahead, ahead]
                for k in range(TAPS - 1):
                    for a in range(2):
                        t = 2 * j + a
                        dve.wait_ge(own_dve, before[a])
                        ins = V.scalar_tensor_tensor(acc[:, r, a], xp[:, r, a, k:k + TOK], cw[:, t, k:k + 1],
                                                     acc[:, r, a], ALU.mult, ALU.add)
                        if k == TAPS - 2 and a == 1:
                            ins.then_inc(conv_done.sem, 1)
                        else:
                            ins.then_inc(own_dve, own.one())
                            before[a] = own.n
                    if k == 0:
                        V.tensor_copy(halo[:, 2 * j:2 * j + 2, :], xp[:, r, :, TOK:TOK + TAPS - 1])\
                            .then_inc(own_dve, own.one())
                dve.wait_ge(own_dve, own.n)

            def mixer_scale(g, c):
                dve.wait_ge(X_sb.sem, X_sb.at(g, c))
                if c or later(g):
                    dve.wait_ge(Yn_ps.sem, Yn_ps.at(g, c - 1))
                dve.wait_ge(da_done.sem, da_done.at(g))
                V.tensor_tensor(heads3(Xdt[:]), heads3(Xt[:]), bc(dts[:, c, :], 2, HD), ALU.mult)\
                    .then_inc(own_dve, own.one())
                dve.wait_ge(own_dve, own.n)
                dve.wait_ge(ecum_done.sem, ecum_done.at(g))
                if c or later(g):
                    dve.wait_ge(S_ps.sem, S_ps.at(g, c - 1))
                V.tensor_tensor(heads3(Xw[:]), heads3(Xdt[:]), bc(ecum[:, 1, c, :], 2, HD), ALU.mult)\
                    .then_inc(Xw_done.sem, 1)

            def mixer_scores(g, c):
                for q in range(2):
                    dve.wait_ge(sc_ps.sem, sc_ps.at(g, 2 * c + q))
                    dve.wait_ge(decay_done.sem, decay_done.at(g, 2 * c + q))
                    if c or later(g):
                        dve.wait_ge(Yn_ps.sem, Yn_ps.at(g, c - 1))
                    V.tensor_tensor(sL[:, 4 * q:4 * q + 4, :], pairb[q][:].rearrange("p (h t) -> p h t", h=4),
                                    Ldec[:, 4 * q:4 * q + 4, :], ALU.mult).then_inc(sL_done.sem, 1)

            def mixer_state(g, c):
                dve.wait_ge(Yi_ps.sem, Yi_ps.at(g, c))
                if later(g):
                    dve.wait_ge(yT_ps.sem, yT_ps.at(g - 1, c))
                    dve.wait_ge(sq_done.sem, sq_done.at(g - 1, c))
                V.tensor_tensor(heads3(yv[:, c]), heads3(ring[1 - c][:]), bc(ecum[:, 0, c, :], 2, HD), ALU.mult)\
                    .then_inc(Yi_read.sem, 1)
                if c == 0:
                    dve.wait_ge(H_kept.sem, H_kept.at(g))
                else:
                    dve.wait_ge(H_done.sem, H_done.at(g, c - 1))
                V.tensor_tensor(heads3(H[:]), heads3(H[:]), bc(ecum[:, 2, c, :], 2, HD), ALU.mult)\
                    .then_inc(own_dve, own.one())
                dve.wait_ge(own_dve, own.n)
                dve.wait_ge(S_ps.sem, S_ps.at(g, c))
                V.tensor_tensor(H[:], H[:], ring[c][:], ALU.add).then_inc(H_done.sem, 1)

            def mixer_gate(g, c):
                dve.wait_ge(DX_done.sem, DX_done.at(g, c))
                dve.wait_ge(Yi_read.sem, Yi_read.at(g, c))
                V.tensor_tensor(yv[:, c], yv[:, c], DX[:], ALU.add).then_inc(own_dve, own.one())
                dve.wait_ge(own_dve, own.n)
                dve.wait_ge(Yn_ps.sem, Yn_ps.at(g, c))
                V.tensor_tensor(yv[:, c], yv[:, c], yb[:], ALU.add).then_inc(Yn_read.sem, 1)
                dve.wait_ge(Yn_read.sem, Yn_read.at(g, c))
                dve.wait_ge(z_done.sem, z_done.at(g, c))
                V.tensor_tensor(yv[:, c], yv[:, c], zs[:, c], ALU.mult).then_inc(y_done.sem, 1)

            def tail_sum(t):
                dve.wait_ge(rooty.sem, rooty.at(t))
                dve.wait_ge(out_ps.sem, out_ps.at(t, CH - 1))
                if later(t):
                    dve.wait_ge(xres_read.sem, xres_read.at(t - 1))
                for c in range(CH):
                    last = V.scalar_tensor_tensor(v[:, c, :], ring[0][:, c * D:(c + 1) * D], rsy[:, c:c + 1],
                                                  u[:, c, :], ALU.mult, ALU.add)
                last.then_inc(out_read.sem, 1)
                dve.wait_ge(out_read.sem, out_read.at(t))
                for c in range(CH):
                    V.bn_stats(sumst[:, c, :], v[:, c, :]).then_inc(own_dve, own.one())
                dve.wait_ge(own_dve, own.n)
                for c in range(CH):
                    last = V.bn_aggr(mv2[:, c, :], sumst[:, c, :])
                last.then_inc(stats3.sem, 1)

            def tail_residual(t):
                dve.wait_ge(root3.sem, root3.at(t))
                for c in range(CH):
                    V.tensor_scalar(v[:, c, :], v[:, c, :], mv2[:, c, 0:1], rs3[:, c:c + 1],
                                    ALU.subtract, ALU.mult).then_inc(own_dve, own.one())
                dve.wait_ge(own_dve, own.n)
                dve.wait_ge(xres_loaded, 16 * (t + 1))
                if later(t):
                    dve.wait_ge(x1_kept.sem, x1_kept.at(t - 1))
                V.tensor_tensor(x1[:], v[:], x_res[:], ALU.add).then_inc(xres_read.sem, 1)
                dve.wait_ge(xres_read.sem, xres_read.at(t))
                for c in range(CH):
                    V.bn_stats(resst[:, c, :], x1[:, c, :]).then_inc(own_dve, own.one())
                dve.wait_ge(own_dve, own.n)
                for c in range(CH):
                    last = V.bn_aggr(mv3[:, c, :], resst[:, c, :])
                last.then_inc(stats4.sem, 1)

            def tail_norm(t, g):
                dve.wait_ge(root4.sem, root4.at(t))
                dve.wait_ge(hT_ps.sem, hT_ps.at(t if g is None else g))
                for c in range(CH):
                    last = V.tensor_scalar(hn[:, c, :], x1[:, c, :], mv3[:, c, 0:1], rs4[:, c:c + 1],
                                           ALU.subtract, ALU.mult)
                last.then_inc(h2_done.sem, 1)

            def ffn_route(e, c):
                dve.wait_ge(sim_sb.sem, sim_sb.at(e, c))
                dve.sem_inc(arrived_dve, 1)
                for s in range(2):
                    for h in range(RH):
                        V.max(s8[:, s, h, :], sim[:, c, s, h, :]).then_inc(own_dve, own.one())
                dve.wait_ge(own_dve, own.n)
                for s in range(2):
                    for h in range(RH):
                        V.max_index(i8[:, s, h, :], s8[:, s, h, :], sim[:, c, s, h, :]).then_inc(own_dve, own.one())
                at = 0
                for first, rows, n in CAND:
                    V.tensor_tensor(cand[:, :, at:at + rows * n].rearrange("p h (r n) -> p h r n", n=n),
                                    bc(s8[:, 0, :, first:first + rows], 3, n), bc(s8[:, 1, :, 0:n], 2, rows),
                                    ALU.add).then_inc(own_dve, own.one())
                    at += rows * n
                dve.wait_ge(own_dve, own.n)
                V.tensor_copy(i8b[:], i8[:]).then_inc(own_dve, own.one())
                for h in range(RH):
                    V.max(c8[:, h, :], cand[:, h, :]).then_inc(own_dve, own.one())
                dve.wait_ge(own_dve, own.n)
                for h in range(RH):
                    V.match_replace(rest[:, h, :], c8[:, h, :], cand[:, h, :], LOWEST).then_inc(own_dve, own.one())
                if later(e):
                    dve.wait_ge(E_done.sem, E_done.at(e - 1, c * RH + RH - 1))
                V.tensor_tensor(ee[:, c, :, 0:XD], sim[:, c, 0, :, 0:XD], bc(s8[:, 0, :, 0], 2, XD),
                                ALU.subtract).then_inc(own_dve, own.one())
                V.tensor_tensor(ee[:, c, :, XD:XD + KEYS], sim[:, c, 1], bc(s8[:, 1, :, 0], 2, KEYS),
                                ALU.subtract).then_inc(own_dve, own.one())
                V.tensor_tensor(ee[:, c, :, XD + KEYS:], cand[:], bc(c8[:, :, 0], 2, NC), ALU.subtract)\
                    .then_inc(earg_done.sem, 1)
                dve.wait_ge(own_dve, own.n)
                V.tensor_tensor(chosen[:], rest[:], cand[:], ALU.not_equal).then_inc(own_dve, own.one())
                V.tensor_tensor(eq[:, :, XD:], bc(i8b[:, 1], 2, KEYS), bc(iota[:], 1, RH), ALU.is_equal)\
                    .then_inc(own_dve, own.one())
                V.tensor_tensor(eq[:, :, 0:XD], bc(i8b[:, 0], 2, XD), bc(iota[:, 0:XD], 1, RH), ALU.is_equal)\
                    .then_inc(own_dve, own.one())
                V.tensor_scalar(cmask[:], i8b[:, 0], float(XD), None, ALU.is_ge).then_inc(own_dve, own.one())
                dve.wait_ge(own_dve, own.n)
                at = 0
                with nc.allow_low_precision("counts up to 8"):
                    for first, rows, n in CAND:
                        part = chosen[:, :, at:at + rows * n].rearrange("p h (r n) -> p h r n", n=n)
                        V.tensor_reduce(n8[:, :, first:first + rows], part, AX_X, ALU.add)\
                            .then_inc(own_dve, own.one())
                        at += rows * n
                dve.wait_ge(own_dve, own.n)
                V.tensor_tensor(eq[:, :, XD:], eq[:, :, XD:], bc(bc(rank_w[:], 1, KEYS), 1, RH), ALU.mult)\
                    .then_inc(own_dve, own.one())
                V.tensor_tensor(eq[:, :, 0:XD], eq[:, :, 0:XD], bc(n8[:], 2, XD), ALU.mult)\
                    .then_inc(own_dve, own.one())
                for half in (4, 2):
                    dve.wait_ge(own_dve, own.n)
                    V.tensor_tensor(eq[:, :, :, 0:half], eq[:, :, :, 0:half], eq[:, :, :, half:2 * half], ALU.add)\
                        .then_inc(own_dve, own.one())
                dve.wait_ge(own_dve, own.n)
                if later(e):
                    dve.wait_ge(D_done.sem, D_done.at(e - 1, c * RH + RH - 1))
                V.tensor_tensor(rk[:, c], eq[:, :, :, 0], eq[:, :, :, 1], ALU.add).then_inc(ranks_done.sem, 1)

            def ffn_clamped(e, c):
                dve.wait_ge(ee_done.sem, ee_done.at(e, c))
                V.tensor_tensor(psel[:], chosen[:], ee[:, c, :, XD + KEYS:], ALU.mult).then_inc(own_dve, own.one())
                dve.wait_ge(own_dve, own.n)
                V.tensor_reduce(den[:], psel[:], AX_X, ALU.add).then_inc(own_dve, own.one())
                if later(e):
                    dve.wait_ge(Zs_done.sem, Zs_done.at(e - 1, c * RH + RH - 1))
                at = 0
                for first, rows, n in CAND:
                    V.tensor_tensor(clz[:, c, :, at:at + rows * n].rearrange("p h (r n) -> p h r n", n=n),
                                    psel[:, :, at:at + rows * n].rearrange("p h (r n) -> p h r n", n=n),
                                    bc(cmask[:, :, first:first + rows], 3, n), ALU.mult).then_inc(own_dve, own.one())
                    at += rows * n
                dve.wait_ge(own_dve, own.n)
                V.reciprocal(rden[:, c], den[:]).then_inc(own_dve, own.one())

            def ffn_experts(e, c, lo, hi):
                if lo == 0:
                    dve.wait_ge(A_ps.sem, A_ps.at(e, c))
                    V.tensor_copy(last_a[:], fA[1][:, 511:512]).then_inc(own_dve, own.one())
                    dve.wait_ge(own_dve, own.n)
                    V.scalar_tensor_tensor(clz[:, c], clz[:, c], last_a[:, 0:1], bc(rden[:, c], 2, NC),
                                           ALU.mult, ALU.mult).then_inc(clz_done.sem, 1)
                flat = [Em[:, h].rearrange("p a b -> p (a b)") for h in range(RH)]

                def mask(h):
                    dve.wait_ge(E_done.sem, E_done.at(e, c * RH + h))
                    dve.wait_ge(D_done.sem, D_done.at(e, c * RH + h))
                    V.scalar_tensor_tensor(flat[h], Dm[:, h].rearrange("p a b -> p (a b)"), float(TOP), flat[h],
                                           ALU.is_gt, ALU.mult).then_inc(P_done.sem, 1)

                for h in range(lo, hi):
                    mask(h)
                    dve.wait_ge(P_done.sem, P_done.at(e, c * RH + h))
                    V.tensor_tensor(flat[h][:, 0:512], flat[h][:, 0:512], fA[0][:], ALU.mult)\
                        .then_inc(own_dve, own.one())
                    V.tensor_tensor(flat[h][:, 512:], flat[h][:, 512:], fA[1][:], ALU.mult).then_inc(Z_done.sem, 1)

            def ffn_stats(e):
                dve.wait_ge(f_sb.sem, f_sb.at(e))
                for c in range(CH):
                    V.bn_stats(fst[:, c, :], f[:, c, :]).then_inc(own_dve, own.one())
                dve.wait_ge(own_dve, own.n)
                for c in range(CH):
                    last = V.bn_aggr(mvf[:, c, :], fst[:, c, :])
                last.then_inc(statsf.sem, 1)

            def ffn_store(e):
                dve.wait_ge(rootf.sem, rootf.at(e))
                for c in range(CH):
                    V.tensor_scalar(f[:, c, :], f[:, c, :], mvf[:, c, 0:1], rsf[:, c:c + 1],
                                    ALU.subtract, ALU.mult).then_inc(own_dve, own.one())
                dve.wait_ge(own_dve, own.n)
                dve.wait_ge(x1_kept.sem, x1_kept.at(e))
                V.tensor_tensor(f[:], f[:], x1_late[:], ALU.add).then_inc(o_done.sem, 1)

            def do_group(g, e, f, n):
                a, b, c = g is not None, e is not None, f is not None

                def conv(*js):
                    for j in js:
                        if a:
                            mixer_conv(g, j)

                if b:
                    tail_residual(e)
                conv(0)
                if b:
                    tail_norm(e, g)
                conv(1)
                if c:
                    ffn_experts(f, 1, 0, 1)
                conv(2)
                if c:
                    ffn_experts(f, 1, 1, 2)
                conv(3)
                if c:
                    ffn_experts(f, 1, 2, 3)
                conv(4)
                if c:
                    ffn_experts(f, 1, 3, RH)
                conv(5)
                if b:
                    ffn_route(e, 0)
                conv(6)
                if b:
                    ffn_clamped(e, 0)
                conv(7, 8, 9)
                if b:
                    ffn_route(e, 1)
                if a:
                    mixer_scale(g, 0)
                if c:
                    ffn_stats(f)
                if a:
                    mixer_scores(g, 0)
                    mixer_state(g, 0)
                if c:
                    ffn_store(f)
                if b:
                    ffn_clamped(e, 1)
                if a:
                    mixer_gate(g, 0)
                    mixer_scale(g, 1)
                if b:
                    ffn_experts(e, 0, 0, 2)
                if a:
                    mixer_scores(g, 1)
                    mixer_state(g, 1)
                    mixer_gate(g, 1)
                if n is not None:
                    mixer_stats(n)
                if b:
                    ffn_experts(e, 0, 2, 3)
                if n is not None:
                    mixer_norm(n, e)
                if a:
                    tail_sum(g)
                if n is not None:
                    mixer_u(n)
                if b:
                    ffn_experts(e, 0, 3, RH)
                dve.wait_ge(own_dve, own.n)
                dve.sem_clear(own_dve)
                own.restart()

            mixer_stats(0)
            mixer_norm(0, None)
            mixer_u(0)
            do_group(0, None, None, 1)
            do_group(1, 0, None, 2)
            do_group(2, 1, 0, 3)
            with dve.Fori(3, NG - 1) as g:
                do_group(g, g - 1, g - 2, g + 1)
            do_group(NG - 1, NG - 2, NG - 3, None)
            do_group(None, NG - 1, NG - 2, None)
            do_group(None, None, NG - 1, None)

        @block.tensor
        def _(pe):
            mm = nc.tensor.matmul
            pe.wait_ge(consts, 1)
            pe.wait_ge(loaded_c, 16 * 9)
            for k in range(DK):
                for s in range(2 * RH):
                    last = mm(ring[k][:, s * KEYS:(s + 1) * KEYS], hid[0:64, s, k * P:(k + 1) * P],
                              xbcT[0:64, 0:2, :].rearrange("p a (b k) -> p (a b) k", k=KEYS)[:, s, :],
                              start=True, stop=True)
                last.then_inc(simw_ps, 1)
            pe.wait_ge(simw_sb, 1)
            pe.wait_ge(folded, 1)
            pe.wait_ge(loaded_w, 16 * 6)

            def mixer_hT(g):
                pe.wait_ge(hn_done.sem, hn_done.at(g))
                if later(g):
                    pe.wait_ge(Yn_read.sem, Yn_read.at(g - 1, CH - 1))
                for c in range(CH):
                    for k in range(DK):
                        last = nc.tensor.transpose(yb[:, k * TOK + c * P:k * TOK + (c + 1) * P],
                                                   hn[:, c, k * P:(k + 1) * P], ident[:])
                last.then_inc(hT_ps.sem, 1)

            def mixer_dt(g):
                pe.wait_ge(hT_sb.sem, hT_sb.at(g))
                if later(g):
                    pe.wait_ge(yT_sb.sem, yT_sb.at(g - 1, 1))
                for c in range(CH):
                    for k in range(DK):
                        last = mm(ring[1][:, c * HEADS:(c + 1) * HEADS], hT[:, k, c * P:(c + 1) * P],
                                  w_in[:, k, INNER + XBC:], start=k == 0, stop=k == DK - 1)
                last.then_inc(dt_ps.sem, 1)

            def mixer_pair(g, j):
                if j == 0:
                    if later(g):
                        pe.wait_ge(out_read.sem, out_read.at(g - 1))
                elif j == 1:
                    pe.wait_ge(dt_sb.sem, dt_sb.at(g))
                elif j in (4, 5):
                    pe.wait_ge(z_done.sem, z_done.at(g, j - 4))
                else:
                    pe.wait_ge(pair_read.sem, pair_read.at(g, j - 2))
                for a in range(2):
                    at = INNER + (2 * j + a) * P
                    for k in range(DK):
                        last = mm(ring[j % 2][:, a * TOK:(a + 1) * TOK], w_in[:, k, at:at + P], hT[:, k, :],
                                  start=k == 0, stop=k == DK - 1)
                last.then_inc(pair_ps.sem, 1)

            def mixer_cum(g, e):
                pe.wait_ge(da_done.sem, da_done.at(g))
                if e is not None:
                    pe.wait_ge(up_done.sem, up_done.at(e, 1))
                n = CH * HEADS
                mm(yb[:, 0:n], tri[:], da[:].rearrange("p c h -> p (c h)"), start=True, stop=True)
                mm(yb[:, n:2 * n], ones[:], da[:].rearrange("p c h -> p (c h)"), start=True, stop=True)\
                    .then_inc(cum_ps.sem, 1)

            def mixer_z(g, c):
                pe.wait_ge(pair_read.sem, pair_read.at(g, 2 + c))
                for k in range(DK):
                    last = mm(ring[c][:], hT[:, k, c * P:(c + 1) * P], w_in[:, k, 0:INNER],
                              start=k == 0, stop=k == DK - 1)
                last.then_inc(z_ps.sem, 1)

            def mixer_rows(g, c, f):
                for q in range(2):
                    if c == 0 and f is not None:
                        pe.wait_ge(WT_sb.sem, WT_sb.at(f, CH + q))
                    elif c or later(g):
                        pe.wait_ge(sL_done.sem, sL_done.at(g, 2 * (c - 1) + q))
                    mm(pairb[q][:], ident_b[:], mask_b[:].rearrange("p h t -> p (h t)"), start=True, stop=False)
                    for i in range(4):
                        h = 4 * q + i
                        last = mm(pairb[q][:, i * P:(i + 1) * P], da[:, c, h:h + 1].to_broadcast([P, P]), tri[:],
                                  start=False, stop=i == 3)
                    last.then_inc(rows_ps.sem, 1)

            def mixer_X(g, c):
                pe.wait_ge(silu_done.sem, silu_done.at(g, XP - 1))
                if c == 0:
                    pe.wait_ge(pair_read.sem, pair_read.at(g, PAIRS - 2))
                else:
                    pe.wait_ge(Yi_read.sem, Yi_read.at(g, 0))
                for i in range(INNER // P):
                    last = nc.tensor.transpose(ring[c][:, i * P:(i + 1) * P],
                                               xbcT[:, i, c * P:(c + 1) * P], ident[:])
                last.then_inc(X_ps.sem, 1)

            def mixer_B(g, c):
                pe.wait_ge(silu_done.sem, silu_done.at(g, XP + BP - 1))
                for q in range(2):
                    pe.wait_ge(decay_done.sem, decay_done.at(g, 2 * c + q))
                    for i in range(4):
                        last = nc.tensor.transpose(pairb[q][:, i * P:(i + 1) * P],
                                                   xbcT[:, INNER // P + 4 * q + i, c * P:(c + 1) * P], ident[:])
                    last.then_inc(Bt_ps.sem, 1)

            def mixer_Yi(g, c):
                pe.wait_ge(silu_done.sem, silu_done.at(g, PAIRS - 1))
                if c == 0:
                    pe.wait_ge(H_kept.sem, H_kept.at(g))
                    pe.wait_ge(pair_read.sem, pair_read.at(g, PAIRS - 1))
                else:
                    pe.wait_ge(H_done.sem, H_done.at(g, c - 1))
                for h in range(HEADS):
                    last = mm(ring[1 - c][:, h * HD:(h + 1) * HD],
                              xbcT[:, INNER // P + HEADS + h, c * P:(c + 1) * P], H[:, h * HD:(h + 1) * HD],
                              start=True, stop=True)
                last.then_inc(Yi_ps.sem, 1)

            def mixer_scores(g, c):
                for q in range(2):
                    pe.wait_ge(Bt_sb.sem, Bt_sb.at(g, 2 * c + q))
                    for i in range(4):
                        h = 4 * q + i
                        last = mm(pairb[q][:, i * P:(i + 1) * P], xbcT[:, INNER // P + h, c * P:(c + 1) * P],
                                  xbcT[:, INNER // P + HEADS + h, c * P:(c + 1) * P], start=True, stop=True)
                    last.then_inc(sc_ps.sem, 1)

            def mixer_S(g, c):
                pe.wait_ge(Xw_done.sem, Xw_done.at(g, c))
                pe.wait_ge(X_sb.sem, X_sb.at(g, c))
                for h in range(HEADS):
                    last = mm(ring[c][:, h * HD:(h + 1) * HD], Btok[:, h, :], Xw[:, h * HD:(h + 1) * HD],
                              start=True, stop=True)
                last.then_inc(S_ps.sem, 1)

            def mixer_Yn(g, c, e):
                if c:
                    pe.wait_ge(Yn_read.sem, Yn_read.at(g, c - 1))
                elif e is not None:
                    pe.wait_ge(up_done.sem, up_done.at(e, FT // 2 - 1))
                else:
                    pe.wait_ge(cum_sb.sem, cum_sb.at(g))
                pe.wait_ge(sL_done.sem, sL_done.at(g, 2 * c + 1))
                for h in range(HEADS):
                    last = mm(yb[:, h * HD:(h + 1) * HD], sL[:, h, :], Xdt[:, h * HD:(h + 1) * HD],
                              start=True, stop=True)
                last.then_inc(Yn_ps.sem, 1)

            def mixer_yT(g, c):
                pe.wait_ge(y_done.sem, y_done.at(g, c))
                if c == 0:
                    pe.wait_ge(Yi_read.sem, Yi_read.at(g, CH - 1))
                else:
                    pe.wait_ge(H_done.sem, H_done.at(g, CH - 1))
                for i in range(INNER // P):
                    last = nc.tensor.transpose(ring[c][:, i * P:(i + 1) * P], yv[:, c, i * P:(i + 1) * P],
                                               ident[:])
                last.then_inc(yT_ps.sem, 1)

            def mixer_out(g, c):
                pe.wait_ge(yT_sb.sem, yT_sb.at(g, c))
                for i in range(INNER // P):
                    last = mm(ring[0][:, c * D:(c + 1) * D], yT[:, i * P:(i + 1) * P], w_out[:, i, :],
                              start=i == 0, stop=i == INNER // P - 1)
                last.then_inc(out_ps.sem, 1)

            def tail_h2T(t, g):
                pe.wait_ge(h2_done.sem, h2_done.at(t))
                if g is not None:
                    pe.wait_ge(hT_sb.sem, hT_sb.at(g))
                else:
                    pe.wait_ge(Yn_read.sem, Yn_read.at(t, CH - 1))
                for c in range(CH):
                    for k in range(DK):
                        last = nc.tensor.transpose(yb[:, k * TOK + c * P:k * TOK + (c + 1) * P],
                                                   hn[:, c, k * P:(k + 1) * P], ident[:])
                last.then_inc(h2T_ps.sem, 1)

            def ffn_sim(e, c):
                if c == 0:
                    pe.wait_ge(h2T_sb.sem, h2T_sb.at(e))
                else:
                    pe.wait_ge(sim_sb.sem, sim_sb.at(e, 0))
                for k in range(DK):
                    last = mm(yb[:], h2T[:, k, c * P:(c + 1) * P], w_sim[:, k, :], start=k == 0, stop=k == DK - 1)
                last.then_inc(sim_ps.sem, 1)

            def ffn_A(e, c):
                if c or later(e):
                    pe.wait_ge(Z_done.sem, Z_done.at(e, c * RH - 1))
                for q in range(2):
                    for k in range(DK):
                        last = mm(fA[q][:], h2T[:, k, c * P:(c + 1) * P], w_de[:, k, q * 512:(q + 1) * 512],
                                  start=k == 0, stop=k == DK - 1)
                last.then_inc(A_ps.sem, 1)

            def ffn_up(e, j, g=None):
                if j == 0:
                    pe.wait_ge(sim_sb.sem, sim_sb.at(e, 1))
                elif g is not None:
                    pe.wait_ge(cum_sb.sem, cum_sb.at(g))
                else:
                    pe.wait_ge(up_done.sem, up_done.at(e, j - 1))
                for a in range(2):
                    for k in range(DK):
                        last = mm(yb[:, a * TOK:(a + 1) * TOK], w_up[:, k, (2 * j + a) * P:(2 * j + a + 1) * P],
                                  h2T[:, k, :], start=k == 0, stop=k == DK - 1)
                last.then_inc(up_ps.sem, 1)

            def ffn_WT(e, c, g):
                pe.wait_ge(W_done.sem, W_done.at(e, c))
                for q in range(2):
                    if c:
                        pe.wait_ge(WT_sb.sem, WT_sb.at(e, q))
                    else:
                        pe.wait_ge(sL_done.sem, sL_done.at(g, 2 * (CH - 1) + q))
                    for i in range(4):
                        last = nc.tensor.transpose(pairb[q][:, i * P:(i + 1) * P],
                                                   W[:, (4 * q + i) * P:(4 * q + i + 1) * P], ident[:])
                    last.then_inc(WT_ps.sem, 1)

            def ffn_down(e, c):
                if c == 0:
                    pe.wait_ge(up_done.sem, up_done.at(e, FT // 2 - 1))
                    if later(e):
                        pe.wait_ge(f_sb.sem, f_sb.at(e - 1))
                    mm(f0[:], zero_b[:], mask_b[:].rearrange("p h t -> p (h t)"), start=True, stop=False)
                for i in range(FT):
                    last = mm(f0[:, c * D:(c + 1) * D], hid[:, i, c * P:(c + 1) * P], w_down[:, i, :],
                              start=False, stop=False)
                last.then_inc(down_ps.sem, 1)

            def ffn_out(e, c):
                for q in range(2):
                    pe.wait_ge(WT_sb.sem, WT_sb.at(e, 2 * c + q))
                    for i in range(4):
                        last = mm(f0[:, c * D:(c + 1) * D], WT[:, 4 * q + i, :], w_ue[:, 4 * q + i, :], start=False,
                                  stop=c == CH - 1 and q == 1 and i == 3)
                last.then_inc(out_part.sem if c == 0 else f_ps.sem, 1)

            def do_group(g, e, f, n):
                a, b, c = g is not None, e is not None, f is not None

                def pairs(*js):
                    for j in js:
                        if a:
                            mixer_pair(g, j)

                if a:
                    mixer_dt(g)
                pairs(0, 1)
                if c:
                    ffn_A(f, 1)
                    ffn_WT(f, 0, f if e is None else e)
                    ffn_out(f, 0)
                if b:
                    tail_h2T(e, g)
                pairs(2)
                if b:
                    ffn_sim(e, 0)
                pairs(3)
                if a:
                    mixer_z(g, 0)
                if b:
                    ffn_sim(e, 1)
                if a:
                    mixer_z(g, 1)
                pairs(4, 5, 6)
                if b:
                    ffn_up(e, 0)
                pairs(7)
                if b:
                    ffn_up(e, 1)
                if a:
                    mixer_cum(g, e)
                pairs(8)
                if b:
                    ffn_up(e, 2, g)
                pairs(9)
                if b:
                    ffn_up(e, 3)
                if a:
                    mixer_X(g, 0)
                if c:
                    ffn_WT(f, 1, None)
                if a:
                    mixer_rows(g, 0, f)
                if c:
                    ffn_out(f, 1)
                if a:
                    mixer_B(g, 0)
                    mixer_Yi(g, 0)
                    mixer_scores(g, 0)
                if b:
                    ffn_A(e, 0)
                if a:
                    mixer_S(g, 0)
                    mixer_Yn(g, 0, e)
                    mixer_X(g, 1)
                    mixer_rows(g, 1, f)
                if b:
                    ffn_down(e, 0)
                if a:
                    mixer_B(g, 1)
                    mixer_Yi(g, 1)
                    mixer_scores(g, 1)
                    mixer_S(g, 1)
                    mixer_yT(g, 0)
                    mixer_Yn(g, 1, e)
                if a:
                    mixer_out(g, 0)
                    mixer_yT(g, 1)
                    mixer_out(g, 1)
                if n is not None:
                    mixer_hT(n)
                if b:
                    ffn_down(e, 1)

            mixer_hT(0)
            do_group(0, None, None, 1)
            do_group(1, 0, None, 2)
            do_group(2, 1, 0, 3)
            with pe.Fori(3, NG - 1) as g:
                do_group(g, g - 1, g - 2, g + 1)
            do_group(NG - 1, NG - 2, NG - 3, None)
            do_group(None, NG - 1, NG - 2, None)
            do_group(None, None, NG - 1, None)


def layouts(i):
    import numpy as np

    def tiles(wT):
        return np.ascontiguousarray(wT.reshape(-1, P, wT.shape[1]).transpose(1, 0, 2))

    def every(a):
        return np.ascontiguousarray(np.broadcast_to(a, (P, a.shape[0])))

    i = {k.replace("L0_", ""): np.asarray(a) for k, a in i.items()}
    return dict(
        x=i["attn_x"].reshape(-1, D),
        in_wT=tiles(i["attn_in_proj_w"].T),
        norm_w=np.ascontiguousarray(i["attn_norm_w"].reshape(DK, P).T),
        conv_w=np.ascontiguousarray(i["attn_conv_w"].reshape(TILES, P, TAPS).transpose(1, 0, 2)),
        conv_b=np.ascontiguousarray(i["attn_conv_b"].reshape(TILES, P).T),
        dt_bias=every(i["attn_dt_bias"]),
        A_log=every(i["attn_A_log"]),
        D_skip=every(i["attn_D_skip"]),
        gnorm_w=np.ascontiguousarray(i["attn_gnorm_w"].reshape(INNER // P, P).T),
        out_wT=tiles(i["attn_out_proj_w"].T),
        upT=tiles(i["ffn_W_up"].T),
        downT=tiles(i["ffn_W_down"].T),
        wq=np.ascontiguousarray(i["ffn_W_q"].reshape(2 * RH, 64, D).transpose(1, 0, 2)),
        keysT=np.ascontiguousarray(i["ffn_keys"].transpose(3, 2, 0, 1).reshape(64, 2, TOK)),
        down_eT=tiles(i["ffn_down_embed"].T),
        up_e=tiles(i["ffn_up_embed"]),
    )


def kernel(**inputs):
    import numpy as np
    import concourse.bacc as bacc
    from concourse.bass_utils import run_bass_kernel_spmd

    nc = bacc.Bacc("TRN2", target_bir_lowering=False, num_devices=1)
    arrays = layouts(inputs)
    args = {n: nc.dram_tensor(f"{n}_dram", a.shape, mybir.dt.from_np(a.dtype), kind="ExternalInput").ap()
            for n, a in arrays.items()}
    out = nc.dram_tensor("out_dram", arrays["x"].shape, F32, kind="ExternalOutput").ap()
    sandwich(nc, out=out, **args)
    r = run_bass_kernel_spmd(nc, [{f"{n}_dram": a for n, a in arrays.items()}], core_ids=[0])
    shape = np.shape(inputs["L0_attn_x"])
    return np.asarray(r.results[0]["out_dram"]).reshape(shape)
```

```python
from contextlib import ExitStack

import concourse.bass as bass
from concourse import mybir

P = 128
ALU = mybir.AluOpType
ACT = mybir.ActivationFunctionType
BF16 = mybir.dt.bfloat16
F32 = mybir.dt.float32
U32 = mybir.dt.uint32
AX_X = mybir.AxisListType.X

D = 256
DK = D // P
HEADS = 8
HD = 64
G = 128
INNER = HEADS * HD
XBC = INNER + 2 * HEADS * G
PROJ = INNER + XBC + HEADS
TAPS = 4
CHUNK = 128
CH = 2
TOK = CH * CHUNK
TILES = XBC // P
PAIRS = TILES // 2
XP, BP = INNER // TOK, HEADS // 2
FF = 1024
FT = FF // P
EXPERTS = 1024
ET = EXPERTS // P
RH = 4
KEYS = 64
XD = EXPERTS // KEYS
TOP = 8
CAND = [(0, 1, 8), (1, 1, 4), (2, 2, 2), (4, 4, 1)]
NC = sum(r * n for _, r, n in CAND)
EPS = 1e-5
LOWEST = -3.0e38
MASKED = -1.0e30
FLT_MAX = 3.4028234e38


class Sig:

    def __init__(self, sem, per=1):
        self.sem, self.per = sem, per

    def at(self, group, k=0):
        return group * self.per + k + 1


def later(group):
    return not (isinstance(group, int) and group == 0)


class Steps:

    def __init__(self):
        self.n = 0

    def one(self):
        self.n += 1
        return 1

    def restart(self):
        self.n = 0


def sandwich(nc, x, in_wT, norm_w, conv_w, conv_b, dt_bias, A_log, D_skip, gnorm_w, out_wT,
             upT, downT, wq, keysT, down_eT, up_e, out):
    NG = x.shape[0] // TOK
    SEQ = 1024 // TOK
    xv = x.rearrange("(g c p) d -> g p c d", c=CH, p=P)
    ov = out.rearrange("(g c p) d -> g p c d", c=CH, p=P)

    with ExitStack() as ctx:
        def sb(name, shape, dt=F32):
            return ctx.enter_context(nc.sbuf_tensor(name, shape, dt))

        def sem(name):
            return ctx.enter_context(nc.semaphore(name))

        def sig(name, per=1):
            return Sig(sem(name), per)

        w_in = sb("w_in", [P, DK, PROJ])
        w_out = sb("w_out", [P, INNER // P, D])
        w_up = sb("w_up", [P, DK, FF])
        w_down = sb("w_down", [P, FT, D])
        w_de = sb("w_de", [P, DK, EXPERTS])
        w_ue = sb("w_ue", [P, ET, D])
        w_sim = sb("w_sim", [P, DK, 2 * RH * KEYS])
        cw = sb("cw", [P, TILES, TAPS])
        cb = sb("cb", [P, TILES])
        nw = sb("nw", [P, DK])
        gw = sb("gw", [P, INNER // P])
        head_c = sb("head_c", [P, 3, HEADS])
        neg_a = sb("neg_a", [P, HEADS])
        tri = sb("tri", [P, P])
        ones = sb("ones", [P, P])
        ident = sb("ident", [P, P])
        ident_b = sb("ident_b", [P, P], BF16)
        zero_b = sb("zero_b", [P, P], BF16)
        mask_b = sb("mask_b", [P, 4, P], BF16)
        iota = sb("iota", [P, KEYS, TOP], BF16)
        rank_w = sb("rank_w", [P, TOP], BF16)
        keep_tab = sb("keep_tab", [P, 2, NG])
        half_neg = sb("half_neg", [P, 2 * CH])

        x_in = sb("x_in", [P, CH, D])
        x_res = sb("x_res", [P, CH, D])
        u = sb("u", [P, CH, D])
        hn = sb("hn", [P, CH, D])
        hT = sb("hT", [P, DK, TOK])
        xp = sb("xp", [P, 2, 2, TAPS - 1 + TOK])
        acc = sb("acc", [P, 2, 2, TOK])
        halo = sb("halo", [P, TILES, TAPS - 1])
        xbcT = sb("xbcT", [P, TILES, TOK])
        keep = sb("keep", [P, 2])
        dtp = sb("dtp", [P, CH, HEADS])
        dt0 = sb("dt0", [P, CH, HEADS])
        dt1 = sb("dt1", [P, CH, HEADS])
        dt2 = sb("dt2", [P, CH, HEADS])
        dte = sb("dte", [P, CH, HEADS])
        dte2 = sb("dte2", [P, CH, HEADS])
        dta = sb("dta", [P, CH, HEADS])
        minus1 = sb("minus1", [P, CH, HEADS])
        dts = sb("dts", [P, CH, HEADS])
        da = sb("da", [P, CH, HEADS])
        cum = sb("cum", [P, 3, CH, HEADS])
        ecum = sb("ecum", [P, 3, CH, HEADS])
        ncum = sb("ncum", [P, CH, HEADS])
        lnst = sb("lnst", [P, CH, 6])
        mv1 = sb("mv1", [P, CH, 2])
        mv2 = sb("mv2", [P, CH, 2])
        mv3 = sb("mv3", [P, CH, 2])
        rs12 = sb("rs12", [P, 2 * CH])
        shift12 = sb("shift12", [P, 2 * CH])
        neg_mean = sb("neg_mean", [P, CH])
        neg_mean4 = sb("neg_mean4", [P, CH])
        shift4 = sb("shift4", [P, CH])
        ve = sb("ve", [P, 2 * CH])
        ve3 = sb("ve3", [P, CH])
        ve4 = sb("ve4", [P, CH])
        vey = sb("vey", [P, CH])
        sumst = sb("sumst", [P, CH, 6])
        resst = sb("resst", [P, CH, 6])
        rsy = sb("rsy", [P, CH])
        rs3 = sb("rs3", [P, CH])
        rs4 = sb("rs4", [P, CH])
        Xt = sb("Xt", [P, INNER])
        Xdt = sb("Xdt", [P, INNER])
        Xw = sb("Xw", [P, INNER])
        DX = sb("DX", [P, INNER])
        Btok = sb("Btok", [P, HEADS, G])
        Ldec = sb("Ldec", [P, HEADS, CHUNK])
        sL = sb("sL", [P, HEADS, CHUNK])
        H = sb("H", [P, INNER])
        zs = sb("zs", [P, CH, INNER])
        yv = sb("yv", [P, CH, INNER])
        ssq = sb("ssq", [P, CH])
        yT = sb("yT", [P, INNER])
        v = sb("v", [P, CH, D])
        x1 = sb("x1", [P, CH, D])
        x1_late = sb("x1_late", [P, CH, D])
        h2T = sb("h2T", [P, DK, TOK])

        hid = sb("hid", [P, FT, TOK])
        sim = sb("sim", [P, CH, 2, RH, KEYS])
        s8 = sb("s8", [P, 2, RH, TOP])
        i8 = sb("i8", [P, 2, RH, TOP], U32)
        i8b = sb("i8b", [P, 2, RH, TOP], BF16)
        cand = sb("cand", [P, RH, NC])
        c8 = sb("c8", [P, RH, TOP])
        rest = sb("rest", [P, RH, NC])
        chosen = sb("chosen", [P, RH, NC])
        n8 = sb("n8", [P, RH, TOP], BF16)
        ee = sb("ee", [P, CH, RH, XD + KEYS + NC])
        psel = sb("psel", [P, RH, NC])
        den = sb("den", [P, RH])
        rden = sb("rden", [P, CH, RH])
        cmask = sb("cmask", [P, RH, TOP])
        clz = sb("clz", [P, CH, RH, NC])
        cls = sb("cls", [P, RH, NC])
        clsum = sb("clsum", [P, CH])
        last_a = sb("last_a", [P, 1])
        eq = sb("eq", [P, RH, XD + KEYS, TOP], BF16)
        rk = sb("rk", [P, CH, RH, XD + KEYS], BF16)
        Dm = sb("Dm", [P, RH, XD, KEYS], BF16)
        Em = sb("Em", [P, RH, XD, KEYS])
        W = sb("W", [P, EXPERTS])
        WT = sb("WT", [P, ET, P])
        f = sb("f", [P, CH, D])
        fst = sb("fst", [P, CH, 6])
        mvf = sb("mvf", [P, CH, 2])
        vf = sb("vf", [P, CH])
        rsf = sb("rsf", [P, CH])

        banks = [ctx.enter_context(nc.psum_tensor(f"bank{i}", [P, 512], F32)) for i in range(6)]
        ring, pairb, yb, f0 = banks[0:2], banks[2:4], banks[4], banks[5]
        fA = ctx.enter_context(nc.psum_tensor("products", [P, EXPERTS], F32))

        loaded_c = sem("loaded_c")
        loaded_in, loaded_out, loaded_w = sem("loaded_in"), sem("loaded_out"), sem("loaded_w")
        consts = sem("consts")
        folded = sem("folded")
        simw_ps, simw_sb = sem("simw_ps"), sem("simw_sb")
        x_loaded, xres_loaded = sem("x_loaded"), sem("xres_loaded")
        x_read = sig("x_read")
        stored = sem("stored")
        own_dve, own_act, own_pool = sem("own_dve"), sem("own_act"), sem("own_pool")
        arrived_dve, arrived_act, arrived_pool = sem("arrived_dve"), sem("arrived_act"), sem("arrived_pool")
        stats1, root1, u_done = sig("stats1"), sig("root1"), sig("u_done")
        hn_done, hT_ps, hT_sb = sig("hn_done"), sig("hT_ps"), sig("hT_sb")
        dt_ps, dt_sb, dt_abs, dte_done, da_done = (sig(n) for n in ("dt_ps", "dt_sb", "dt_abs", "dte_done", "da_done"))
        cum_ps, cum_sb, cum_diff, ecum_done = (sig(n) for n in ("cum_ps", "cum_sb", "cum_diff", "ecum_done"))
        pair_ps, pair_copied, pair_read = sig("pair_ps", PAIRS), sig("pair_copied", PAIRS), sig("pair_read", PAIRS)
        ahead_done, halo_taken, halo_kept = sig("ahead_done", PAIRS), sig("halo_taken", PAIRS), sig("halo_kept")
        conv_done, silu_done = sig("conv_done", TILES), sig("silu_done", PAIRS)
        rows_ps, decay_done = sig("rows_ps", 2 * CH), sig("decay_done", 2 * CH)
        X_ps, X_sb, z_ps, z_done = sig("X_ps", CH), sig("X_sb", CH), sig("z_ps", CH), sig("z_done", CH)
        Bt_ps, Bt_sb = sig("Bt_ps", 2 * CH), sig("Bt_sb", 2 * CH)
        sc_ps, sL_done = sig("sc_ps", 2 * CH), sig("sL_done", 2 * CH)
        Yi_ps, Yi_read = sig("Yi_ps", CH), sig("Yi_read", CH)
        Xdt_done, Xw_done, DX_done = sig("Xdt_done", CH), sig("Xw_done", CH), sig("DX_done", CH)
        S_ps, H_scaled, H_done, H_kept = sig("S_ps", CH), sig("H_scaled", CH), sig("H_done", CH), sig("H_kept")
        bounds_done = sig("bounds_done")
        Yn_ps, Yn_read = sig("Yn_ps", CH), sig("Yn_read", CH)
        y_done, sq_done = sig("y_done", CH), sig("sq_done", CH)
        yT_ps, yT_sb = sig("yT_ps", CH), sig("yT_sb", CH)
        rooty, out_ps, out_read = sig("rooty"), sig("out_ps", CH), sig("out_read")
        stats3, root3, stats4, root4 = sig("stats3"), sig("root3"), sig("stats4"), sig("root4")
        h2_done, h2T_ps, h2T_sb, xres_read = sig("h2_done"), sig("h2T_ps"), sig("h2T_sb"), sig("xres_read")
        sim_ps, sim_sb = sig("sim_ps", CH), sig("sim_sb", CH)
        A_ps = sig("A_ps", CH)
        up_ps, up_done = sig("up_ps", FT // 2), sig("up_done", FT // 2)
        earg_done, ee_done, ranks_done = sig("earg_done", CH), sig("ee_done", CH), sig("ranks_done", CH)
        D_done, E_done, P_done, Zs_done = (
            sig(n, CH * RH) for n in ("D_done", "E_done", "P_done", "Zs_done"))
        Z_done = sig("Z_done", CH * RH)
        clz_done, cls_done = sig("clz_done", CH), sig("cls_done", CH)
        W_part, W_done = sig("W_part", CH * (RH - 1)), sig("W_done", CH)
        WT_ps, WT_sb = sig("WT_ps", 2 * CH), sig("WT_sb", 2 * CH)
        out_part, f_ps, f_sb, x1_kept = sig("out_part"), sig("f_ps"), sig("f_sb"), sig("x1_kept")
        down_ps = sig("down_ps", CH)
        statsf, rootf, o_done = sig("statsf"), sig("rootf"), sig("o_done")

        block = ctx.enter_context(nc.Block())

        def bc(ap, axis, n):
            return ap.unsqueeze(axis).to_broadcast([*ap.shape[:axis], n, *ap.shape[axis:]])

        def heads3(ap):
            return ap.rearrange("p (h d) -> p h d", h=HEADS)

        @block.sync
        def _(sp):
            sp.dma_start(x_in[:], xv[0]).then_inc(x_loaded, 16)
            sp.dma_start(nw[:], norm_w).then_inc(loaded_c, 16)
            sp.dma_start(gw[:], gnorm_w).then_inc(loaded_c, 16)
            sp.dma_start(cw[:], conv_w).then_inc(loaded_c, 16)
            sp.dma_start(cb[:], conv_b).then_inc(loaded_c, 16)
            sp.dma_start(head_c[:, 0, :], dt_bias).then_inc(loaded_c, 16)
            sp.dma_start(head_c[:, 1, :], A_log).then_inc(loaded_c, 16)
            sp.dma_start(head_c[:, 2, :], D_skip).then_inc(loaded_c, 16)
            sp.dma_start(hid[0:64, :, :], wq).then_inc(loaded_c, 16)
            sp.dma_start(xbcT[0:64, 0:2, :], keysT).then_inc(loaded_c, 16)
            sp.dma_start(w_in[:], in_wT).then_inc(loaded_in, 16)
            sp.dma_start(w_out[:], out_wT).then_inc(loaded_out, 16)
            sp.dma_start(w_up[:], upT).then_inc(loaded_w, 16)
            sp.dma_start(w_de[:], down_eT).then_inc(loaded_w, 16)
            sp.dma_start(w_down[:], downT).then_inc(loaded_w, 16)
            sp.dma_start(w_ue[:], up_e).then_inc(loaded_w, 16)

            def rows_of(g, more):
                if later(g):
                    sp.wait_ge(xres_read.sem, xres_read.at(g - 1))
                sp.dma_start(x_res[:], xv[g]).then_inc(xres_loaded, 16)
                if more:
                    sp.wait_ge(x_read.sem, x_read.at(g))
                    sp.dma_start(x_in[:], xv[g + 1]).then_inc(x_loaded, 16)

            def store(e):
                sp.wait_ge(o_done.sem, o_done.at(e))
                sp.dma_start(ov[e], f[:]).then_inc(stored, 16)

            rows_of(0, True)
            rows_of(1, True)
            store(0)
            with sp.Fori(2, NG - 1) as g:
                rows_of(g, True)
                store(g - 1)
            rows_of(NG - 1, False)
            store(NG - 2)
            store(NG - 1)
            sp.wait_ge(stored, 16 * NG)

        @block.gpsimd
        def _(pool):
            own = Steps()
            nc.gpsimd.memset(tri[:], 1.0).then_inc(own_pool, own.one())
            nc.gpsimd.memset(ones[:], 1.0).then_inc(own_pool, own.one())
            nc.gpsimd.memset(ident[:], 0.0).then_inc(own_pool, own.one())
            nc.gpsimd.memset(mask_b[:], 0.0).then_inc(own_pool, own.one())
            nc.gpsimd.memset(zero_b[:], 0.0).then_inc(own_pool, own.one())
            nc.gpsimd.memset(halo[:], 0.0).then_inc(own_pool, own.one())
            nc.gpsimd.memset(H[:], 0.0).then_inc(own_pool, own.one())
            nc.gpsimd.memset(minus1[:], -1.0).then_inc(own_pool, own.one())
            nc.gpsimd.memset(half_neg[:], -0.5).then_inc(own_pool, own.one())
            nc.gpsimd.memset(keep_tab[:, 0], FLT_MAX).then_inc(own_pool, own.one())
            nc.gpsimd.memset(keep_tab[:, 1], -FLT_MAX).then_inc(own_pool, own.one())
            for r in range(TOP):
                nc.gpsimd.memset(rank_w[:, r:r + 1], float(TOP - r)).then_inc(own_pool, own.one())
            nc.gpsimd.iota(iota[:], pattern=[[1, KEYS], [0, TOP]], base=0, channel_multiplier=0,
                           allow_small_or_imprecise_dtypes=True).then_inc(own_pool, own.one())
            pool.wait_ge(own_pool, own.n)
            nc.gpsimd.memset(keep_tab[:, :, 0:NG:SEQ], 0.0).then_inc(own_pool, own.one())
            nc.gpsimd.affine_select(out=tri[:], in_=tri[:], compare_op=ALU.is_ge, fill=0.0,
                                   base=0, pattern=[[1, P]], channel_multiplier=-1)\
                .then_inc(own_pool, own.one())
            nc.gpsimd.affine_select(out=mask_b[:], in_=mask_b[:], compare_op=ALU.is_ge, fill=MASKED,
                                   base=0, pattern=[[0, 4], [1, P]], channel_multiplier=-1)\
                .then_inc(own_pool, own.one())
            nc.gpsimd.affine_select(out=ident[:], in_=ident[:], compare_op=ALU.not_equal, fill=1.0,
                                   base=0, pattern=[[-1, P]], channel_multiplier=1)\
                .then_inc(own_pool, own.one())
            pool.wait_ge(own_pool, own.n)
            nc.gpsimd.tensor_copy(ident_b[:], ident[:]).then_inc(consts, 1)
            pool.wait_ge(own_pool, own.n)
            pool.sem_clear(own_pool)
            own.restart()

            def mixer_norm(g):
                pool.wait_ge(stats1.sem, stats1.at(g))
                pool.sem_inc(arrived_pool, 1)
                nc.gpsimd.tensor_scalar(ve[:, 0:CH], mv1[:, :, 1], EPS, None, ALU.add).then_inc(own_pool, own.one())
                nc.gpsimd.tensor_scalar(ve[:, CH:], mv1[:, :, 1], 1.0 + EPS, EPS * EPS, ALU.mult, ALU.add)\
                    .then_inc(own_pool, own.one())
                pool.wait_ge(own_pool, own.n)
                if later(g):
                    pool.wait_ge(hn_done.sem, hn_done.at(g - 1))
                    pool.wait_ge(u_done.sem, u_done.at(g - 1))
                nc.gpsimd.tensor_tensor(rs12[:], ve[:], half_neg[:], ALU.pow).then_inc(own_pool, own.one())
                pool.sem_inc(arrived_pool, 1)
                nc.gpsimd.tensor_scalar(neg_mean[:], mv1[:, :, 0], -1.0, None, ALU.mult).then_inc(own_pool, own.one())
                pool.wait_ge(own_pool, own.n)
                nc.gpsimd.tensor_tensor(shift12[:].rearrange("p (n c) -> p n c", n=2),
                                        rs12[:].rearrange("p (n c) -> p n c", n=2), bc(neg_mean[:], 1, 2), ALU.mult)\
                    .then_inc(root1.sem, 1)

            def mixer_dt_abs(g):
                pool.wait_ge(dt_sb.sem, dt_sb.at(g))
                nc.gpsimd.tensor_tensor(dt0[:], dtp[:], bc(head_c[:, 0, :], 1, CH), ALU.add)\
                    .then_inc(own_pool, own.one())
                pool.wait_ge(own_pool, own.n)
                nc.gpsimd.tensor_scalar(dt2[:], dt0[:], 0.0, 2.0, ALU.max, ALU.mult).then_inc(own_pool, own.one())
                pool.wait_ge(own_pool, own.n)
                nc.gpsimd.tensor_tensor(dt1[:], dt2[:], dt0[:], ALU.subtract).then_inc(dt_abs.sem, 1)

            def mixer_dt(g):
                pool.wait_ge(dte_done.sem, dte_done.at(g))
                pool.sem_inc(arrived_pool, 1)
                nc.gpsimd.tensor_scalar(dt1[:], dte[:], 2.0, None, ALU.add).then_inc(own_pool, own.one())
                pool.wait_ge(own_pool, own.n)
                nc.gpsimd.tensor_tensor(dts[:], dt1[:], minus1[:], ALU.pow).then_inc(own_pool, own.one())
                pool.wait_ge(own_pool, own.n)
                nc.gpsimd.tensor_tensor(dt1[:], dts[:], dte[:], ALU.mult).then_inc(own_pool, own.one())
                pool.wait_ge(own_pool, own.n)
                nc.gpsimd.tensor_tensor(dte2[:], dt1[:], dt1[:], ALU.mult).then_inc(own_pool, own.one())
                pool.wait_ge(own_pool, own.n)
                nc.gpsimd.tensor_scalar(dta[:], dte2[:], 2.0 / 17, 2.0 / 15, ALU.mult, ALU.add)\
                    .then_inc(own_pool, own.one())
                for n in (13, 11, 9, 7, 5, 3, 1):
                    pool.wait_ge(own_pool, own.n)
                    nc.gpsimd.tensor_tensor(dta[:], dta[:], dte2[:], ALU.mult).then_inc(own_pool, own.one())
                    pool.wait_ge(own_pool, own.n)
                    nc.gpsimd.tensor_scalar(dta[:], dta[:], 2.0 / n, None, ALU.add).then_inc(own_pool, own.one())
                pool.wait_ge(own_pool, own.n)
                nc.gpsimd.tensor_tensor(dta[:], dta[:], dt1[:], ALU.mult).then_inc(own_pool, own.one())
                nc.gpsimd.tensor_scalar(dt2[:], dt2[:], 0.5, None, ALU.mult).then_inc(own_pool, own.one())
                pool.wait_ge(own_pool, own.n)
                if later(g):
                    pool.wait_ge(Xw_done.sem, Xw_done.at(g - 1, CH - 1))
                nc.gpsimd.tensor_tensor(dts[:], dta[:], dt2[:], ALU.add).then_inc(own_pool, own.one())
                pool.wait_ge(own_pool, own.n)
                if later(g):
                    pool.wait_ge(rows_ps.sem, rows_ps.at(g - 1, 2 * CH - 1))
                nc.gpsimd.tensor_tensor(da[:], dts[:], bc(neg_a[:], 1, CH), ALU.mult).then_inc(da_done.sem, 1)

            def mixer_cum(g):
                pool.wait_ge(cum_sb.sem, cum_sb.at(g))
                nc.gpsimd.tensor_tensor(cum[:, 1], cum[:, 2], cum[:, 0], ALU.subtract).then_inc(own_pool, own.one())
                if later(g):
                    pool.wait_ge(decay_done.sem, decay_done.at(g - 1, 2 * CH - 1))
                pool.wait_ge(own_pool, own.n)
                pool.sem_inc(arrived_pool, 1)
                nc.gpsimd.tensor_scalar(ncum[:], cum[:, 0], -1.0, None, ALU.mult).then_inc(cum_diff.sem, 1)

            def mixer_keep(g):
                pool.wait_ge(bounds_done.sem, bounds_done.at(g))
                if later(g):
                    pool.wait_ge(H_done.sem, H_done.at(g - 1, CH - 1))
                    pool.wait_ge(Yi_ps.sem, Yi_ps.at(g - 1, CH - 1))
                pool.sem_inc(arrived_pool, 1)
                nc.gpsimd.tensor_scalar(H[:], H[:], keep[:, 0:1], keep[:, 1:2], ALU.min, ALU.max)\
                    .then_inc(H_kept.sem, 1)

            def mixer_scale(g, c):
                pool.wait_ge(X_sb.sem, X_sb.at(g, c))
                if c or later(g):
                    pool.wait_ge(Yn_ps.sem, Yn_ps.at(g, c - 1))
                pool.wait_ge(da_done.sem, da_done.at(g))
                nc.gpsimd.tensor_tensor(heads3(Xdt[:]), heads3(Xt[:]), bc(dts[:, c, :], 2, HD), ALU.mult)\
                    .then_inc(Xdt_done.sem, 1)
                pool.wait_ge(Xdt_done.sem, Xdt_done.at(g, c))
                pool.wait_ge(ecum_done.sem, ecum_done.at(g))
                if c or later(g):
                    pool.wait_ge(S_ps.sem, S_ps.at(g, c - 1))
                nc.gpsimd.tensor_tensor(heads3(Xw[:]), heads3(Xdt[:]), bc(ecum[:, 1, c, :], 2, HD), ALU.mult)\
                    .then_inc(Xw_done.sem, 1)

            def mixer_decay(g, c):
                if c == 0:
                    pool.wait_ge(H_kept.sem, H_kept.at(g))
                else:
                    pool.wait_ge(H_done.sem, H_done.at(g, c - 1))
                pool.wait_ge(ecum_done.sem, ecum_done.at(g))
                pool.wait_ge(Yi_ps.sem, Yi_ps.at(g, c))
                nc.gpsimd.tensor_tensor(heads3(H[:]), heads3(H[:]), bc(ecum[:, 2, c, :], 2, HD), ALU.mult)\
                    .then_inc(H_scaled.sem, 1)

            def mixer_skip(g, c):
                pool.wait_ge(X_sb.sem, X_sb.at(g, c))
                if c or later(g):
                    pool.wait_ge(Yn_ps.sem, Yn_ps.at(g, c - 1))
                nc.gpsimd.tensor_tensor(DX[:].rearrange("p (h d) -> p h d", h=HEADS),
                                        Xt[:].rearrange("p (h d) -> p h d", h=HEADS),
                                        bc(head_c[:, 2, :], 2, HD), ALU.mult).then_inc(DX_done.sem, 1)

            def mixer_root_y(g):
                pool.wait_ge(sq_done.sem, sq_done.at(g, CH - 1))
                pool.sem_inc(arrived_pool, 1)
                nc.gpsimd.tensor_scalar(vey[:], ssq[:], 1.0 / INNER, EPS, ALU.mult, ALU.add)\
                    .then_inc(own_pool, own.one())
                pool.wait_ge(own_pool, own.n)
                nc.gpsimd.tensor_tensor(rsy[:], vey[:], half_neg[:, 0:CH], ALU.pow).then_inc(rooty.sem, 1)

            def tail_root(t, stats, mv, scratch, dst, done):
                pool.wait_ge(stats.sem, stats.at(t))
                pool.sem_inc(arrived_pool, 1)
                nc.gpsimd.tensor_scalar(scratch[:], mv[:, :, 1], EPS, None, ALU.add).then_inc(own_pool, own.one())
                pool.wait_ge(own_pool, own.n)
                nc.gpsimd.tensor_tensor(dst[:], scratch[:], half_neg[:, 0:CH], ALU.pow).then_inc(done.sem, 1)

            def tail_root4(t):
                pool.wait_ge(stats4.sem, stats4.at(t))
                if later(t):
                    pool.wait_ge(h2_done.sem, h2_done.at(t - 1))
                pool.sem_inc(arrived_pool, 1)
                nc.gpsimd.tensor_scalar(ve4[:], mv3[:, :, 1], EPS, None, ALU.add).then_inc(own_pool, own.one())
                nc.gpsimd.tensor_scalar(neg_mean4[:], mv3[:, :, 0], -1.0, None, ALU.mult).then_inc(own_pool, own.one())
                pool.wait_ge(own_pool, own.n)
                nc.gpsimd.tensor_tensor(rs4[:], ve4[:], half_neg[:, 0:CH], ALU.pow).then_inc(own_pool, own.one())
                pool.wait_ge(own_pool, own.n)
                nc.gpsimd.tensor_tensor(shift4[:], rs4[:], neg_mean4[:], ALU.mult).then_inc(root4.sem, 1)

            def weigh(e, c, *heads):
                for h in heads:
                    if c or later(e):
                        pool.wait_ge(W_part.sem, W_part.at(e, (c - 1) * (RH - 1) + max(h - 1, 0)))
                    if h == 0:
                        pool.wait_ge(ee_done.sem, ee_done.at(e, c))
                    nc.gpsimd.tensor_tensor(Em[:, h], bc(ee[:, c, h, 0:XD], 2, KEYS),
                                            bc(ee[:, c, h, XD:XD + KEYS], 1, XD), ALU.mult).then_inc(E_done.sem, 1)

            def rank(e, c, *heads):
                for h in heads:
                    if c or later(e):
                        pool.wait_ge(P_done.sem, P_done.at(e, (c - 1) * RH + h))
                    if h == 0:
                        pool.wait_ge(ranks_done.sem, ranks_done.at(e, c))
                    nc.gpsimd.tensor_tensor(Dm[:, h], bc(rk[:, c, h, 0:XD], 2, KEYS),
                                            bc(rk[:, c, h, XD:], 1, XD), ALU.add).then_inc(D_done.sem, 1)

            def collect(e, c, *heads):
                flat = [Em[:, h].rearrange("p a b -> p (a b)") for h in range(RH)]
                for h in heads:
                    if h == 1:
                        pool.wait_ge(Zs_done.sem, Zs_done.at(e, c * RH))
                        if c or later(e):
                            pool.wait_ge(WT_ps.sem, WT_ps.at(e, 2 * (c - 1) + 1))
                    pool.wait_ge(Zs_done.sem, Zs_done.at(e, c * RH + h))
                    if h >= 2:
                        pool.wait_ge(W_part.sem, W_part.at(e, c * (RH - 1) + h - 2))
                    nc.gpsimd.tensor_tensor(W[:], flat[0] if h == 1 else W[:], flat[h], ALU.add)\
                        .then_inc(W_part.sem, 1)
                    if h == RH - 1:
                        pool.wait_ge(cls_done.sem, cls_done.at(e, c))
                        pool.wait_ge(W_part.sem, W_part.at(e, c * (RH - 1) + RH - 2))
                        nc.gpsimd.tensor_tensor(W[:, EXPERTS - 1:], W[:, EXPERTS - 1:], clsum[:, c:c + 1], ALU.add)\
                            .then_inc(W_done.sem, 1)

            def do_group(g, e, f, n):
                a, b, c = g is not None, e is not None, f is not None
                if a:
                    mixer_dt_abs(g)
                if b:
                    tail_root4(e)
                if c:
                    weigh(f, 1, 0)
                    collect(f, 0, 2, 3)
                    weigh(f, 1, 1, 2, 3)
                    rank(f, 1, 3)
                if a:
                    mixer_dt(g)
                    mixer_keep(g)
                if c:
                    collect(f, 1, 1, 2, 3)
                if a:
                    mixer_cum(g)
                if b:
                    weigh(e, 0, 0)
                    rank(e, 0, 0)
                    weigh(e, 0, 1)
                    rank(e, 0, 1)
                    weigh(e, 0, 2)
                    rank(e, 0, 2)
                    weigh(e, 0, 3)
                    rank(e, 0, 3)
                if a:
                    mixer_scale(g, 0)
                    mixer_skip(g, 0)
                    mixer_decay(g, 0)
                if c:
                    tail_root(f, statsf, mvf, vf, rsf, rootf)
                if a:
                    mixer_scale(g, 1)
                    mixer_skip(g, 1)
                    mixer_decay(g, 1)
                if b:
                    rank(e, 1, 0, 1)
                if a:
                    mixer_root_y(g)
                if n is not None:
                    mixer_norm(n)
                if b:
                    collect(e, 0, 1)
                if a:
                    tail_root(g, stats3, mv2, ve3, rs3, root3)
                if b:
                    rank(e, 1, 2)
                pool.wait_ge(own_pool, own.n)
                pool.sem_clear(own_pool)
                own.restart()

            mixer_norm(0)
            do_group(0, None, None, 1)
            do_group(1, 0, None, 2)
            do_group(2, 1, 0, 3)
            with pool.Fori(3, NG - 1) as g:
                do_group(g, g - 1, g - 2, g + 1)
            do_group(NG - 1, NG - 2, NG - 3, None)
            do_group(None, NG - 1, NG - 2, None)
            do_group(None, None, NG - 1, None)

        @block.scalar
        def _(act):
            own = Steps()
            act.wait_ge(loaded_c, 16 * 9)
            nc.scalar.activation(neg_a[:], head_c[:, 1, :], ACT.Exp).then_inc(own_act, own.one())
            act.wait_ge(own_act, own.n)
            nc.scalar.mul(neg_a[:], neg_a[:], -1.0).then_inc(own_act, own.one())
            for k in range(DK):
                act.wait_ge(simw_ps, k + 1)
                nc.scalar.activation(w_sim[:, k, :], ring[k][:, :], ACT.Copy).then_inc(own_act, own.one())
            act.wait_ge(own_act, own.n)
            act.sem_inc(simw_sb, 1)
            act.wait_ge(own_act, own.n)
            act.sem_clear(own_act)
            own.restart()

            def mixer_norm(g, t):
                act.wait_ge(root1.sem, root1.at(g))
                if t is not None:
                    act.wait_ge(h2T_ps.sem, h2T_ps.at(t))
                elif later(g):
                    act.wait_ge(hT_ps.sem, hT_ps.at(g - 1))
                for c in range(CH):
                    last = nc.scalar.activation(hn[:, c, :], x_in[:, c, :], ACT.Identity,
                                                scale=rs12[:, CH + c:CH + c + 1], bias=shift12[:, CH + c:CH + c + 1])
                last.then_inc(hn_done.sem, 1)

            def mixer_u(g):
                act.wait_ge(root1.sem, root1.at(g))
                if later(g):
                    act.wait_ge(out_read.sem, out_read.at(g - 1))
                for c in range(CH):
                    last = nc.scalar.activation(u[:, c, :], x_in[:, c, :], ACT.Identity,
                                                scale=rs12[:, c:c + 1], bias=shift12[:, c:c + 1])
                last.then_inc(u_done.sem, 1)
                act.wait_ge(u_done.sem, u_done.at(g))
                act.sem_inc(x_read.sem, 1)

            def mixer_hT(g):
                act.wait_ge(hT_ps.sem, hT_ps.at(g))
                nc.scalar.activation(hT[:], yb[:].rearrange("p (k t) -> p k t", k=DK), ACT.Copy)\
                    .then_inc(hT_sb.sem, 1)

            def mixer_dt(g):
                act.wait_ge(dt_ps.sem, dt_ps.at(g))
                if later(g):
                    act.wait_ge(da_done.sem, da_done.at(g - 1))
                nc.scalar.activation(dtp[:], yb[:, 0:CH * HEADS].rearrange("p (c h) -> p c h", c=CH), ACT.Copy)\
                    .then_inc(dt_sb.sem, 1)

            def mixer_dt_exp(g):
                act.wait_ge(dt_abs.sem, dt_abs.at(g))
                nc.scalar.activation(dte[:], dt1[:], ACT.Exp, scale=-1.0).then_inc(dte_done.sem, 1)

            def silu(g, j):
                act.wait_ge(conv_done.sem, conv_done.at(g, 2 * j + 1))
                nc.scalar.activation(xbcT[:, 2 * j:2 * j + 2, :], acc[:, j % 2], ACT.Silu)\
                    .then_inc(silu_done.sem, 1)

            def mixer_pair(g, j):
                r = j % 2
                ps = ring[j % 2]
                act.wait_ge(pair_ps.sem, pair_ps.at(g, j))
                if j >= 2 or later(g):
                    act.wait_ge(conv_done.sem, conv_done.at(g, 2 * j - 3))
                if j == 0:
                    act.wait_ge(halo_kept.sem, halo_kept.at(g))
                nc.scalar.activation(xp[:, r, :, 0:TAPS - 1], halo[:, 2 * j:2 * j + 2, :], ACT.Copy)\
                    .then_inc(ahead_done.sem, 1)
                nc.scalar.activation(xp[:, r, :, TAPS - 1:], ps[:].rearrange("p (a t) -> p a t", a=2), ACT.Copy)\
                    .then_inc(pair_copied.sem, 1)
                act.wait_ge(ahead_done.sem, ahead_done.at(g, j))
                nc.scalar.activation(halo[:, 2 * j:2 * j + 2, :],
                                     ps[:].rearrange("p (a t) -> p a t", a=2)[:, :, TOK - TAPS + 1:], ACT.Copy)\
                    .then_inc(halo_taken.sem, 1)
                if j >= 2 or later(g):
                    act.wait_ge(silu_done.sem, silu_done.at(g, j - 2))
                for a in range(2):
                    t = 2 * j + a
                    last = nc.scalar.activation(acc[:, r, a], ps[:, a * TOK:(a + 1) * TOK], ACT.Identity,
                                                scale=cw[:, t, TAPS - 1:TAPS], bias=cb[:, t:t + 1])
                last.then_inc(pair_read.sem, 1)

            def mixer_cum(g):
                act.wait_ge(cum_ps.sem, cum_ps.at(g))
                if later(g):
                    act.wait_ge(ecum_done.sem, ecum_done.at(g - 1))
                nc.scalar.activation(cum[:, 0:3:2],
                                     yb[:, 0:2 * CH * HEADS].rearrange("p (a c h) -> p a c h", a=2, c=CH), ACT.Copy)\
                    .then_inc(cum_sb.sem, 1)

            def mixer_exp(g):
                act.wait_ge(cum_diff.sem, cum_diff.at(g))
                if later(g):
                    act.wait_ge(H_done.sem, H_done.at(g - 1, CH - 1))
                nc.scalar.activation(ecum[:], cum[:], ACT.Exp).then_inc(ecum_done.sem, 1)

            def mixer_decay(g, c):
                for q in range(2):
                    act.wait_ge(rows_ps.sem, rows_ps.at(g, 2 * c + q))
                    k = 2 * c + q
                    if k >= 2 or later(g):
                        act.wait_ge(sL_done.sem, sL_done.at(g, k - 2))
                    for i in range(4):
                        h = 4 * q + i
                        last = nc.scalar.activation(Ldec[:, h, :], pairb[q][:, i * P:(i + 1) * P], ACT.Exp,
                                                    bias=ncum[:, c, h:h + 1])
                    last.then_inc(decay_done.sem, 1)

            def mixer_move(g, c):
                act.wait_ge(X_ps.sem, X_ps.at(g, c))
                if c or later(g):
                    act.wait_ge(Xw_done.sem, Xw_done.at(g, c - 1))
                if c or later(g):
                    act.wait_ge(DX_done.sem, DX_done.at(g, c - 1))
                nc.scalar.activation(Xt[:], ring[c][:], ACT.Copy).then_inc(X_sb.sem, 1)

            def mixer_B(g, c):
                for q in range(2):
                    act.wait_ge(Bt_ps.sem, Bt_ps.at(g, 2 * c + q))
                    if c or later(g):
                        act.wait_ge(S_ps.sem, S_ps.at(g, c - 1))
                    nc.scalar.activation(Btok[:, 4 * q:4 * q + 4, :],
                                         pairb[q][:].rearrange("p (h t) -> p h t", h=4), ACT.Copy)\
                        .then_inc(Bt_sb.sem, 1)

            def mixer_z(g, c):
                act.wait_ge(z_ps.sem, z_ps.at(g, c))
                if later(g):
                    act.wait_ge(sq_done.sem, sq_done.at(g - 1, c))
                nc.scalar.activation(zs[:, c], ring[c][:], ACT.Silu).then_inc(z_done.sem, 1)

            def mixer_square(g, c):
                act.wait_ge(y_done.sem, y_done.at(g, c))
                if c == 0 and later(g):
                    act.wait_ge(rooty.sem, rooty.at(g - 1))
                nc.scalar.activation(zs[:, c], yv[:, c], ACT.Square, accum_out=ssq[:, c:c + 1])\
                    .then_inc(sq_done.sem, 1)

            def mixer_yT(g, c):
                act.wait_ge(yT_ps.sem, yT_ps.at(g, c))
                if c or later(g):
                    act.wait_ge(out_ps.sem, out_ps.at(g, c - 1))
                nc.scalar.activation(yT[:], ring[c][:], ACT.Copy).then_inc(yT_sb.sem, 1)

            def tail_norm(t, g):
                act.wait_ge(root4.sem, root4.at(t))
                act.wait_ge(hT_ps.sem, hT_ps.at(t if g is None else g))
                for c in range(CH):
                    last = nc.scalar.activation(hn[:, c, :], x1[:, c, :], ACT.Identity, scale=rs4[:, c:c + 1],
                                                bias=shift4[:, c:c + 1])
                last.then_inc(h2_done.sem, 1)

            def tail_keep(t):
                act.wait_ge(xres_read.sem, xres_read.at(t))
                if later(t):
                    act.wait_ge(o_done.sem, o_done.at(t - 1))
                nc.scalar.activation(x1_late[:], x1[:], ACT.Copy).then_inc(x1_kept.sem, 1)

            def tail_h2T(t):
                act.wait_ge(h2T_ps.sem, h2T_ps.at(t))
                if later(t):
                    act.wait_ge(A_ps.sem, A_ps.at(t - 1, CH - 1))
                nc.scalar.activation(h2T[:], yb[:].rearrange("p (k t) -> p k t", k=DK), ACT.Copy)\
                    .then_inc(h2T_sb.sem, 1)

            def ffn_sim(e, c):
                act.wait_ge(sim_ps.sem, sim_ps.at(e, c))
                if later(e):
                    act.wait_ge(earg_done.sem, earg_done.at(e - 1, c))
                nc.scalar.activation(sim[:, c].rearrange("p a h k -> p (a h k)"), yb[:], ACT.Copy)\
                    .then_inc(sim_sb.sem, 1)

            def ffn_up(e, j):
                act.wait_ge(up_ps.sem, up_ps.at(e, j))
                if later(e):
                    act.wait_ge(down_ps.sem, down_ps.at(e - 1, CH - 1))
                nc.scalar.activation(hid[:, 2 * j:2 * j + 2, :], yb[:].rearrange("p (a t) -> p a t", a=2), ACT.Silu)\
                    .then_inc(up_done.sem, 1)

            def ffn_exp(e, c):
                act.wait_ge(earg_done.sem, earg_done.at(e, c))
                nc.scalar.activation(ee[:, c], ee[:, c], ACT.Exp).then_inc(ee_done.sem, 1)

            def ffn_experts(e, c, *heads):
                if 0 in heads:
                    act.wait_ge(clz_done.sem, clz_done.at(e, c))
                    if c or later(e):
                        act.wait_ge(cls_done.sem, cls_done.at(e, c - 1))
                    if later(e):
                        act.wait_ge(W_done.sem, W_done.at(e - 1, c))
                    nc.scalar.activation(cls[:], clz[:, c], ACT.Silu, accum_out=clsum[:, c:c + 1])\
                        .then_inc(cls_done.sem, 1)
                for h in heads:
                    act.wait_ge(Z_done.sem, Z_done.at(e, c * RH + h))
                    flat = Em[:, h].rearrange("p a b -> p (a b)")
                    nc.scalar.activation(flat, flat, ACT.Silu, scale=rden[:, c, h:h + 1]).then_inc(Zs_done.sem, 1)

            def ffn_WT(e, c):
                for q in range(2):
                    act.wait_ge(WT_ps.sem, WT_ps.at(e, 2 * c + q))
                    if c:
                        act.wait_ge(out_part.sem, out_part.at(e))
                    elif later(e):
                        act.wait_ge(f_ps.sem, f_ps.at(e - 1))
                    nc.scalar.activation(WT[:, 4 * q:4 * q + 4, :],
                                         pairb[q][:].rearrange("p (h t) -> p h t", h=4), ACT.Copy)\
                        .then_inc(WT_sb.sem, 1)

            def ffn_out(e):
                act.wait_ge(f_ps.sem, f_ps.at(e))
                if later(e):
                    act.wait_ge(stored, 16 * e)
                nc.scalar.activation(f[:], f0[:].rearrange("p (c d) -> p c d", c=CH), ACT.Copy).then_inc(f_sb.sem, 1)

            def do_group(g, e, f, n):
                a, b, c = g is not None, e is not None, f is not None

                def pairs(*js):
                    for j in js:
                        if a:
                            if j >= 2:
                                silu(g, j - 2)
                            mixer_pair(g, j)

                pairs(0, 1)
                if a:
                    mixer_dt(g)
                pairs(2)
                if b:
                    tail_norm(e, g)
                pairs(3)
                if b:
                    tail_h2T(e)
                if a:
                    mixer_dt_exp(g)
                    mixer_z(g, 0)
                if b:
                    ffn_sim(e, 0)
                if c:
                    ffn_WT(f, 0)
                    ffn_experts(f, 1, 0)
                if a:
                    mixer_z(g, 1)
                pairs(4)
                if b:
                    ffn_sim(e, 1)
                pairs(5)
                if c:
                    ffn_experts(f, 1, 1)
                pairs(6)
                if c:
                    ffn_experts(f, 1, 2, 3)
                if b:
                    ffn_up(e, 0)
                pairs(7)
                if b:
                    ffn_up(e, 1)
                    ffn_exp(e, 0)
                if a:
                    mixer_cum(g)
                pairs(8)
                if b:
                    ffn_up(e, 2)
                pairs(9)
                if b:
                    ffn_up(e, 3)
                if a:
                    silu(g, PAIRS - 2)
                    silu(g, PAIRS - 1)
                    mixer_move(g, 0)
                if c:
                    ffn_WT(f, 1)
                if a:
                    mixer_exp(g)
                    mixer_decay(g, 0)
                if c:
                    ffn_out(f)
                if a:
                    mixer_B(g, 0)
                if b:
                    ffn_exp(e, 1)
                if a:
                    mixer_move(g, 1)
                    mixer_decay(g, 1)
                    mixer_square(g, 0)
                    mixer_B(g, 1)
                if b:
                    tail_keep(e)
                    ffn_experts(e, 0, 0, 1)
                if a:
                    mixer_yT(g, 0)
                    mixer_square(g, 1)
                    mixer_yT(g, 1)
                if b:
                    ffn_experts(e, 0, 2)
                if n is not None:
                    mixer_norm(n, e)
                    mixer_hT(n)
                    mixer_u(n)
                if b:
                    ffn_experts(e, 0, 3)

            mixer_norm(0, None)
            mixer_hT(0)
            mixer_u(0)
            do_group(0, None, None, 1)
            do_group(1, 0, None, 2)
            do_group(2, 1, 0, 3)
            with act.Fori(3, NG - 1) as g:
                do_group(g, g - 1, g - 2, g + 1)
            do_group(NG - 1, NG - 2, NG - 3, None)
            do_group(None, NG - 1, NG - 2, None)
            do_group(None, None, NG - 1, None)

        @block.vector
        def _(dve):
            own = Steps()
            V = nc.vector
            dve.wait_ge(loaded_c, 16 * 9)
            dve.wait_ge(loaded_in, 16)
            for k in range(DK):
                last = V.tensor_scalar(w_in[:, k, :], w_in[:, k, :], nw[:, k:k + 1], None, ALU.mult)
                last.then_inc(own_dve, own.one())
            dve.wait_ge(own_dve, own.n)
            dve.sem_inc(folded, 1)
            dve.wait_ge(consts, 1)

            dve.wait_ge(own_dve, own.n)
            dve.sem_clear(own_dve)
            own.restart()

            def mixer_stats(g):
                dve.wait_ge(x_loaded, 16 * (g + 1))
                if later(g):
                    dve.wait_ge(root1.sem, root1.at(g - 1))
                for c in range(CH):
                    V.bn_stats(lnst[:, c, :], x_in[:, c, :]).then_inc(own_dve, own.one())
                dve.wait_ge(own_dve, own.n)
                for c in range(CH):
                    last = V.bn_aggr(mv1[:, c, :], lnst[:, c, :])
                last.then_inc(stats1.sem, 1)
                if later(g):
                    dve.wait_ge(halo_kept.sem, halo_kept.at(g - 1))
                    dve.wait_ge(H_kept.sem, H_kept.at(g - 1))
                V.tensor_copy(keep[:].unsqueeze(2), keep_tab[:, :, bass.ds(g, 1)]).then_inc(bounds_done.sem, 1)
                dve.wait_ge(bounds_done.sem, bounds_done.at(g))
                if later(g):
                    dve.wait_ge(halo_taken.sem, halo_taken.at(g - 1, PAIRS - 1))
                V.tensor_scalar(halo[:], halo[:], keep[:, 0:1], keep[:, 1:2], ALU.min, ALU.max)\
                    .then_inc(halo_kept.sem, 1)

            def mixer_conv(g, j):
                r = j % 2
                dve.wait_ge(pair_read.sem, pair_read.at(g, j))
                dve.wait_ge(ahead_done.sem, ahead_done.at(g, j))
                dve.wait_ge(pair_copied.sem, pair_copied.at(g, j))
                before = [0, 0]
                for k in range(TAPS - 1):
                    for a in range(2):
                        t = 2 * j + a
                        if k:
                            dve.wait_ge(own_dve, before[a])
                        ins = V.scalar_tensor_tensor(acc[:, r, a], xp[:, r, a, k:k + TOK], cw[:, t, k:k + 1],
                                                     acc[:, r, a], ALU.mult, ALU.add)
                        if k == TAPS - 2:
                            ins.then_inc(conv_done.sem, 1)
                        else:
                            ins.then_inc(own_dve, own.one())
                            before[a] = own.n

            def mixer_scores(g, c):
                for q in range(2):
                    dve.wait_ge(sc_ps.sem, sc_ps.at(g, 2 * c + q))
                    dve.wait_ge(decay_done.sem, decay_done.at(g, 2 * c + q))
                    if c or later(g):
                        dve.wait_ge(Yn_ps.sem, Yn_ps.at(g, c - 1))
                    V.tensor_tensor(sL[:, 4 * q:4 * q + 4, :], pairb[q][:].rearrange("p (h t) -> p h t", h=4),
                                    Ldec[:, 4 * q:4 * q + 4, :], ALU.mult).then_inc(sL_done.sem, 1)

            def mixer_state(g, c):
                dve.wait_ge(Yi_ps.sem, Yi_ps.at(g, c))
                if later(g):
                    dve.wait_ge(yT_ps.sem, yT_ps.at(g - 1, c))
                    dve.wait_ge(sq_done.sem, sq_done.at(g - 1, c))
                V.tensor_tensor(heads3(yv[:, c]), heads3(ring[1 - c][:]), bc(ecum[:, 0, c, :], 2, HD), ALU.mult)\
                    .then_inc(Yi_read.sem, 1)

            def mixer_step(g, c):
                dve.wait_ge(H_scaled.sem, H_scaled.at(g, c))
                dve.wait_ge(S_ps.sem, S_ps.at(g, c))
                V.tensor_tensor(H[:], H[:], ring[c][:], ALU.add).then_inc(H_done.sem, 1)

            def mixer_gate(g, c):
                dve.wait_ge(Yi_read.sem, Yi_read.at(g, c))
                dve.wait_ge(Yn_ps.sem, Yn_ps.at(g, c))
                V.tensor_tensor(yv[:, c], yv[:, c], yb[:], ALU.add).then_inc(Yn_read.sem, 1)
                dve.wait_ge(Yn_read.sem, Yn_read.at(g, c))
                dve.wait_ge(z_done.sem, z_done.at(g, c))
                V.tensor_tensor(yv[:, c], yv[:, c], zs[:, c], ALU.mult).then_inc(y_done.sem, 1)

            def tail_sum(t):
                dve.wait_ge(rooty.sem, rooty.at(t))
                dve.wait_ge(u_done.sem, u_done.at(t))
                dve.wait_ge(out_ps.sem, out_ps.at(t, CH - 1))
                if later(t):
                    dve.wait_ge(xres_read.sem, xres_read.at(t - 1))
                for c in range(CH):
                    last = V.scalar_tensor_tensor(v[:, c, :], ring[0][:, c * D:(c + 1) * D], rsy[:, c:c + 1],
                                                  u[:, c, :], ALU.mult, ALU.add)
                last.then_inc(out_read.sem, 1)
                dve.wait_ge(out_read.sem, out_read.at(t))
                for c in range(CH):
                    V.bn_stats(sumst[:, c, :], v[:, c, :]).then_inc(own_dve, own.one())
                dve.wait_ge(own_dve, own.n)
                for c in range(CH):
                    last = V.bn_aggr(mv2[:, c, :], sumst[:, c, :])
                last.then_inc(stats3.sem, 1)

            def tail_residual(t):
                dve.wait_ge(root3.sem, root3.at(t))
                for c in range(CH):
                    V.tensor_scalar(v[:, c, :], v[:, c, :], mv2[:, c, 0:1], rs3[:, c:c + 1],
                                    ALU.subtract, ALU.mult).then_inc(own_dve, own.one())
                dve.wait_ge(own_dve, own.n)
                dve.wait_ge(xres_loaded, 16 * (t + 1))
                if later(t):
                    dve.wait_ge(x1_kept.sem, x1_kept.at(t - 1))
                    dve.wait_ge(h2_done.sem, h2_done.at(t - 1))
                V.tensor_tensor(x1[:], v[:], x_res[:], ALU.add).then_inc(xres_read.sem, 1)
                dve.wait_ge(xres_read.sem, xres_read.at(t))
                for c in range(CH):
                    V.bn_stats(resst[:, c, :], x1[:, c, :]).then_inc(own_dve, own.one())
                dve.wait_ge(own_dve, own.n)
                for c in range(CH):
                    last = V.bn_aggr(mv3[:, c, :], resst[:, c, :])
                last.then_inc(stats4.sem, 1)

            def ffn_route(e, c):
                dve.wait_ge(sim_sb.sem, sim_sb.at(e, c))
                dve.sem_inc(arrived_dve, 1)
                best = []
                for s in range(2):
                    for h in range(RH):
                        V.max(s8[:, s, h, :], sim[:, c, s, h, :]).then_inc(own_dve, own.one())
                        best.append(own.n)
                for s in range(2):
                    for h in range(RH):
                        dve.wait_ge(own_dve, best[s * RH + h])
                        V.max_index(i8[:, s, h, :], s8[:, s, h, :], sim[:, c, s, h, :]).then_inc(own_dve, own.one())
                numbered = own.n
                at = 0
                for first, rows, n in CAND:
                    V.tensor_tensor(cand[:, :, at:at + rows * n].rearrange("p h (r n) -> p h r n", n=n),
                                    bc(s8[:, 0, :, first:first + rows], 3, n), bc(s8[:, 1, :, 0:n], 2, rows),
                                    ALU.add).then_inc(own_dve, own.one())
                    at += rows * n
                summed = own.n
                if later(e):
                    dve.wait_ge(E_done.sem, E_done.at(e - 1, c * RH + RH - 1))
                V.tensor_tensor(ee[:, c, :, 0:XD], sim[:, c, 0, :, 0:XD], bc(s8[:, 0, :, 0], 2, XD),
                                ALU.subtract).then_inc(own_dve, own.one())
                V.tensor_tensor(ee[:, c, :, XD:XD + KEYS], sim[:, c, 1], bc(s8[:, 1, :, 0], 2, KEYS),
                                ALU.subtract).then_inc(own_dve, own.one())
                dve.wait_ge(own_dve, numbered)
                V.tensor_copy(i8b[:], i8[:]).then_inc(own_dve, own.one())
                copied = own.n
                dve.wait_ge(own_dve, summed)
                for h in range(RH):
                    V.max(c8[:, h, :], cand[:, h, :]).then_inc(own_dve, own.one())
                picked = own.n
                dve.wait_ge(own_dve, copied)
                V.tensor_tensor(eq[:, :, XD:], bc(i8b[:, 1], 2, KEYS), bc(iota[:], 1, RH), ALU.is_equal)\
                    .then_inc(own_dve, own.one())
                V.tensor_tensor(eq[:, :, 0:XD], bc(i8b[:, 0], 2, XD), bc(iota[:, 0:XD], 1, RH), ALU.is_equal)\
                    .then_inc(own_dve, own.one())
                compared = own.n
                dve.wait_ge(own_dve, picked)
                V.tensor_tensor(ee[:, c, :, XD + KEYS:], cand[:], bc(c8[:, :, 0], 2, NC), ALU.subtract)\
                    .then_inc(earg_done.sem, 1)
                for h in range(RH):
                    V.match_replace(rest[:, h, :], c8[:, h, :], cand[:, h, :], LOWEST).then_inc(own_dve, own.one())
                replaced = own.n
                dve.wait_ge(own_dve, compared)
                V.tensor_tensor(eq[:, :, XD:], eq[:, :, XD:], bc(bc(rank_w[:], 1, KEYS), 1, RH), ALU.mult)\
                    .then_inc(own_dve, own.one())
                dve.wait_ge(own_dve, replaced)
                V.tensor_tensor(chosen[:], rest[:], cand[:], ALU.not_equal).then_inc(own_dve, own.one())
                marked = own.n
                V.tensor_scalar(cmask[:], i8b[:, 0], float(XD), None, ALU.is_ge).then_inc(own_dve, own.one())
                dve.wait_ge(own_dve, marked)
                at = 0
                with nc.allow_low_precision("counts up to 8"):
                    for first, rows, n in CAND:
                        part = chosen[:, :, at:at + rows * n].rearrange("p h (r n) -> p h r n", n=n)
                        V.tensor_reduce(n8[:, :, first:first + rows], part, AX_X, ALU.add)\
                            .then_inc(own_dve, own.one())
                        at += rows * n
                dve.wait_ge(own_dve, own.n)
                V.tensor_tensor(eq[:, :, 0:XD], eq[:, :, 0:XD], bc(n8[:], 2, XD), ALU.mult)\
                    .then_inc(own_dve, own.one())
                for half in (4, 2):
                    dve.wait_ge(own_dve, own.n)
                    V.tensor_tensor(eq[:, :, :, 0:half], eq[:, :, :, 0:half], eq[:, :, :, half:2 * half], ALU.add)\
                        .then_inc(own_dve, own.one())
                dve.wait_ge(own_dve, own.n)
                if later(e):
                    dve.wait_ge(D_done.sem, D_done.at(e - 1, c * RH + RH - 1))
                V.tensor_tensor(rk[:, c], eq[:, :, :, 0], eq[:, :, :, 1], ALU.add).then_inc(ranks_done.sem, 1)

            def ffn_clamped(e, c):
                dve.wait_ge(ee_done.sem, ee_done.at(e, c))
                V.tensor_tensor(psel[:], chosen[:], ee[:, c, :, XD + KEYS:], ALU.mult).then_inc(own_dve, own.one())
                dve.wait_ge(own_dve, own.n)
                V.tensor_reduce(den[:], psel[:], AX_X, ALU.add).then_inc(own_dve, own.one())
                divisor = own.n
                if later(e):
                    dve.wait_ge(Zs_done.sem, Zs_done.at(e - 1, c * RH + RH - 1))
                at = 0
                for first, rows, n in CAND:
                    V.tensor_tensor(clz[:, c, :, at:at + rows * n].rearrange("p h (r n) -> p h r n", n=n),
                                    psel[:, :, at:at + rows * n].rearrange("p h (r n) -> p h r n", n=n),
                                    bc(cmask[:, :, first:first + rows], 3, n), ALU.mult).then_inc(own_dve, own.one())
                    at += rows * n
                dve.wait_ge(own_dve, divisor)
                V.reciprocal(rden[:, c], den[:]).then_inc(own_dve, own.one())

            def ffn_last(e, c):
                dve.wait_ge(A_ps.sem, A_ps.at(e, c))
                V.tensor_copy(last_a[:], fA[:, EXPERTS - 1:]).then_inc(own_dve, own.one())
                dve.wait_ge(own_dve, own.n)
                V.scalar_tensor_tensor(clz[:, c], clz[:, c], last_a[:, 0:1], bc(rden[:, c], 2, NC),
                                       ALU.mult, ALU.mult).then_inc(clz_done.sem, 1)

            def ffn_mask(e, c, *heads):
                for h in heads:
                    flat = Em[:, h].rearrange("p a b -> p (a b)")
                    dve.wait_ge(E_done.sem, E_done.at(e, c * RH + h))
                    dve.wait_ge(D_done.sem, D_done.at(e, c * RH + h))
                    V.scalar_tensor_tensor(flat, Dm[:, h].rearrange("p a b -> p (a b)"), float(TOP), flat,
                                           ALU.is_gt, ALU.mult).then_inc(P_done.sem, 1)

            def ffn_times(e, c, *heads):
                for h in heads:
                    flat = Em[:, h].rearrange("p a b -> p (a b)")
                    dve.wait_ge(P_done.sem, P_done.at(e, c * RH + h))
                    V.tensor_tensor(flat, flat, fA[:], ALU.mult).then_inc(Z_done.sem, 1)

            def ffn_stats(e):
                dve.wait_ge(f_sb.sem, f_sb.at(e))
                for c in range(CH):
                    V.bn_stats(fst[:, c, :], f[:, c, :]).then_inc(own_dve, own.one())
                dve.wait_ge(own_dve, own.n)
                for c in range(CH):
                    last = V.bn_aggr(mvf[:, c, :], fst[:, c, :])
                last.then_inc(statsf.sem, 1)

            def ffn_store(e):
                dve.wait_ge(rootf.sem, rootf.at(e))
                for c in range(CH):
                    V.tensor_scalar(f[:, c, :], f[:, c, :], mvf[:, c, 0:1], rsf[:, c:c + 1],
                                    ALU.subtract, ALU.mult).then_inc(own_dve, own.one())
                dve.wait_ge(own_dve, own.n)
                dve.wait_ge(x1_kept.sem, x1_kept.at(e))
                V.tensor_tensor(f[:], f[:], x1_late[:], ALU.add).then_inc(o_done.sem, 1)

            def do_group(g, e, f, n):
                a, b, c = g is not None, e is not None, f is not None

                def conv(*js):
                    for j in js:
                        if a:
                            mixer_conv(g, j)

                if b:
                    tail_residual(e)
                conv(0, 1)
                if c:
                    ffn_last(f, 1)
                    ffn_mask(f, 1, 0)
                conv(2, 3)
                if c:
                    ffn_times(f, 1, 0)
                    ffn_mask(f, 1, 1)
                    ffn_times(f, 1, 1)
                    ffn_mask(f, 1, 2)
                conv(4)
                if c:
                    ffn_times(f, 1, 2)
                    ffn_mask(f, 1, 3)
                conv(5)
                if c:
                    ffn_times(f, 1, 3)
                if b:
                    ffn_route(e, 0)
                conv(6)
                if b:
                    ffn_clamped(e, 0)
                conv(7, 8, 9)
                if b:
                    ffn_route(e, 1)
                if c:
                    ffn_stats(f)
                if a:
                    mixer_scores(g, 0)
                    mixer_state(g, 0)
                if b:
                    ffn_clamped(e, 1)
                    ffn_last(e, 0)
                    ffn_mask(e, 0, 0)
                if c:
                    ffn_store(f)
                if a:
                    mixer_gate(g, 0)
                    mixer_step(g, 0)
                if b:
                    ffn_times(e, 0, 0)
                    ffn_mask(e, 0, 1)
                if a:
                    mixer_scores(g, 1)
                if b:
                    ffn_times(e, 0, 1)
                if a:
                    mixer_state(g, 1)
                if b:
                    ffn_mask(e, 0, 2)
                if a:
                    mixer_gate(g, 1)
                if b:
                    ffn_times(e, 0, 2)
                if a:
                    mixer_step(g, 1)
                if n is not None:
                    mixer_stats(n)
                if b:
                    ffn_mask(e, 0, 3)
                    ffn_times(e, 0, 3)
                if a:
                    tail_sum(g)
                dve.wait_ge(own_dve, own.n)
                dve.sem_clear(own_dve)
                own.restart()

            mixer_stats(0)
            dve.wait_ge(loaded_out, 16)
            for k in range(INNER // P):
                V.tensor_scalar(w_out[:, k, :], w_out[:, k, :], gw[:, k:k + 1], None, ALU.mult)\
                    .then_inc(own_dve, own.one())
            dve.wait_ge(own_dve, own.n)
            dve.sem_inc(folded, 1)
            do_group(0, None, None, 1)
            do_group(1, 0, None, 2)
            do_group(2, 1, 0, 3)
            with dve.Fori(3, NG - 1) as g:
                do_group(g, g - 1, g - 2, g + 1)
            do_group(NG - 1, NG - 2, NG - 3, None)
            do_group(None, NG - 1, NG - 2, None)
            do_group(None, None, NG - 1, None)

        @block.tensor
        def _(pe):
            mm = nc.tensor.matmul
            pe.wait_ge(consts, 1)
            pe.wait_ge(loaded_c, 16 * 9)
            for k in range(DK):
                for s in range(2 * RH):
                    last = mm(ring[k][:, s * KEYS:(s + 1) * KEYS], hid[0:64, s, k * P:(k + 1) * P],
                              xbcT[0:64, 0:2, :].rearrange("p a (b k) -> p (a b) k", k=KEYS)[:, s, :],
                              start=True, stop=True)
                last.then_inc(simw_ps, 1)
            pe.wait_ge(simw_sb, 1)
            pe.wait_ge(folded, 1)

            def mixer_hT(g):
                pe.wait_ge(hn_done.sem, hn_done.at(g))
                if later(g):
                    pe.wait_ge(Yn_read.sem, Yn_read.at(g - 1, CH - 1))
                for c in range(CH):
                    for k in range(DK):
                        last = nc.tensor.transpose(yb[:, k * TOK + c * P:k * TOK + (c + 1) * P],
                                                   hn[:, c, k * P:(k + 1) * P], ident[:])
                last.then_inc(hT_ps.sem, 1)

            def mixer_dt(g):
                pe.wait_ge(hT_sb.sem, hT_sb.at(g))
                for c in range(CH):
                    for k in range(DK):
                        last = mm(yb[:, c * HEADS:(c + 1) * HEADS], hT[:, k, c * P:(c + 1) * P],
                                  w_in[:, k, INNER + XBC:], start=k == 0, stop=k == DK - 1)
                last.then_inc(dt_ps.sem, 1)

            def mixer_pair(g, j):
                if j == 0:
                    pe.wait_ge(hT_sb.sem, hT_sb.at(g))
                    if later(g):
                        pe.wait_ge(out_read.sem, out_read.at(g - 1))
                elif j == 1:
                    if later(g):
                        pe.wait_ge(yT_sb.sem, yT_sb.at(g - 1, CH - 1))
                elif j in (4, 5):
                    pe.wait_ge(z_done.sem, z_done.at(g, j - 4))
                else:
                    pe.wait_ge(pair_read.sem, pair_read.at(g, j - 2))
                for a in range(2):
                    at = INNER + (2 * j + a) * P
                    for k in range(DK):
                        last = mm(ring[j % 2][:, a * TOK:(a + 1) * TOK], w_in[:, k, at:at + P], hT[:, k, :],
                                  start=k == 0, stop=k == DK - 1)
                last.then_inc(pair_ps.sem, 1)

            def mixer_cum(g, e):
                pe.wait_ge(da_done.sem, da_done.at(g))
                if e is not None:
                    pe.wait_ge(up_done.sem, up_done.at(e, 1))
                n = CH * HEADS
                mm(yb[:, 0:n], tri[:], da[:].rearrange("p c h -> p (c h)"), start=True, stop=True)
                mm(yb[:, n:2 * n], ones[:], da[:].rearrange("p c h -> p (c h)"), start=True, stop=True)\
                    .then_inc(cum_ps.sem, 1)

            def mixer_z(g, c):
                pe.wait_ge(pair_read.sem, pair_read.at(g, 2 + c))
                for k in range(DK):
                    last = mm(ring[c][:], hT[:, k, c * P:(c + 1) * P], w_in[:, k, 0:INNER],
                              start=k == 0, stop=k == DK - 1)
                last.then_inc(z_ps.sem, 1)

            def mixer_rows(g, c, f):
                for q in range(2):
                    if c == 0 and f is not None:
                        pe.wait_ge(WT_sb.sem, WT_sb.at(f, CH + q))
                    elif c or later(g):
                        pe.wait_ge(sL_done.sem, sL_done.at(g, 2 * (c - 1) + q))
                    mm(pairb[q][:], ident_b[:], mask_b[:].rearrange("p h t -> p (h t)"), start=True, stop=False)
                    for i in range(4):
                        h = 4 * q + i
                        last = mm(pairb[q][:, i * P:(i + 1) * P], da[:, c, h:h + 1].to_broadcast([P, P]), tri[:],
                                  start=False, stop=i == 3)
                    last.then_inc(rows_ps.sem, 1)

            def mixer_X(g, c):
                pe.wait_ge(silu_done.sem, silu_done.at(g, XP - 1))
                if c == 0:
                    pe.wait_ge(pair_read.sem, pair_read.at(g, PAIRS - 2))
                else:
                    pe.wait_ge(Yi_read.sem, Yi_read.at(g, 0))
                for i in range(INNER // P):
                    last = nc.tensor.transpose(ring[c][:, i * P:(i + 1) * P],
                                               xbcT[:, i, c * P:(c + 1) * P], ident[:])
                last.then_inc(X_ps.sem, 1)

            def mixer_B(g, c):
                pe.wait_ge(silu_done.sem, silu_done.at(g, XP + BP - 1))
                for q in range(2):
                    pe.wait_ge(decay_done.sem, decay_done.at(g, 2 * c + q))
                    for i in range(4):
                        last = nc.tensor.transpose(pairb[q][:, i * P:(i + 1) * P],
                                                   xbcT[:, INNER // P + 4 * q + i, c * P:(c + 1) * P], ident[:])
                    last.then_inc(Bt_ps.sem, 1)

            def mixer_Yi(g, c):
                pe.wait_ge(silu_done.sem, silu_done.at(g, PAIRS - 1))
                if c == 0:
                    pe.wait_ge(H_kept.sem, H_kept.at(g))
                    pe.wait_ge(pair_read.sem, pair_read.at(g, PAIRS - 1))
                else:
                    pe.wait_ge(H_done.sem, H_done.at(g, c - 1))
                for h in range(HEADS):
                    last = mm(ring[1 - c][:, h * HD:(h + 1) * HD],
                              xbcT[:, INNER // P + HEADS + h, c * P:(c + 1) * P], H[:, h * HD:(h + 1) * HD],
                              start=True, stop=True)
                last.then_inc(Yi_ps.sem, 1)

            def mixer_scores(g, c):
                for q in range(2):
                    pe.wait_ge(Bt_sb.sem, Bt_sb.at(g, 2 * c + q))
                    for i in range(4):
                        h = 4 * q + i
                        last = mm(pairb[q][:, i * P:(i + 1) * P], xbcT[:, INNER // P + h, c * P:(c + 1) * P],
                                  xbcT[:, INNER // P + HEADS + h, c * P:(c + 1) * P], start=True, stop=True)
                    last.then_inc(sc_ps.sem, 1)

            def mixer_S(g, c):
                pe.wait_ge(Xw_done.sem, Xw_done.at(g, c))
                pe.wait_ge(X_sb.sem, X_sb.at(g, c))
                for h in range(HEADS):
                    last = mm(ring[c][:, h * HD:(h + 1) * HD], Btok[:, h, :], Xw[:, h * HD:(h + 1) * HD],
                              start=True, stop=True)
                last.then_inc(S_ps.sem, 1)

            def mixer_Yn(g, c, e):
                if c:
                    pe.wait_ge(Yn_read.sem, Yn_read.at(g, c - 1))
                elif e is not None:
                    pe.wait_ge(up_done.sem, up_done.at(e, FT // 2 - 1))
                else:
                    pe.wait_ge(cum_sb.sem, cum_sb.at(g))
                pe.wait_ge(DX_done.sem, DX_done.at(g, c))
                mm(yb[:], ident[:], DX[:], start=True, stop=False)
                pe.wait_ge(Xdt_done.sem, Xdt_done.at(g, c))
                pe.wait_ge(sL_done.sem, sL_done.at(g, 2 * c + 1))
                for h in range(HEADS):
                    last = mm(yb[:, h * HD:(h + 1) * HD], sL[:, h, :], Xdt[:, h * HD:(h + 1) * HD],
                              start=False, stop=h == HEADS - 1)
                last.then_inc(Yn_ps.sem, 1)

            def mixer_yT(g, c):
                pe.wait_ge(y_done.sem, y_done.at(g, c))
                if c == 0:
                    pe.wait_ge(Yi_read.sem, Yi_read.at(g, CH - 1))
                else:
                    pe.wait_ge(H_done.sem, H_done.at(g, CH - 1))
                for i in range(INNER // P):
                    last = nc.tensor.transpose(ring[c][:, i * P:(i + 1) * P], yv[:, c, i * P:(i + 1) * P],
                                               ident[:])
                last.then_inc(yT_ps.sem, 1)

            def mixer_out(g, c):
                pe.wait_ge(folded, 2)
                pe.wait_ge(yT_sb.sem, yT_sb.at(g, c))
                for i in range(INNER // P):
                    last = mm(ring[0][:, c * D:(c + 1) * D], yT[:, i * P:(i + 1) * P], w_out[:, i, :],
                              start=i == 0, stop=i == INNER // P - 1)
                last.then_inc(out_ps.sem, 1)

            def tail_h2T(t, g):
                pe.wait_ge(h2_done.sem, h2_done.at(t))
                if g is not None:
                    pe.wait_ge(dt_sb.sem, dt_sb.at(g))
                else:
                    pe.wait_ge(Yn_read.sem, Yn_read.at(t, CH - 1))
                for c in range(CH):
                    for k in range(DK):
                        last = nc.tensor.transpose(yb[:, k * TOK + c * P:k * TOK + (c + 1) * P],
                                                   hn[:, c, k * P:(k + 1) * P], ident[:])
                last.then_inc(h2T_ps.sem, 1)

            def ffn_sim(e, c):
                if c == 0:
                    pe.wait_ge(h2T_sb.sem, h2T_sb.at(e))
                else:
                    pe.wait_ge(sim_sb.sem, sim_sb.at(e, 0))
                for k in range(DK):
                    last = mm(yb[:], h2T[:, k, c * P:(c + 1) * P], w_sim[:, k, :], start=k == 0, stop=k == DK - 1)
                last.then_inc(sim_ps.sem, 1)

            def ffn_A(e, c):
                if c or later(e):
                    pe.wait_ge(Z_done.sem, Z_done.at(e, c * RH - 1))
                for q in range(2):
                    for k in range(DK):
                        last = mm(fA[:, q * 512:(q + 1) * 512], h2T[:, k, c * P:(c + 1) * P],
                                  w_de[:, k, q * 512:(q + 1) * 512],
                                  start=k == 0, stop=k == DK - 1)
                last.then_inc(A_ps.sem, 1)

            def ffn_up(e, j, g=None):
                if j == 0:
                    pe.wait_ge(sim_sb.sem, sim_sb.at(e, 1))
                elif g is not None:
                    pe.wait_ge(cum_sb.sem, cum_sb.at(g))
                else:
                    pe.wait_ge(up_done.sem, up_done.at(e, j - 1))
                for a in range(2):
                    for k in range(DK):
                        last = mm(yb[:, a * TOK:(a + 1) * TOK], w_up[:, k, (2 * j + a) * P:(2 * j + a + 1) * P],
                                  h2T[:, k, :], start=k == 0, stop=k == DK - 1)
                last.then_inc(up_ps.sem, 1)

            def ffn_WT(e, c, g):
                pe.wait_ge(W_done.sem, W_done.at(e, c))
                for q in range(2):
                    if c:
                        pe.wait_ge(WT_sb.sem, WT_sb.at(e, q))
                    else:
                        pe.wait_ge(sL_done.sem, sL_done.at(g, 2 * (CH - 1) + q))
                    for i in range(4):
                        last = nc.tensor.transpose(pairb[q][:, i * P:(i + 1) * P],
                                                   W[:, (4 * q + i) * P:(4 * q + i + 1) * P], ident[:])
                    last.then_inc(WT_ps.sem, 1)

            def ffn_down(e, c):
                if c == 0:
                    pe.wait_ge(up_done.sem, up_done.at(e, FT // 2 - 1))
                    if later(e):
                        pe.wait_ge(f_sb.sem, f_sb.at(e - 1))
                    mm(f0[:], zero_b[:], mask_b[:].rearrange("p h t -> p (h t)"), start=True, stop=False)
                for i in range(FT):
                    last = mm(f0[:, c * D:(c + 1) * D], hid[:, i, c * P:(c + 1) * P], w_down[:, i, :],
                              start=False, stop=False)
                last.then_inc(down_ps.sem, 1)

            def ffn_out(e, c):
                for q in range(2):
                    pe.wait_ge(WT_sb.sem, WT_sb.at(e, 2 * c + q))
                    for i in range(4):
                        last = mm(f0[:, c * D:(c + 1) * D], WT[:, 4 * q + i, :], w_ue[:, 4 * q + i, :], start=False,
                                  stop=c == CH - 1 and q == 1 and i == 3)
                last.then_inc(out_part.sem if c == 0 else f_ps.sem, 1)

            def do_group(g, e, f, n):
                a, b, c = g is not None, e is not None, f is not None

                def pairs(*js):
                    for j in js:
                        if a:
                            mixer_pair(g, j)

                pairs(0, 1)
                if a:
                    mixer_dt(g)
                pairs(2)
                if c:
                    ffn_A(f, 1)
                pairs(3)
                if b:
                    tail_h2T(e, g)
                if a:
                    mixer_z(g, 0)
                    mixer_z(g, 1)
                if b:
                    ffn_sim(e, 0)
                if c:
                    ffn_WT(f, 0, f if e is None else e)
                pairs(4)
                if b:
                    ffn_sim(e, 1)
                pairs(5)
                if c:
                    ffn_down(f, 0)
                pairs(6)
                if c:
                    ffn_down(f, 1)
                if b:
                    ffn_up(e, 0)
                pairs(7)
                if b:
                    ffn_up(e, 1)
                if c:
                    ffn_out(f, 0)
                if a:
                    mixer_cum(g, e)
                pairs(8)
                if b:
                    ffn_up(e, 2, g)
                pairs(9)
                if b:
                    ffn_up(e, 3)
                if a:
                    mixer_X(g, 0)
                if c:
                    ffn_WT(f, 1, None)
                if b:
                    ffn_A(e, 0)
                if a:
                    mixer_rows(g, 0, f)
                if c:
                    ffn_out(f, 1)
                if a:
                    mixer_B(g, 0)
                    mixer_scores(g, 0)
                    mixer_Yi(g, 0)
                    mixer_Yn(g, 0, e)
                    mixer_X(g, 1)
                    mixer_rows(g, 1, f)
                    mixer_S(g, 0)
                    mixer_B(g, 1)
                    mixer_scores(g, 1)
                    mixer_Yi(g, 1)
                    mixer_Yn(g, 1, e)
                    mixer_yT(g, 0)
                    mixer_S(g, 1)
                    mixer_out(g, 0)
                    mixer_yT(g, 1)
                    mixer_out(g, 1)
                if n is not None:
                    mixer_hT(n)

            mixer_hT(0)
            do_group(0, None, None, 1)
            pe.wait_ge(loaded_w, 16 * 4)
            do_group(1, 0, None, 2)
            do_group(2, 1, 0, 3)
            with pe.Fori(3, NG - 1) as g:
                do_group(g, g - 1, g - 2, g + 1)
            do_group(NG - 1, NG - 2, NG - 3, None)
            do_group(None, NG - 1, NG - 2, None)
            do_group(None, None, NG - 1, None)


def layouts(i):
    import numpy as np

    def tiles(wT):
        return np.ascontiguousarray(wT.reshape(-1, P, wT.shape[1]).transpose(1, 0, 2))

    def every(a):
        return np.ascontiguousarray(np.broadcast_to(a, (P, a.shape[0])))

    i = {k.replace("L0_", ""): np.asarray(a) for k, a in i.items()}
    return dict(
        x=i["attn_x"].reshape(-1, D),
        in_wT=tiles(i["attn_in_proj_w"].T),
        norm_w=np.ascontiguousarray(i["attn_norm_w"].reshape(DK, P).T),
        conv_w=np.ascontiguousarray(i["attn_conv_w"].reshape(TILES, P, TAPS).transpose(1, 0, 2)),
        conv_b=np.ascontiguousarray(i["attn_conv_b"].reshape(TILES, P).T),
        dt_bias=every(i["attn_dt_bias"]),
        A_log=every(i["attn_A_log"]),
        D_skip=every(i["attn_D_skip"]),
        gnorm_w=np.ascontiguousarray(i["attn_gnorm_w"].reshape(INNER // P, P).T),
        out_wT=tiles(i["attn_out_proj_w"].T),
        upT=tiles(i["ffn_W_up"].T),
        downT=tiles(i["ffn_W_down"].T),
        wq=np.ascontiguousarray(i["ffn_W_q"].reshape(2 * RH, 64, D).transpose(1, 0, 2)),
        keysT=np.ascontiguousarray(i["ffn_keys"].transpose(3, 2, 0, 1).reshape(64, 2, TOK)),
        down_eT=tiles(i["ffn_down_embed"].T),
        up_e=tiles(i["ffn_up_embed"]),
    )


def kernel(**inputs):
    import numpy as np
    import concourse.bacc as bacc
    from concourse.bass_utils import run_bass_kernel_spmd

    nc = bacc.Bacc("TRN2", target_bir_lowering=False, num_devices=1)
    arrays = layouts(inputs)
    args = {n: nc.dram_tensor(f"{n}_dram", a.shape, mybir.dt.from_np(a.dtype), kind="ExternalInput").ap()
            for n, a in arrays.items()}
    out = nc.dram_tensor("out_dram", arrays["x"].shape, F32, kind="ExternalOutput").ap()
    sandwich(nc, out=out, **args)
    r = run_bass_kernel_spmd(nc, [{f"{n}_dram": a for n, a in arrays.items()}], core_ids=[0])
    shape = np.shape(inputs["L0_attn_x"])
    return np.asarray(r.results[0]["out_dram"]).reshape(shape)
```
